# Optimizing a Trainium2 kernel written in Bass

```python
import numpy as np
import jax
import jax.numpy as jnp

def _softmax(x, axis=-1):
    return jax.nn.softmax(x, axis=axis)

def _gelu(x):
    return jax.nn.gelu(x, approximate=True)

def _silu(x):
    return jax.nn.silu(x)

def _sigmoid(x):
    return jax.nn.sigmoid(x)

def _layernorm(x, axis=-1, eps=1e-05):
    m = jnp.mean(x, axis=axis, keepdims=True)
    v = jnp.var(x, axis=axis, keepdims=True)
    return (x - m) / jnp.sqrt(v + eps)

def _scatter_add(tgt, idx, src, axis=0):
    return tgt.at[idx].add(src)

def _segment_sum(src, seg, n):
    return jax.ops.segment_sum(src, seg, n)
kernel_name = 'mk_conv_seq_d2_conv_nchw64_r4_22c021'

def setup_inputs(seed: int=0):
    np.random.seed(seed)
    _w = jnp.asarray

    def _rec_inputs():
        import jax
        import jax.numpy as jnp
        _gk = jax.random.key(seed)
        x = -0.000125 + 0.9999 * jax.random.normal(jax.random.fold_in(_gk, 1), (8, 16, 64, 64), jnp.float32)
        return x
    x = _rec_inputs()

    def _L0_conv_setup():
        import jax, jax.numpy as jnp
        import numpy as np
        from jax import lax
        B, C, H, W = (8, 16, 64, 64)
        WSIZES = [8, 8]
        DRATES = [1, 2]
        SHIFT = True
        CS = C // len(WSIZES)
        SCALE = CS ** (-0.5)
        EPS = 1e-06

        def _ln2d(x, w, b):
            mu = x.mean(1, keepdims=True)
            var = ((x - mu) ** 2).mean(1, keepdims=True)
            y = (x - mu) / jnp.sqrt(var + EPS)
            return w[None, :, None, None] * y + b[None, :, None, None]

        def _conv1d(x, w, pad, dil):
            return lax.conv_general_dilated(x, w, (1,), ((pad, pad),), rhs_dilation=(dil,), dimension_numbers=('NCH', 'OIH', 'NCH'))

        def _eca(x, w1, w2, w3, wc):
            y = x.mean((2, 3))[:, None, :]
            y1 = _conv1d(y, w1, 1, 1)
            y2 = _conv1d(y, w2, 2, 2)
            y3 = _conv1d(y, w3, 4, 4)
            y = _conv1d(jnp.concatenate([y1, y2, y3], axis=1), wc, 1, 1)
            return jax.nn.sigmoid(jnp.transpose(y, (0, 2, 1))[..., None])

        def _conv1x1(x, w):
            return jnp.einsum('bchw,oc->bohw', x, w)

        def _win(x, ws):
            b, c, h, w = x.shape
            nh, nw = (h // ws, w // ws)
            x = x.reshape(b, c, nh, ws, nw, ws).transpose(0, 2, 4, 3, 5, 1)
            return x.reshape(b * nh * nw, ws * ws, c)

        def _unwin(x, b, nh, nw, ws):
            c = x.shape[-1]
            x = x.reshape(b, nh, nw, ws, ws, c).transpose(0, 5, 1, 3, 2, 4)
            return x.reshape(b, c, nh * ws, nw * ws)
        key = jax.random.key(seed)
        ks = jax.random.split(key, 16)
        g = lambda k, shape: jax.random.normal(k, shape, jnp.float32) * 0.02
        return {'x0': jax.random.normal(ks[0], (B, C, H, W), jnp.float32), 'ln_w': jnp.ones((C,), jnp.float32), 'ln_b': jnp.zeros((C,), jnp.float32), 'dw_w': g(ks[1], (C, 1, 3, 3)), 'dw_b': jnp.zeros((C,), jnp.float32), 'eca_w1': g(ks[2], (1, 1, 3)), 'eca_w2': g(ks[3], (1, 1, 3)), 'eca_w3': g(ks[4], (1, 1, 3)), 'eca_wc': g(ks[5], (1, 3, 3)), 'wq': g(ks[6], (C, C)), 'wk': g(ks[7], (C, C)), 'wv': g(ks[8], (C, C)), 'down_w': g(ks[9], (CS, 1, 2, 2)), 'down_b': jnp.zeros((CS,), jnp.float32), 'sa_w': g(ks[10], (1, C)), 'sa_b': jnp.zeros((1,), jnp.float32), 'po_w': g(ks[11], (C, C)), 'po_b': jnp.zeros((C,), jnp.float32)}
    _L0_conv_all = _L0_conv_setup()
    _L0_conv_in = {k: v for k, v in _L0_conv_all.items() if k in ('ln_w', 'ln_b', 'dw_w', 'dw_b', 'eca_w1', 'eca_w2', 'eca_w3', 'eca_wc', 'wq', 'wk', 'wv', 'down_w', 'down_b', 'sa_w', 'sa_b', 'po_w', 'po_b')}
    del _L0_conv_all

    def _L1_conv_setup():
        import jax, jax.numpy as jnp
        import numpy as np
        KK = 9
        BN_EPS = 1e-05

        def _dcn_bn_act_res(x, w_off, b_off, w, b, gamma, beta):
            B, C, H, W = x.shape
            O = w.shape[0]
            om = jax.lax.conv_general_dilated(x, w_off, window_strides=(1, 1), padding=[(1, 1), (1, 1)], dimension_numbers=('NCHW', 'OIHW', 'NCHW')) + b_off[None, :, None, None]
            off_y = om[:, :KK]
            off_x = om[:, KK:2 * KK]
            mask = jax.nn.sigmoid(om[:, 2 * KK:])
            ky, kx = jnp.meshgrid(jnp.arange(3), jnp.arange(3), indexing='ij')
            ky = ky.reshape(KK).astype(jnp.float32) - 1.0
            kx = kx.reshape(KK).astype(jnp.float32) - 1.0
            hs = jnp.arange(H, dtype=jnp.float32)
            ws = jnp.arange(W, dtype=jnp.float32)
            py = off_y + hs[None, None, :, None] + ky[None, :, None, None]
            px = off_x + ws[None, None, None, :] + kx[None, :, None, None]
            y0 = jnp.floor(py)
            x0 = jnp.floor(px)
            wy = py - y0
            wx = px - x0
            y0i = y0.astype(jnp.int32)
            x0i = x0.astype(jnp.int32)

            def gather(img, yi, xi):
                valid = (yi >= 0) & (yi < H) & (xi >= 0) & (xi < W)
                yc = jnp.clip(yi, 0, H - 1)
                xc = jnp.clip(xi, 0, W - 1)
                return img[:, yc, xc] * valid[None].astype(img.dtype)

            def sample_one(img, yi, xi, wy_, wx_):
                v00 = gather(img, yi, xi)
                v01 = gather(img, yi, xi + 1)
                v10 = gather(img, yi + 1, xi)
                v11 = gather(img, yi + 1, xi + 1)
                w00 = ((1 - wy_) * (1 - wx_))[None]
                w01 = ((1 - wy_) * wx_)[None]
                w10 = (wy_ * (1 - wx_))[None]
                w11 = (wy_ * wx_)[None]
                return v00 * w00 + v01 * w01 + v10 * w10 + v11 * w11
            sampled = jax.vmap(sample_one)(x, y0i, x0i, wy, wx)
            sampled = sampled * mask[:, None]
            out = jnp.einsum('bckhw,ock->bohw', sampled, w.reshape(O, C, KK))
            out = out + b[None, :, None, None]
            mu = out.mean(axis=(0, 2, 3), keepdims=True)
            var = out.var(axis=(0, 2, 3), keepdims=True)
            out = (out - mu) * jax.lax.rsqrt(var + BN_EPS)
            out = out * gamma[None, :, None, None] + beta[None, :, None, None]
            return jax.nn.relu(out) + x
        key = jax.random.key(seed)
        ks = jax.random.split(key, 8)
        B, C, H, W = (2, 16, 64, 64)
        O = 16
        x = jax.random.normal(ks[0], (B, C, H, W), dtype=jnp.float32)
        w_off = jax.random.normal(ks[1], (3 * KK, C, 3, 3), dtype=jnp.float32) * 0.05
        b_off = jnp.zeros((3 * KK,), dtype=jnp.float32)
        w = jax.random.normal(ks[2], (O, C, 3, 3), dtype=jnp.float32) * (1.0 / np.sqrt(C * KK))
        b = jnp.zeros((O,), dtype=jnp.float32)
        gamma = jnp.ones((O,), dtype=jnp.float32)
        beta = jnp.zeros((O,), dtype=jnp.float32)
        return {'x': x, 'w_off': w_off, 'b_off': b_off, 'w': w, 'b': b, 'gamma': gamma, 'beta': beta}
    _L1_conv_all = _L1_conv_setup()
    _L1_conv_in = {k: v for k, v in _L1_conv_all.items() if k in ('w_off', 'b_off', 'w', 'b', 'gamma', 'beta')}
    del _L1_conv_all
    return {'x': x, 'L0_conv_ln_w': _L0_conv_in['ln_w'], 'L0_conv_ln_b': _L0_conv_in['ln_b'], 'L0_conv_dw_w': _L0_conv_in['dw_w'], 'L0_conv_dw_b': _L0_conv_in['dw_b'], 'L0_conv_eca_w1': _L0_conv_in['eca_w1'], 'L0_conv_eca_w2': _L0_conv_in['eca_w2'], 'L0_conv_eca_w3': _L0_conv_in['eca_w3'], 'L0_conv_eca_wc': _L0_conv_in['eca_wc'], 'L0_conv_wq': _L0_conv_in['wq'], 'L0_conv_wk': _L0_conv_in['wk'], 'L0_conv_wv': _L0_conv_in['wv'], 'L0_conv_down_w': _L0_conv_in['down_w'], 'L0_conv_down_b': _L0_conv_in['down_b'], 'L0_conv_sa_w': _L0_conv_in['sa_w'], 'L0_conv_sa_b': _L0_conv_in['sa_b'], 'L0_conv_po_w': _L0_conv_in['po_w'], 'L0_conv_po_b': _L0_conv_in['po_b'], 'L1_conv_w_off': _L1_conv_in['w_off'], 'L1_conv_b_off': _L1_conv_in['b_off'], 'L1_conv_w': _L1_conv_in['w'], 'L1_conv_b': _L1_conv_in['b'], 'L1_conv_gamma': _L1_conv_in['gamma'], 'L1_conv_beta': _L1_conv_in['beta']}

def reference(x, L0_conv_ln_w, L0_conv_ln_b, L0_conv_dw_w, L0_conv_dw_b, L0_conv_eca_w1, L0_conv_eca_w2, L0_conv_eca_w3, L0_conv_eca_wc, L0_conv_wq, L0_conv_wk, L0_conv_wv, L0_conv_down_w, L0_conv_down_b, L0_conv_sa_w, L0_conv_sa_b, L0_conv_po_w, L0_conv_po_b, L1_conv_w_off, L1_conv_b_off, L1_conv_w, L1_conv_b, L1_conv_gamma, L1_conv_beta):
    import jax
    import jax.numpy as jnp

    def _L0_conv_ref(x0, ln_w, ln_b, dw_w, dw_b, eca_w1, eca_w2, eca_w3, eca_wc, wq, wk, wv, down_w, down_b, sa_w, sa_b, po_w, po_b):
        import jax, jax.numpy as jnp
        import numpy as np
        from jax import lax
        B, C, H, W = (8, 16, 64, 64)
        WSIZES = [8, 8]
        DRATES = [1, 2]
        SHIFT = True
        CS = C // len(WSIZES)
        SCALE = CS ** (-0.5)
        EPS = 1e-06

        def _ln2d(x, w, b):
            mu = x.mean(1, keepdims=True)
            var = ((x - mu) ** 2).mean(1, keepdims=True)
            y = (x - mu) / jnp.sqrt(var + EPS)
            return w[None, :, None, None] * y + b[None, :, None, None]

        def _conv1d(x, w, pad, dil):
            return lax.conv_general_dilated(x, w, (1,), ((pad, pad),), rhs_dilation=(dil,), dimension_numbers=('NCH', 'OIH', 'NCH'))

        def _eca(x, w1, w2, w3, wc):
            y = x.mean((2, 3))[:, None, :]
            y1 = _conv1d(y, w1, 1, 1)
            y2 = _conv1d(y, w2, 2, 2)
            y3 = _conv1d(y, w3, 4, 4)
            y = _conv1d(jnp.concatenate([y1, y2, y3], axis=1), wc, 1, 1)
            return jax.nn.sigmoid(jnp.transpose(y, (0, 2, 1))[..., None])

        def _conv1x1(x, w):
            return jnp.einsum('bchw,oc->bohw', x, w)

        def _win(x, ws):
            b, c, h, w = x.shape
            nh, nw = (h // ws, w // ws)
            x = x.reshape(b, c, nh, ws, nw, ws).transpose(0, 2, 4, 3, 5, 1)
            return x.reshape(b * nh * nw, ws * ws, c)

        def _unwin(x, b, nh, nw, ws):
            c = x.shape[-1]
            x = x.reshape(b, nh, nw, ws, ws, c).transpose(0, 5, 1, 3, 2, 4)
            return x.reshape(b, c, nh * ws, nw * ws)
        b, c, h, w = x0.shape
        x = _ln2d(x0, ln_w, ln_b)
        x1 = lax.conv_general_dilated(x, dw_w, (1, 1), ((1, 1), (1, 1)), feature_group_count=c, dimension_numbers=('NCHW', 'OIHW', 'NCHW'))
        x1 = x1 + dw_b[None, :, None, None]
        ca = _eca(x1, eca_w1, eca_w2, eca_w3, eca_wc)
        vs = jnp.split(_conv1x1(x, wv) * ca, len(WSIZES), axis=1)
        qs = jnp.split(_conv1x1(x, wq), len(WSIZES), axis=1)
        ks_ = jnp.split(_conv1x1(x, wk), len(WSIZES), axis=1)
        ys = []
        for idx in range(len(WSIZES)):
            ws = WSIZES[idx]
            ds = ws // DRATES[idx]
            q = qs[idx]
            if SHIFT:
                q = jnp.roll(q, (-ws // 2, -ws // 2), (2, 3))
            q = _win(q, ws)
            if DRATES[idx] != 1:

                def down(t):
                    t = lax.conv_general_dilated(t, down_w, (2, 2), 'VALID', feature_group_count=CS, dimension_numbers=('NCHW', 'OIHW', 'NCHW'))
                    return t + down_b[None, :, None, None]
                k = down(ks_[idx])
                v = down(vs[idx])
                if SHIFT:
                    k = jnp.roll(k, (-ds // 2, -ds // 2), (2, 3))
                    v = jnp.roll(v, (-ds // 2, -ds // 2), (2, 3))
                k = _win(k, ds)
                v = _win(v, ds)
            else:
                k, v = (ks_[idx], vs[idx])
                if SHIFT:
                    k = jnp.roll(k, (-ws // 2, -ws // 2), (2, 3))
                    v = jnp.roll(v, (-ws // 2, -ws // 2), (2, 3))
                k = _win(k, ws)
                v = _win(v, ws)
            atn = jax.nn.softmax(jnp.einsum('nqc,nkc->nqk', q, k) * SCALE, axis=-1)
            y_ = jnp.einsum('nqk,nkc->nqc', atn, v)
            y_ = _unwin(y_, b, h // ws, w // ws, ws)
            if SHIFT:
                y_ = jnp.roll(y_, (ws // 2, ws // 2), (2, 3))
            ys.append(y_)
        y = jnp.concatenate(ys, axis=1)
        x1m = jax.nn.sigmoid(_conv1x1(y, sa_w) + sa_b[None, :, None, None]) * x1
        y = _conv1x1(y + x1m, po_w) + po_b[None, :, None, None]
        return y + x0

    def _L1_conv_ref(x, w_off, b_off, w, b, gamma, beta):
        import jax, jax.numpy as jnp
        import numpy as np
        KK = 9
        BN_EPS = 1e-05

        def _dcn_bn_act_res(x, w_off, b_off, w, b, gamma, beta):
            B, C, H, W = x.shape
            O = w.shape[0]
            om = jax.lax.conv_general_dilated(x, w_off, window_strides=(1, 1), padding=[(1, 1), (1, 1)], dimension_numbers=('NCHW', 'OIHW', 'NCHW')) + b_off[None, :, None, None]
            off_y = om[:, :KK]
            off_x = om[:, KK:2 * KK]
            mask = jax.nn.sigmoid(om[:, 2 * KK:])
            ky, kx = jnp.meshgrid(jnp.arange(3), jnp.arange(3), indexing='ij')
            ky = ky.reshape(KK).astype(jnp.float32) - 1.0
            kx = kx.reshape(KK).astype(jnp.float32) - 1.0
            hs = jnp.arange(H, dtype=jnp.float32)
            ws = jnp.arange(W, dtype=jnp.float32)
            py = off_y + hs[None, None, :, None] + ky[None, :, None, None]
            px = off_x + ws[None, None, None, :] + kx[None, :, None, None]
            y0 = jnp.floor(py)
            x0 = jnp.floor(px)
            wy = py - y0
            wx = px - x0
            y0i = y0.astype(jnp.int32)
            x0i = x0.astype(jnp.int32)

            def gather(img, yi, xi):
                valid = (yi >= 0) & (yi < H) & (xi >= 0) & (xi < W)
                yc = jnp.clip(yi, 0, H - 1)
                xc = jnp.clip(xi, 0, W - 1)
                return img[:, yc, xc] * valid[None].astype(img.dtype)

            def sample_one(img, yi, xi, wy_, wx_):
                v00 = gather(img, yi, xi)
                v01 = gather(img, yi, xi + 1)
                v10 = gather(img, yi + 1, xi)
                v11 = gather(img, yi + 1, xi + 1)
                w00 = ((1 - wy_) * (1 - wx_))[None]
                w01 = ((1 - wy_) * wx_)[None]
                w10 = (wy_ * (1 - wx_))[None]
                w11 = (wy_ * wx_)[None]
                return v00 * w00 + v01 * w01 + v10 * w10 + v11 * w11
            sampled = jax.vmap(sample_one)(x, y0i, x0i, wy, wx)
            sampled = sampled * mask[:, None]
            out = jnp.einsum('bckhw,ock->bohw', sampled, w.reshape(O, C, KK))
            out = out + b[None, :, None, None]
            mu = out.mean(axis=(0, 2, 3), keepdims=True)
            var = out.var(axis=(0, 2, 3), keepdims=True)
            out = (out - mu) * jax.lax.rsqrt(var + BN_EPS)
            out = out * gamma[None, :, None, None] + beta[None, :, None, None]
            return jax.nn.relu(out) + x
        return _dcn_bn_act_res(x, w_off, b_off, w, b, gamma, beta)

    def _gn(v, G=32, eps=1e-05):
        B_, C_, H_, W_ = v.shape
        g = v.reshape(B_, G, C_ // G, H_, W_)
        m = jnp.mean(g, axis=(2, 3, 4), keepdims=True)
        s = jnp.var(g, axis=(2, 3, 4), keepdims=True)
        return ((g - m) / jnp.sqrt(s + eps)).reshape(v.shape)

    def _ln_c(v, eps=1e-06):
        m = jnp.mean(v, axis=1, keepdims=True)
        s = jnp.var(v, axis=1, keepdims=True)
        return (v - m) / jnp.sqrt(s + eps)

    def _ln_t(v, eps=1e-05):
        m = jnp.mean(v, axis=-1, keepdims=True)
        s = jnp.var(v, axis=-1, keepdims=True)
        return (v - m) / jnp.sqrt(s + eps)

    def _to_tokens(v):
        B_, C_, H_, W_ = v.shape
        return v.reshape(B_, C_, H_ * W_).transpose(0, 2, 1)

    def _from_tokens(t, like):
        B_, C_, H_, W_ = like.shape
        return t.transpose(0, 2, 1).reshape(B_, C_, H_, W_)
    x = _L0_conv_ref(x, L0_conv_ln_w, L0_conv_ln_b, L0_conv_dw_w, L0_conv_dw_b, L0_conv_eca_w1, L0_conv_eca_w2, L0_conv_eca_w3, L0_conv_eca_wc, L0_conv_wq, L0_conv_wk, L0_conv_wv, L0_conv_down_w, L0_conv_down_b, L0_conv_sa_w, L0_conv_sa_b, L0_conv_po_w, L0_conv_po_b)
    x = _L1_conv_ref(x, L1_conv_w_off, L1_conv_b_off, L1_conv_w, L1_conv_b, L1_conv_gamma, L1_conv_beta)
    return x

_drawn_inputs = setup_inputs


def setup_inputs(seed=0):
    import zlib

    import numpy as np

    out = dict(_drawn_inputs(seed))
    spreads = {'L0_conv_ln_w': (1.0, 0.6),
     'L0_conv_ln_b': (0.0, 0.8),
     'L0_conv_dw_b': (0.0, 0.8),
     'L0_conv_down_b': (0.0, 0.8),
     'L0_conv_po_b': (0.0, 0.1),
     'L1_conv_b_off': (0.0, 0.1),
     'L1_conv_b': (0.0, 2.0),
     'L1_conv_gamma': (1.0, 0.2),
     'L1_conv_beta': (0.0, 0.1)}
    factors = {'L0_conv_dw_w': 8.0,
     'L0_conv_eca_w1': 56.857,
     'L0_conv_eca_w2': 58.603,
     'L0_conv_eca_w3': 43.528,
     'L0_conv_eca_wc': 24.078,
     'L0_conv_wq': 8.0,
     'L0_conv_wk': 8.0,
     'L0_conv_wv': 8.0,
     'L0_conv_down_w': 8.0,
     'L0_conv_sa_w': 8.0,
     'L0_conv_po_w': 6.159}
    for name, (base, spread) in spreads.items():
        noise = np.random.default_rng([zlib.crc32(name.encode()), seed]).standard_normal(out[name].shape)
        drawn = base * np.exp(spread * noise) if base else spread * noise
        out[name] = jnp.asarray(drawn.astype(out[name].dtype))
    for name, factor in factors.items():
        out[name] = (out[name] * factor).astype(out[name].dtype)
    return out
```

```python
from contextlib import ExitStack

import numpy as np

import concourse.bass as bass
from concourse import mybir

F32 = mybir.dt.float32
BF16 = mybir.dt.bfloat16
ALU = mybir.AluOpType
ACT = mybir.ActivationFunctionType
AX = mybir.AxisListType

B, C, H, W = 8, 16, 64, 64
HW = H * W
P = B * C
WS = 8
NWR = H // WS
CS = C // 2
SCALE = CS ** -0.5
SHIFT = WS // 2
HE = H + SHIFT
K1 = WS * WS
K2 = (WS // 2) ** 2
CH = 512
NCH = HW // CH
RPC = CH // W
KK = 9
OC = 3 * KK
PAIRS = B // 2
BR = 4
NR = 2 * BR + 1
TOP = BR + 1
NBLK = -(-H // NR)
IR = TOP + NBLK * NR
LN_EPS, BN_EPS = 1e-6, 1e-5
SP3 = 32

_WCOLS = [("wq", C), ("wk", C), ("wv", C), ("po", C), ("sa", 1), ("woff", KK * OC), ("w", KK * C),
          ("ln_w", 1), ("ln_b", 1), ("dw_b", 1), ("po_b", 1), ("dw", KK), ("down", 4), ("down_b", 1),
          ("b", 1), ("gamma", 1), ("beta", 1)]
_RCOLS = [("w1", 3), ("w2", 3), ("w3", 3), ("wc", 9), ("sa_b", 1)]
_CCOLS = [("ident", P), ("eps_ln", 1), ("eps_bn", 1), ("bmask", B), ("h0", B), ("h1", B), ("ec", C), ("bmt", P), ("osum", P),
          ("negx", 1), ("m1", 1), ("m2", 1), ("kxadd", 1), ("xg", CH), ("jrel", NR),
          ("jabs", NBLK * NR), ("yabs", H * KK)]


def _columns(spec):
    at, out = 0, {}
    for name, n in spec:
        out[name] = (at, at + n)
        at += n
    return out, at


WCOL, NWC = _columns(_WCOLS)
RCOL, NRC = _columns(_RCOLS)
CCOL, NCC = _columns(_CCOLS)


def constants():
    c = np.zeros((P, NCC), np.float32)

    def put(name, a):
        c[:a.shape[0], CCOL[name][0]:CCOL[name][1]] = a.reshape(a.shape[0], -1)

    p = np.arange(P)
    bm = (p[:, None] // C == np.arange(B)).astype(np.float32)
    put("ident", np.eye(P, dtype=np.float32))
    put("bmask", bm)
    put("h0", bm * (p[:, None] % C < CS))
    put("h1", bm * (p[:, None] % C >= CS))
    put("ec", (p[:, None] % C == np.arange(C)).astype(np.float32))
    put("bmt", bm.T)
    put("osum", (p[:, None] % C == p[None] % C).astype(np.float32))
    put("negx", -(p[:, None] % W).astype(np.float32))
    put("m1", (p[:96, None] >= SP3).astype(np.float32))
    put("m2", (p[:96, None] >= 2 * SP3).astype(np.float32))
    ch = np.arange(PAIRS * OC) % OC
    isx = (ch >= KK) & (ch < 2 * KK)
    put("kxadd", (isx * (ch % 3 - 1.0))[:, None].astype(np.float32))
    put("xg", isx[:, None] * (np.arange(CH) % W)[None].astype(np.float32))
    put("jrel", np.tile(np.arange(NR) - float(BR), (P, 1)))
    put("jabs", np.tile(np.arange(NBLK * NR) * 1.0, (P, 1)))
    y, k = np.meshgrid(np.arange(H), np.arange(KK), indexing="ij")
    put("yabs", np.tile((y + k // 3 - 1.0).reshape(1, -1), (P, 1)))
    sel = np.zeros((96, KK, 2, W), np.float32)
    for s in range(3):
        for h in range(2):
            for k in range(KK):
                sel[s * SP3 + h * KK + k, k, h] = 1.0
    put("eps_ln", np.full((P, 1), LN_EPS))
    put("eps_bn", np.full((P, 1), BN_EPS))
    return c, sel.reshape(96, -1)


def build(nc, x, wpack, rpack, boff, consts, selc, out):
    ctx = ExitStack()
    with ctx:
        def sb(name, shape, dt=F32):
            return ctx.enter_context(nc.sbuf_tensor(name, shape, dt))

        def sem(name):
            return ctx.enter_context(nc.semaphore(name))

        om_dram = nc.dram_tensor("om_scratch", (B * OC, HW), F32, kind="Internal").ap()

        x0t = sb("x0", [P, HW])
        wr = sb("wr", [P, NWC])
        rp = sb("rp", [P, NRC])
        cst = sb("cst", [P, NCC])
        bcol = sb("bcol", [PAIRS * OC, 1])
        xp = sb("xp", [P, (H + 2) * (W + 2)])
        bd = sb("bd", [P, 6, P])
        MEAN, WQ, WK, WV, PO, SA = range(6)
        woff = sb("woff", [P, 2, KK, PAIRS * OC])
        selb = sb("selb", [96, KK, P], BF16)
        two = sb("two", [P, 2, 2 * CH])
        small = sb("small", [P, 64])
        ecab = sb("ecab", [B, 128])
        flag = sb("flag", [1, 1], mybir.dt.int32)

        def cutter(name, n):
            region, at = sb(name, [P, n]), [0]

            def cut(k):
                if k is None:
                    at[0] = 0
                    return None
                at[0] += k
                assert at[0] <= n, (name, at[0], n)
                return region[:, at[0] - k:at[0]]
            return cut

        cut = cutter("region", 27680)
        xe = cut(HE * HE)
        qw = cut(HW)
        kw = cut(HW)
        vw = cut(HW)
        kv = cut(NWR * NWR * 2 * K2)
        x1 = cut(HW)
        ye = cut(HE * HE)
        cut(None)
        img = cut(IR * KK * C)
        osam = cut(H * PAIRS * C)
        st = cut(HW)
        z = st
        aw = cut(H * KK * NR)
        mk = cut(H * PAIRS * KK)
        cut2 = cutter("region2", 7776)
        kb = cut2(2 * 2 * B * K1).rearrange("p (u w k) -> p u w k", u=2, w=2)
        kvb = cut2(2 * 2 * 2 * B * K2).rearrange("p (u w t k) -> p u w t k", u=2, w=2, t=2)
        ee = cut2(2 * B * (K1 + K2)).rearrange("p (u k) -> p u k", u=2)
        pts = cut2(2 * 5 * P).rearrange("p (u t k) -> p u t k", u=2, t=5)
        v0 = cut2(2 * 2 * P).rearrange("p (u w a b c) -> p u w a b c", u=2, w=2, a=4, b=2)
        v1 = cut2(2 * 2 * P).rearrange("p (u w k) -> p u w k", u=2, w=2)
        qs = cut2(2 * 2 * K1).rearrange("p (u w k) -> p u w k", u=2, w=2)
        vs = cut2(2 * 2 * 2 * K1).rearrange("p (u w d k) -> p u w d k", u=2, w=2, d=2)
        on = cut2(2 * P).rearrange("p (u k) -> p u k", u=2)
        sm = cut2(2 * 3 * 2 * B).rearrange("p (u t k) -> p u t k", u=2, t=3)
        cut2(None)
        wt = cut2(2 * KK * P).rearrange("p (u k s) -> p u k s", u=2, k=KK)
        uu = cut2(2 * KK * NR * C).rearrange("p (u a o) -> p u a o", u=2, o=C)
        sx = cut2(HW // 2).bitcast(BF16)
        tmpb = cut2(HW // 8).bitcast(BF16)
        py = x0t[:, 0:H * PAIRS * KK]
        ab = x0t[:, H * PAIRS * KK:H * PAIRS * KK + 2 * KK * W].rearrange("p (u k) -> p u k", u=2)
        x0 = x0t[:, :]

        PS = ctx.enter_context(nc.psum_tensor("PS", [P, 8, 512], F32))

        def w_(name):
            return wr[:, WCOL[name][0]:WCOL[name][1]]

        def r_(name):
            return rp[:, RCOL[name][0]:RCOL[name][1]]

        def c_(name, parts=P):
            return cst[0:parts, CCOL[name][0]:CCOL[name][1]]

        def grid(flat, c):
            return flat.rearrange("p (r c) -> p r c", c=c)

        ident = c_("ident")
        xe3, ye3, x13, xp3 = grid(xe, HE), grid(ye, HE), grid(x1, W), grid(xp[:, :], W + 2)
        x03 = grid(x0, W)
        img4 = img.rearrange("p (r k o) -> p r k o", k=KK, o=C)
        os4 = osam.rearrange("p (r g o) -> p r g o", g=PAIRS, o=C)
        aw4 = aw.rearrange("p (r k j) -> p r k j", k=KK, j=NR)
        mk4 = mk.rearrange("p (r g k) -> p r g k", g=PAIRS, k=KK)
        py4 = py.rearrange("p (r g k) -> p r g k", g=PAIRS, k=KK)
        kv4 = kv.rearrange("p (w t k) -> p w t k", t=2, k=K2)

        def mid(ap, n):
            return ap.unsqueeze(1).to_broadcast([ap.shape[0], n, ap.shape[1]])

        def end(ap, n):
            return ap.unsqueeze(len(ap.shape)).to_broadcast(list(ap.shape) + [n])

        def done(n, per=1):
            return (n + 3) * per

        def free(n, per=1):
            return (n + 1) * per

        x_in, w_in = sem("x_in"), sem("w_in")
        bd_ready, pads_ready = sem("bd_ready"), sem("pads_ready")
        mu_ready, xc_ready, sq_ready, var_ready = sem("mu_ready"), sem("xc_ready"), sem("sq_ready"), sem("var_ready")
        std_ready, rstd_ready, xn_ready, ln_ready = sem("std_ready"), sem("rstd_ready"), sem("xn_ready"), sem("ln_ready")
        ext_ready = sem("ext_ready")
        qkv_ready, q_out, k_out, v_out = sem("qkv_ready"), sem("q_out"), sem("k_out"), sem("v_out")
        down_step, conv_step, eca_step = sem("down_step"), sem("conv_step"), sem("eca_step")
        eca_sum, eca_pre, eca_gate, eca_back = sem("eca_sum"), sem("eca_pre"), sem("eca_gate"), sem("eca_back")
        staged, s_ready, vt_ready, max_ready = sem("staged"), sem("s_ready"), sem("vt_ready"), sem("max_ready")
        sub_ready, exp_ready, sum_ready, rcp_ready = sem("sub_ready"), sem("exp_ready"), sem("sum_ready"), sem("rcp_ready")
        vt_out, pt_ready, pt_out, o_ready = sem("vt_out"), sem("pt_ready"), sem("pt_out"), sem("o_ready")
        on_ready, ot_ready, ye_out, yext_ready = sem("on_ready"), sem("ot_ready"), sem("ye_out"), sem("yext_ready")
        yc_ready, gate_ready, sg_ready, gx_ready = sem("yc_ready"), sem("gate_ready"), sem("sg_ready"), sem("gx_ready")
        tt_ready, po_ready, xl_ready = sem("tt_ready"), sem("po_ready"), sem("xl_ready")
        om_ready, om_out, tr_ready, py_out, mk_out = sem("om_ready"), sem("om_out"), sem("tr_ready"), sem("py_out"), sem("mk_out")
        om_done = sem("om_done")
        om_stored = [sem("om_stored0"), sem("om_stored1")]
        zeros_ready = sem("zeros_ready")
        pool_turn = sem("pool_turn")
        ox_in, ox_step, px_ready = sem("ox_in"), sem("ox_step"), sem("px_ready")
        is_ready, im_ready, im_out = sem("is_ready"), sem("im_ready"), sem("im_out")
        ad_ready, aa_ready, ar_ready, aw_ready = sem("ad_ready"), sem("aa_ready"), sem("ar_ready"), sem("aw_ready")
        bc_ready, ab_ready, wt_ready, t_ready = sem("bc_ready"), sem("ab_ready"), sem("wt_ready"), sem("t_ready")
        u_ready, os_ready = sem("u_ready"), sem("os_ready")
        off_max, off_row, off_step, flag_ready = sem("off_max"), sem("off_row"), sem("off_step"), sem("flag_ready")
        abs_ready, part_ready = sem("abs_ready"), sem("part_ready")
        ob_ready, ot2_ready, z_ready, bn_step = sem("ob_ready"), sem("ot2_ready"), sem("z_ready"), sem("bn_step")
        bn_sum, bn_mean, bn_sq, bn_var, bn_std, bn_aff = [sem("bn_" + n) for n in "sum mean sq var std aff".split()]
        f_ready, r_ready, stored = sem("f_ready"), sem("r_ready"), sem("stored")

        def branches(eng, passes):
            eng.wait_ge(flag_ready, 1)
            large = eng.value_load(flag[0:1, 0:1], min_val=0, max_val=1)
            with eng.If(large == 0):
                with eng.Fori(0, PAIRS) as g:
                    passes(g, g, None)
                eng.nop()
            with eng.Else():
                with eng.Fori(0, PAIRS) as g:
                    with eng.Fori(0, NBLK) as band:
                        passes(g * NBLK + band, g, band)
                eng.nop()

        block = ctx.enter_context(nc.Block())
        LAST = 2

        @block.sync
        def _(sp):
            sp.dma_start(x0, x.rearrange("b c h w -> (b c) (h w)")).then_inc(x_in, 16)
            for b in range(B):
                sp.dma_start(wr[C * b:C * (b + 1), :], wpack).then_inc(w_in, 16)
            sp.dma_start(rp[:, :], rpack.to_broadcast([P, NRC])).then_inc(w_in, 16)
            sp.dma_start(cst[:, :], consts).then_inc(w_in, 16)
            for b in range(PAIRS):
                sp.dma_start(bcol[OC * b:OC * (b + 1), :], boff).then_inc(w_in, 16)
            sp.dma_start(two[0:96, :, :].rearrange("p a b -> p (a b)")[:, 0:KK * P], selc).then_inc(w_in, 16)

            sp.sem_inc(om_done, 2)
            with sp.Fori(0, NCH // 2) as step:
                i = step * 2
                for u in range(2):
                    n = i + u
                    sp.wait_ge(om_out, done(n, 2))
                    for h in range(2):
                        sp.dma_start(om_dram[h * PAIRS * OC:(h + 1) * PAIRS * OC, bass.ds(n * CH, CH)],
                                     two[0:PAIRS * OC, u, h * CH:(h + 1) * CH]).then_inc(om_stored[u], 16)
                    sp.wait_ge(om_stored[u], 16 * i + 32)
                    sp.sem_inc(om_done, 1)
            sp.wait_ge(zeros_ready, 1)

            def load_px(p, g, band):
                sp.wait_ge(ox_step, 20 * p + 20)
                for s in range(3):
                    for h in range(2):
                        sp.dma_start(st[SP3 * s + KK * h:SP3 * s + KK * (h + 1), :],
                                     om_dram[bass.ds(g * OC + h * PAIRS * OC + KK, KK), :]).then_inc(ox_in, 16)

            branches(sp, load_px)
            with sp.Fori(0, 4) as n:
                sp.wait_ge(r_ready, n + 1)
                sp.dma_start(out.rearrange("b c h w -> (b c) (h w)")[:, bass.ds(n * 1024, 1024)],
                             z[:, bass.ds(n * 1024, 1024)]).then_inc(stored, 16)
            sp.wait_ge(stored, 64)

        @block.gpsimd
        def _(pool):
            pool.memset(v0, 0.0).then_inc(pads_ready, 1)
            pool.memset(xp[:, :], 0.0).then_inc(pads_ready, 1)
            pool.wait_ge(ln_ready, done(NCH - 1))
            pool.tensor_copy(xe3[:, H:HE, 0:W], xe3[:, 0:SHIFT, 0:W]).then_inc(ext_ready, 1)
            pool.wait_ge(ext_ready, 1)
            pool.tensor_copy(xe3[:, :, W:HE], xe3[:, :, 0:SHIFT]).then_inc(ext_ready, 1)
            pool.sem_inc(staged, 8)
            pool.wait_ge(k_out, done(NCH - 1))
            pool.wait_ge(q_out, done(NCH - 1))
            pool.wait_ge(v_out, done(NCH - 1))
            pool.wait_ge(down_step, 8)
            with pool.Fori(0, 32 // 2) as step:
                i = step * 2
                for u in range(2):
                    n = i + u
                    pool.wait_ge(vt_ready, free(n))
                    pool.sem_inc(pool_turn, 1)
                    pool.tensor_copy(qs[:, u], qw[:, bass.ds(n * 2 * K1, 2 * K1)].rearrange("p (w k) -> p w k", w=2)).then_inc(staged, 1)
                    pool.tensor_copy(vs[:, u], vw[:, bass.ds(n * 2 * K1, 2 * K1)].rearrange("p (w k) -> p w k", w=2).unsqueeze(2).to_broadcast([P, 2, 2, K1])).then_inc(staged, 1)
                    pool.tensor_tensor(
                        kb[:, u].rearrange("p w (b k) -> p w b k", b=B),
                        kw[:, bass.ds(n * 2 * K1, 2 * K1)].rearrange("p (w k) -> p w k", w=2).unsqueeze(2).to_broadcast([P, 2, B, K1]),
                        mid(c_("h0"), 2).unsqueeze(3).to_broadcast([P, 2, B, K1]), ALU.mult).then_inc(staged, 1)
                    pool.tensor_tensor(
                        kvb[:, u].rearrange("p w t (b k) -> p (w t) b k", b=B),
                        kv[:, bass.ds(n * 4 * K2, 4 * K2)].rearrange("p (w k) -> p w k", w=4).unsqueeze(2).to_broadcast([P, 4, B, K2]),
                        mid(c_("h1"), 4).unsqueeze(3).to_broadcast([P, 4, B, K2]), ALU.mult).then_inc(staged, 1)
            pool.wait_ge(ye_out, done(31))
            pool.tensor_copy(ye3[:, 0:SHIFT, SHIFT:HE], ye3[:, H:HE, SHIFT:HE]).then_inc(yext_ready, 1)
            pool.wait_ge(yext_ready, 1)
            pool.tensor_copy(ye3[:, 0:H, 0:SHIFT], ye3[:, 0:H, W:HE]).then_inc(yext_ready, 1)
            pool.wait_ge(xl_ready, done(NCH - 1))
            pool.memset(st[0:96, :], 0.0).then_inc(zeros_ready, 1)
            pool.memset(img, 0.0).then_inc(zeros_ready, 1)
            pool.memset(wt, 0.0).then_inc(zeros_ready, 1)
            pool.sem_inc(is_ready, 4)
            pool.sem_inc(ad_ready, 2)
            pool.sem_inc(aw_ready, 2)
            pool.sem_inc(ox_step, 20)
            pool.wait_ge(om_done, done(NCH - 1))
            pool.wait_ge(py_out, done(NCH - 1, 2))
            pool.wait_ge(mk_out, done(NCH - 1, 2))

            def tables(p, g, band):
                for yc in range(NCH):
                    n, u = p * NCH + yc, yc % 2
                    pool.wait_ge(im_ready, free(n))
                    pool.sem_inc(pool_turn, 1)
                    for h in range(2):
                        pool.tensor_tensor(
                            two[:, u, :].rearrange("p (r h c) -> p r h c", h=2, c=W)[:, :, h, :],
                            xp3[:, 1 + RPC * yc:1 + RPC * (yc + 1), 1:1 + W],
                            c_("bmask")[:, bass.ds(g + h * PAIRS, 1)].unsqueeze(2).to_broadcast([P, RPC, W]),
                            ALU.mult).then_inc(is_ready, 1)
                pool.wait_ge(ox_in, 96 * p + 96)
                pool.wait_ge(bc_ready, p * H + LAST)
                pool.sem_inc(pool_turn, 1)
                for q in range(4):
                    part = st[0:96, q * 1024:(q + 1) * 1024]
                    for j in range(5):
                        if j == 0 or j == 2:
                            ins = pool.tensor_scalar(tmpb[0:96, :], part, c_("m1" if j == 0 else "m2", 96), None, ALU.mult)
                        elif j == 1 or j == 3:
                            ins = pool.tensor_tensor(part, part, tmpb[0:96, :], ALU.subtract)
                        else:
                            ins = pool.tensor_copy(sx[0:96, q * 1024:(q + 1) * 1024], part)
                        ins.then_inc(ox_step, 1)
                        pool.wait_ge(ox_step, 20 * p + 20 + 5 * q + j + 1)
                        pool.sem_inc(pool_turn, 1)
                grid_rows = c_("jrel") if band is None else c_("jabs")[:, bass.ds(band * NR, NR)]
                if band is not None:
                    pool.wait_ge(abs_ready, 1)
                pool.wait_ge(u_ready, p * H + LAST)
                pool.sem_inc(pool_turn, 1)
                for yc in range(NCH):
                    n = p * NCH + yc
                    rows = slice(RPC * yc, RPC * (yc + 1))
                    pool.tensor_tensor(
                        aw4[:, rows],
                        py4[:, rows, bass.ds(g, 1), :].rearrange("p r g k -> p (r g) k").unsqueeze(3).to_broadcast([P, RPC, KK, NR]),
                        mid(grid_rows, RPC).unsqueeze(2).to_broadcast([P, RPC, KK, NR]), ALU.subtract).then_inc(ad_ready, 1)
                for yc in range(NCH):
                    n = p * NCH + yc
                    rows = slice(RPC * yc, RPC * (yc + 1))
                    pool.wait_ge(ar_ready, done(n))
                    pool.sem_inc(pool_turn, 1)
                    pool.tensor_tensor(
                        aw4[:, rows], aw4[:, rows],
                        mk4[:, rows, bass.ds(g, 1), :].rearrange("p r g k -> p (r g) k").unsqueeze(3).to_broadcast([P, RPC, KK, NR]),
                        ALU.mult).then_inc(aw_ready, 1)


            branches(pool, tables)

        @block.vector
        def _(dve):
            v = nc.vector
            for s, n in ((xc_ready, 2), (rstd_ready, 2), (xn_ready, 2), (ln_ready, 2), (k_out, 2),
                         (max_ready, 4), (sub_ready, 4), (sum_ready, 4), (rcp_ready, 2), (on_ready, 4),
                         (yc_ready, 2), (gx_ready, 2), (tt_ready, 2), (xl_ready, 2), (om_out, 4),
                         (u_ready, 2), (os_ready, 2), (ob_ready, 2)):
                dve.sem_inc(s, n)
            dve.wait_ge(w_in, 240)
            bm = c_("bmask")
            v.tensor_scalar(bd[:, MEAN, :].rearrange("p (b c) -> p b c", b=B), end(bm, C), 1.0 / C, None, ALU.mult).then_inc(bd_ready, 1)
            for slot, name in ((WQ, "wq"), (WK, "wk"), (WV, "wv"), (PO, "po")):
                v.tensor_tensor(bd[:, slot, :].rearrange("p (b c) -> p b c", b=B), mid(w_(name), B), end(bm, C), ALU.mult).then_inc(bd_ready, 1)
            v.tensor_scalar(bd[:, SA, :].rearrange("p (b c) -> p b c", b=B), end(bm, C), w_("sa"), None, ALU.mult).then_inc(bd_ready, 1)
            for h in range(2):
                v.tensor_tensor(
                    woff[:, h].rearrange("p t (b k) -> p t b k", b=PAIRS),
                    w_("woff").rearrange("p (t k) -> p t k", k=OC).unsqueeze(2).to_broadcast([P, KK, PAIRS, OC]),
                    mid(bm[:, PAIRS * h:PAIRS * (h + 1)], KK).unsqueeze(3).to_broadcast([P, KK, PAIRS, OC]),
                    ALU.mult).then_inc(bd_ready, 1)
            v.tensor_copy(selb[:, :, :].rearrange("p k m -> p (k m)"), two[0:96, :, :].rearrange("p a b -> p (a b)")[:, 0:KK * P]).then_inc(bd_ready, 1)
            v.tensor_scalar(bcol[:, :], bcol[:, :], c_("kxadd", PAIRS * OC), None, ALU.add).then_inc(bd_ready, 1)
            v.memset(ecab[:, :], 0.0).then_inc(bd_ready, 1)
            dve.wait_ge(bd_ready, 11)
            with dve.Fori(0, NCH // 2) as step:
                i = step * 2
                for u in range(2):
                    n = i + u
                    rows = xe3[:, bass.ds(n * RPC, RPC), 0:W]
                    dve.wait_ge(mu_ready, done(n))
                    v.tensor_tensor(rows, x03[:, bass.ds(n * RPC, RPC), :], grid(PS[:, u, :], W), ALU.subtract).then_inc(xc_ready, 1)
                    dve.wait_ge(std_ready, done(n))
                    v.reciprocal(two[:, u, CH:2 * CH], two[:, u, CH:2 * CH]).then_inc(rstd_ready, 1)
                    dve.wait_ge(rstd_ready, done(n))
                    dve.wait_ge(xc_ready, done(n))
                    v.tensor_tensor(rows, rows, grid(two[:, u, CH:2 * CH], W), ALU.mult).then_inc(xn_ready, 1)
                    dve.wait_ge(xn_ready, done(n))
                    v.tensor_scalar(rows, rows, w_("ln_w"), w_("ln_b"), ALU.mult, ALU.add).then_inc(ln_ready, 1)
            with dve.Fori(0, NCH // 2) as step:
                i = step * 2
                for u in range(2):
                    n = i + u
                    dve.wait_ge(qkv_ready, done(n))
                    v.tensor_copy(kw[:, bass.ds(n * CH, CH)].rearrange("p (j r c) -> p r j c", j=NWR, r=WS),
                                  PS[:, 2 + u, :].rearrange("p (r j c) -> p r j c", j=NWR, r=WS)).then_inc(k_out, 1)
            dve.wait_ge(k_out, done(NCH - 1))
            dve.wait_ge(v_out, done(NCH - 1))
            for tap in range(4):
                for t, src in enumerate((kw, vw)):
                    o = kv4[:, :, t, :].rearrange("p w (r s) -> p w r s", r=4)
                    s4 = src.rearrange("p (w r a s b) -> p a b w r s", r=4, a=2, s=4, b=2)[:, tap // 2, tap % 2]
                    if tap == 0:
                        ins = v.tensor_scalar(o, s4, w_("down")[:, 0:1], w_("down_b") if t == 0 else 0.0, ALU.mult, ALU.add)
                    else:
                        dve.wait_ge(down_step, 2 * tap - 1 + t)
                        ins = v.scalar_tensor_tensor(o, s4, w_("down")[:, tap:tap + 1], o, ALU.mult, ALU.add)
                    ins.then_inc(down_step, 1)
            taps = [(0, 0)] + [(dy, dx) for dy in (-1, 0, 1) for dx in (-1, 0, 1) if (dy, dx) != (0, 0)]
            for n, (dy, dx) in enumerate(taps):
                wcol = w_("dw")[:, 3 * (dy + 1) + dx + 1:3 * (dy + 1) + dx + 2]
                if n == 0:
                    ins = v.tensor_scalar(x13, xe3[:, 0:H, 0:W], wcol, w_("dw_b"), ALU.mult, ALU.add)
                else:
                    ra, rb, ca, cb = max(0, -dy), H - max(0, dy), max(0, -dx), W - max(0, dx)
                    dve.wait_ge(conv_step, n)
                    ins = v.scalar_tensor_tensor(x13[:, ra:rb, ca:cb], xe3[:, ra + dy:rb + dy, ca + dx:cb + dx], wcol,
                                                 x13[:, ra:rb, ca:cb], ALU.mult, ALU.add)
                ins.then_inc(conv_step, 1)
            dve.wait_ge(conv_step, 9)
            v.reduce_sum(small[:, 0:1], x1, axis=AX.X).then_inc(eca_step, 1)
            dve.wait_ge(eca_step, 1)
            v.tensor_scalar(small[:, 16:32], c_("ec"), small[:, 0:1], None, ALU.mult).then_inc(eca_step, 1)
            dve.wait_ge(eca_sum, 1)
            v.tensor_scalar(ecab[:, 4:20], PS[0:B, 6, 0:C], 1.0 / HW, None, ALU.mult).then_inc(eca_step, 1)
            dve.wait_ge(eca_step, 3)
            steps = 3
            for t in range(3):
                for j, d in enumerate((1, 2, 4)):
                    zz = ecab[:, 33 + 20 * j:33 + 20 * j + C]
                    src = ecab[:, 4 + (t - 1) * d:4 + (t - 1) * d + C]
                    wc = r_("w%d" % (j + 1))[0:B, t:t + 1]
                    if t == 0:
                        ins = v.tensor_scalar(zz, src, wc, None, ALU.mult)
                    else:
                        dve.wait_ge(eca_step, steps - 2)
                        ins = v.scalar_tensor_tensor(zz, src, wc, zz, ALU.mult, ALU.add)
                    ins.then_inc(eca_step, 1)
                    steps += 1
            for j in range(3):
                for t in range(3):
                    src = ecab[:, 32 + 20 * j + t:32 + 20 * j + t + C]
                    wc = r_("wc")[0:B, 3 * j + t:3 * j + t + 1]
                    acc = ecab[:, 92:92 + C]
                    dve.wait_ge(eca_step, steps)
                    if j == t == 0:
                        ins = v.tensor_scalar(acc, src, wc, None, ALU.mult)
                    else:
                        ins = v.scalar_tensor_tensor(acc, src, wc, acc, ALU.mult, ALU.add)
                    ins.then_inc(eca_step, 1)
                    steps += 1
            dve.wait_ge(eca_step, steps)
            v.tensor_copy(ecab[:, 92:92 + C], ecab[:, 92:92 + C]).then_inc(eca_pre, 1)

            def scores(n, u):
                dve.wait_ge(s_ready, done(n))
                s0 = PS[:, u, :].rearrange("p (b k) -> p b k", b=B)
                s1 = PS[:, 2, 0:P].rearrange("p (b k) -> p b k", b=B)
                v.reduce_max(sm[:, u, 0, 0:B], s0, axis=AX.X).then_inc(max_ready, 1)
                v.reduce_max(sm[:, u, 0, B:2 * B], s1, axis=AX.X).then_inc(max_ready, 1)
                dve.wait_ge(pt_ready, free(n))
                dve.wait_ge(max_ready, done(n, 2))
                v.tensor_tensor(ee[:, u, 0:B * K1].rearrange("p (b k) -> p b k", b=B), s0,
                                end(sm[:, u, 0, 0:B], K1), ALU.subtract).then_inc(sub_ready, 1)
                v.tensor_tensor(ee[:, u, B * K1:].rearrange("p (b k) -> p b k", b=B), s1,
                                end(sm[:, u, 0, B:2 * B], K2), ALU.subtract).then_inc(sub_ready, 1)

            def sums(n, u):
                dve.wait_ge(exp_ready, done(n))
                v.reduce_sum(sm[:, u, 1, 0:B], ee[:, u, 0:B * K1].rearrange("p (b k) -> p b k", b=B), axis=AX.X).then_inc(sum_ready, 1)
                v.reduce_sum(sm[:, u, 1, B:2 * B], ee[:, u, B * K1:].rearrange("p (b k) -> p b k", b=B), axis=AX.X).then_inc(sum_ready, 1)
                dve.wait_ge(sum_ready, done(n, 2))
                v.reciprocal(sm[:, u, 2, :], sm[:, u, 1, :]).then_inc(rcp_ready, 1)
                dve.wait_ge(rcp_ready, done(n))
                dve.wait_ge(o_ready, done(n))
                dve.wait_ge(ot_ready, free(n))
                for hd in range(2):
                    v.tensor_tensor(on[:, u, :].rearrange("p (b c) -> p b c", b=B)[:, :, CS * hd:CS * (hd + 1)],
                                    PS[:, 3, hd * P:(hd + 1) * P].rearrange("p (b c) -> p b c", b=B)[:, :, CS * hd:CS * (hd + 1)],
                                    end(sm[:, u, 2, B * hd:B * (hd + 1)], CS), ALU.mult).then_inc(on_ready, 1)

            for n in range(4):
                scores(n, n % 2)
                if n >= 1:
                    sums(n - 1, (n - 1) % 2)
            with dve.Fori(4 // 4, 32 // 4) as step:
                i = step * 4
                for jj in range(4):
                    scores(i + jj, jj % 2)
                    sums(i + jj - 1, (jj - 1) % 2)
            sums(31, 1)
            dve.wait_ge(eca_back, 1)
            v.tensor_tensor(small[:, 32:48], PS[:, 6, 32:48], c_("ec"), ALU.mult).then_inc(eca_step, 1)
            dve.wait_ge(eca_step, steps + 1)
            v.reduce_sum(small[:, 1:2], small[:, 32:48], axis=AX.X).then_inc(eca_step, 1)
            dve.wait_ge(eca_step, steps + 2)
            dve.wait_ge(yext_ready, 2)

            def yc_(n, u):
                dve.wait_ge(po_ready, free(n))
                v.tensor_scalar(grid(two[:, u, 0:CH], W), ye3[:, bass.ds(n * RPC, RPC), 0:W],
                                small[:, 1:2], w_("down_b"), ALU.mult, ALU.add).then_inc(yc_ready, 1)

            def mix(n, u):
                dve.wait_ge(sg_ready, done(n))
                v.tensor_tensor(two[:, u, CH:], two[:, u, CH:], x1[:, bass.ds(n * CH, CH)], ALU.mult).then_inc(gx_ready, 1)
                dve.wait_ge(gx_ready, done(n))
                v.tensor_tensor(two[:, u, 0:CH], two[:, u, 0:CH], two[:, u, CH:], ALU.add).then_inc(tt_ready, 1)

            with dve.Fori(0, NCH // 2) as step:
                i = step * 2
                for u in range(2):
                    yc_(i + u, u)
                for u in range(2):
                    mix(i + u, u)
                for u in range(2):
                    n = i + u
                    dve.wait_ge(po_ready, done(n))
                    v.scalar_tensor_tensor(xp3[:, bass.ds(n * RPC + 1, RPC), 1:1 + W], grid(PS[:, 2 + u, :], W), w_("po_b"),
                                           x03[:, bass.ds(n * RPC, RPC), :], ALU.add, ALU.add).then_inc(xl_ready, 1)
            with dve.Fori(0, NCH // 2) as step:
                i = step * 2
                for u in range(2):
                    n = i + u
                    dve.wait_ge(om_ready, done(n, 2))
                    dve.wait_ge(tr_ready, free(n))
                    dve.wait_ge(om_done, free(n))
                    for h in range(2):
                        v.scalar_tensor_tensor(two[0:PAIRS * OC, u, h * CH:(h + 1) * CH], PS[0:PAIRS * OC, 2 * h + u, :],
                                               bcol[:, :], c_("xg", PAIRS * OC), ALU.add, ALU.add).then_inc(om_out, 1)
            dve.wait_ge(py_out, done(NCH - 1, 2))
            v.tensor_reduce(small[:, 10:11], py, AX.X, ALU.max, apply_absolute_value=True).then_inc(off_max, 1)
            dve.wait_ge(off_row, 1)
            v.reduce_max(small[0:1, 11:12], PS[0:1, 3, 0:P], axis=AX.X).then_inc(off_step, 1)
            dve.wait_ge(off_step, 1)
            v.tensor_scalar(flag[:, :], small[0:1, 11:12], float(BR), None, ALU.is_gt).then_inc(flag_ready, 1)

            def interpolate(p, g, band):
                with dve.Fori(0, H // RPC) as step:
                    y0 = step * RPC
                    dve.wait_ge(aw_ready, p * NCH + NCH + LAST)
                    for r in range(RPC):
                        u = r % 2
                        y = y0 + r
                        n = p * H + y
                        dve.wait_ge(t_ready, done(n))
                        for b in range(3):
                            ins = v.tensor_tensor(
                                uu[:, u, 27 * b:27 * (b + 1), :], PS[:, 3 * u + b, 0:432].rearrange("p (a o) -> p a o", o=C),
                                aw4[:, bass.ds(y, 1), 3 * b:3 * b + 3, :].rearrange("p y k j -> p (y k j)").unsqueeze(2).to_broadcast([P, 27, C]),
                                ALU.mult)
                        ins.then_inc(u_ready, 1)
                        dve.wait_ge(u_ready, done(n))
                        total = os4[:, bass.ds(y, 1), bass.ds(g, 1), :].rearrange("p y g o -> p (y g o)")
                        if band is None:
                            v.tensor_reduce(total, uu[:, u].rearrange("p a o -> p o a"), AX.X, ALU.add).then_inc(os_ready, 1)
                        else:
                            dve.wait_ge(os_ready, n + LAST)
                            v.tensor_reduce(small[:, 16:32], uu[:, u].rearrange("p a o -> p o a"), AX.X, ALU.add).then_inc(part_ready, 1)
                            dve.wait_ge(part_ready, n + 1)
                            v.tensor_tensor(total, total, small[:, 16:32], ALU.add).then_inc(os_ready, 1)

            dve.wait_ge(flag_ready, 1)
            large = dve.value_load(flag[0:1, 0:1], min_val=0, max_val=1)
            with dve.If(large == 0):
                with dve.Fori(0, PAIRS) as g:
                    interpolate(g, g, None)
                dve.wait_ge(os_ready, done(PAIRS * H - 1))
            with dve.Else():
                dve.wait_ge(zeros_ready, 3)
                v.memset(osam, 0.0).then_inc(off_step, 1)
                dve.wait_ge(off_step, 2)
                v.tensor_tensor(py4, py4, c_("yabs").rearrange("p (r k) -> p r k", k=KK).unsqueeze(2).to_broadcast([P, H, PAIRS, KK]),
                                ALU.add).then_inc(abs_ready, 1)
                with dve.Fori(0, PAIRS) as g:
                    with dve.Fori(0, NBLK) as band:
                        interpolate(g * NBLK + band, g, band)
                dve.wait_ge(os_ready, done(NBLK * PAIRS * H - 1))
            with dve.Fori(0, NCH // 2) as step:
                i = step * 2
                for u in range(2):
                    n = i + u
                    dve.wait_ge(ot2_ready, free(n))
                    v.tensor_copy(two[:, u, 0:CH], osam[:, bass.ds(n * CH, CH)]).then_inc(ob_ready, 1)
            dve.wait_ge(z_ready, done(NCH - 1))
            v.reduce_sum(small[:, 2:3], small[:, 8:16], axis=AX.X).then_inc(bn_sum, 1)
            dve.wait_ge(bn_mean, 1)
            v.tensor_scalar(small[:, 4:5], PS[:, 2, 0:1], -1.0 / (B * HW), None, ALU.mult).then_inc(bn_step, 1)
            dve.wait_ge(bn_std, 1)
            v.reciprocal(small[:, 6:7], small[:, 6:7]).then_inc(bn_step, 1)
            dve.wait_ge(bn_step, 2)
            v.tensor_tensor(small[:, 6:7], small[:, 6:7], w_("gamma"), ALU.mult).then_inc(bn_step, 1)
            dve.wait_ge(bn_step, 3)
            v.scalar_tensor_tensor(small[:, 7:8], small[:, 4:5], small[:, 6:7], w_("beta"), ALU.mult, ALU.add).then_inc(bn_aff, 1)
            with dve.Fori(0, 4) as n:
                dve.wait_ge(f_ready, n + 1)
                zc = z[:, bass.ds(n * 1024, 1024)]
                v.tensor_tensor(grid(zc, W), grid(zc, W), xp3[:, bass.ds(n * 16 + 1, 16), 1:1 + W], ALU.add).then_inc(r_ready, 1)

        @block.scalar
        def _(act):
            a = nc.scalar
            for s, n in ((sq_ready, 2), (std_ready, 2), (q_out, 2), (v_out, 2), (exp_ready, 2), (vt_out, 6), (pt_out, 4),
                         (ye_out, 2), (sg_ready, 2), (mk_out, 4), (py_out, 4), (im_out, 6), (ab_ready, 4), (wt_ready, 4), (aa_ready, 2), (ar_ready, 2), (z_ready, 2)):
                act.sem_inc(s, n)
            with act.Fori(0, NCH // 2) as step:
                i = step * 2
                for u in range(2):
                    n = i + u
                    act.wait_ge(bd_ready, 11)
                    act.wait_ge(xc_ready, done(n))
                    act.wait_ge(var_ready, free(n))
                    a.activation(grid(two[:, u, 0:CH], W), xe3[:, bass.ds(n * RPC, RPC), 0:W], ACT.Square).then_inc(sq_ready, 1)
                    act.wait_ge(var_ready, done(n))
                    act.wait_ge(xn_ready, free(n))
                    a.activation(two[:, u, CH:], PS[:, 2 + u, :], ACT.Sqrt, bias=c_("eps_ln")).then_inc(std_ready, 1)
            with act.Fori(0, NCH // 2) as step:
                i = step * 2
                for u in range(2):
                    n = i + u
                    act.wait_ge(qkv_ready, done(n))
                    for dst, bank, s in ((qw, u, q_out), (vw, 4 + u, v_out)):
                        a.activation(dst[:, bass.ds(n * CH, CH)].rearrange("p (j r c) -> p r j c", j=NWR, r=WS),
                                     PS[:, bank, :].rearrange("p (r j c) -> p r j c", j=NWR, r=WS), ACT.Copy).then_inc(s, 1)

            def values(n, u):
                act.wait_ge(vt_ready, done(n))
                act.wait_ge(o_ready, free(n))
                for h in range(2):
                    a.activation(v0[64 * h:64 * (h + 1), u, :, :, h, :],
                                 PS[64 * h:64 * (h + 1), 4, 0:256].rearrange("p (w a b c) -> p w a b c", w=2, a=4, b=2)[:, :, :, h, :],
                                 ACT.Copy).then_inc(vt_out, 1)
                a.activation(v1[:, u].rearrange("p w k -> p (w k)"), PS[:, 4, 256:512], ACT.Copy).then_inc(vt_out, 1)

            def exps(n, u):
                act.wait_ge(sub_ready, done(n, 2))
                a.activation(ee[:, u, :], ee[:, u, :], ACT.Exp, scale=SCALE).then_inc(exp_ready, 1)

            def probs(n, u):
                act.wait_ge(pt_ready, done(n))
                act.wait_ge(o_ready, free(n))
                a.activation(pts[:, u, 0:4, :].rearrange("p t k -> p (t k)"), PS[:, 6, :], ACT.Copy).then_inc(pt_out, 1)
                a.activation(pts[:, u, 4, :], PS[:, 7, 0:P], ACT.Copy).then_inc(pt_out, 1)

            def write(n, row, col):
                act.wait_ge(ot_ready, done(n))
                for_rows = ye3[:, bass.ds(row, WS), col:col + 2 * WS] if not isinstance(row, int) else ye3[:, row:row + WS, col:col + 2 * WS]
                a.activation(for_rows.rearrange("p r (w c) -> p w r c", w=2),
                             PS[:, 5, 0:P].rearrange("p (w r c) -> p w r c", w=2, r=WS), ACT.Copy).then_inc(ye_out, 1)

            act.wait_ge(pads_ready, 2)
            for n in range(4):
                values(n, n % 2)
                exps(n, n % 2)
                if n >= 1:
                    probs(n - 1, (n - 1) % 2)
                if n >= 2:
                    write(n - 2, SHIFT, 16 * (n - 2) + SHIFT)
            with act.Fori(1, NWR) as i:
                for jj in range(4):
                    n = 4 * i + jj
                    values(n, jj % 2)
                    exps(n, jj % 2)
                    probs(n - 1, (jj - 1) % 2)
                    write(n - 2, WS * i + SHIFT - (WS if jj < 2 else 0), 16 * ((jj - 2) % 4) + SHIFT)
            probs(31, 1)
            write(30, WS * (NWR - 1) + SHIFT, 32 + SHIFT)
            write(31, WS * (NWR - 1) + SHIFT, 48 + SHIFT)
            act.wait_ge(eca_pre, 1)
            a.activation(ecab[:, 108:108 + C], ecab[:, 92:92 + C], ACT.Sigmoid).then_inc(eca_gate, 1)
            with act.Fori(0, NCH // 2) as step:
                i = step * 2
                for u in range(2):
                    n = i + u
                    act.wait_ge(gate_ready, done(n))
                    act.wait_ge(tt_ready, free(n))
                    a.activation(two[:, u, CH:], PS[:, u, :], ACT.Sigmoid, bias=r_("sa_b")).then_inc(sg_ready, 1)
            with act.Fori(0, NCH // 2) as step:
                i = step * 2
                for u in range(2):
                    n = i + u
                    act.wait_ge(tr_ready, done(n))
                    for q in range(2):
                        a.activation(py4[:, bass.ds(n * RPC + 4 * q, 4)],
                                     PS[:, 4 + 2 * u + q, 0:4 * PAIRS * OC].rearrange("p (r g k) -> p r g k", r=4, k=OC)[:, :, :, 0:KK],
                                     ACT.Copy).then_inc(py_out, 1)
                        a.activation(mk4[:, bass.ds(n * RPC + 4 * q, 4)],
                                     PS[:, 4 + 2 * u + q, 0:4 * PAIRS * OC].rearrange("p (r g k) -> p r g k", r=4, k=OC)[:, :, :, 2 * KK:3 * KK],
                                     ACT.Sigmoid).then_inc(mk_out, 1)

            def row(n, y, u):
                act.wait_ge(bc_ready, done(n))
                a.activation(ab[:, u, 0:320], PS[:, 6, 0:320], ACT.Abs, bias=c_("negx")).then_inc(ab_ready, 1)
                a.activation(ab[:, u, 320:576], PS[:, 7, 0:256], ACT.Abs, bias=c_("negx")).then_inc(ab_ready, 1)
                act.wait_ge(t_ready, free(n))
                act.wait_ge(ab_ready, done(n, 2))
                for h in range(2):
                    a.activation(wt[W * h:W * (h + 1), u, :, W * h:W * (h + 1)],
                                 ab[W * h:W * (h + 1), u, :].rearrange("p (k c) -> p k c", k=KK), ACT.Relu, bias=1.0, scale=-1.0).then_inc(wt_ready, 1)

            act.wait_ge(zeros_ready, 3)

            def weights(p, g, band):
                act.wait_ge(t_ready, p * H + LAST)
                for yc in range(NCH):
                    n, u = p * NCH + yc, yc % 2
                    act.wait_ge(im_ready, done(n))
                    for b, k in enumerate((3, 3, 2)):
                        r = TOP + RPC * yc + 3 * b
                        a.activation(img4[:, r:r + k], PS[:, 4 * u + b, 0:144 * k].rearrange("p (r k o) -> p r k o", k=KK, o=C), ACT.Copy).then_inc(im_out, 1)
                for yc in range(NCH):
                    n = p * NCH + yc
                    rows = aw4[:, RPC * yc:RPC * (yc + 1)].rearrange("p r k j -> p (r k j)")
                    act.wait_ge(ad_ready, done(n))
                    a.activation(rows, rows, ACT.Abs).then_inc(aa_ready, 1)
                for yc in range(NCH):
                    n = p * NCH + yc
                    rows = aw4[:, RPC * yc:RPC * (yc + 1)].rearrange("p r k j -> p (r k j)")
                    act.wait_ge(aa_ready, done(n))
                    a.activation(rows, rows, ACT.Relu, bias=1.0, scale=-1.0).then_inc(ar_ready, 1)
                with act.Fori(0, H // RPC) as step:
                    y0 = step * RPC
                    for r in range(RPC):
                        row(p * H + y0 + r, y0 + r, r % 2)
            branches(act, weights)
            with act.Fori(0, NCH // 2) as step:
                i = step * 2
                for u in range(2):
                    n = i + u
                    act.wait_ge(ot2_ready, done(n))
                    a.activation(z[:, bass.ds(n * CH, CH)], PS[:, u, :], ACT.Identity, bias=w_("b"),
                                 accum_out=small[:, bass.ds(n + 8, 1)]).then_inc(z_ready, 1)
            act.wait_ge(z_ready, done(NCH - 1))
            act.wait_ge(bn_step, 1)
            a.activation(aw[:, 0:HW], z, ACT.Square, bias=small[:, 4:5], accum_out=small[:, 5:6]).then_inc(bn_sq, 1)
            act.wait_ge(bn_var, 1)
            a.activation(small[:, 6:7], PS[:, 2, 1:2], ACT.Sqrt, bias=c_("eps_bn"), scale=1.0 / (B * HW)).then_inc(bn_std, 1)
            act.wait_ge(bn_aff, 1)
            with act.Fori(0, 4) as n:
                zc = z[:, bass.ds(n * 1024, 1024)]
                a.activation(zc, zc, ACT.Relu, bias=small[:, 7:8], scale=small[:, 6:7]).then_inc(f_ready, 1)

        @block.tensor
        def _(pe):
            def mm(o, l, r, start=True, stop=True):
                return nc.tensor.matmul(o, l, r, start=start, stop=stop)

            for s, n in ((mu_ready, 2), (var_ready, 2), (qkv_ready, 2), (s_ready, 2), (vt_ready, 2), (pt_ready, 2), (o_ready, 2),
                         (ot_ready, 2), (gate_ready, 2), (po_ready, 2), (om_ready, 4), (tr_ready, 2), (im_ready, 2), (bc_ready, 2),
                         (t_ready, 2), (ot2_ready, 2)):
                pe.sem_inc(s, n)
            pe.wait_ge(x_in, 16)
            pe.wait_ge(bd_ready, 11)
            with pe.Fori(0, NCH // 2) as step:
                i = step * 2
                for u in range(2):
                    n = i + u
                    pe.wait_ge(xc_ready, free(n))
                    mm(PS[:, u, :], bd[:, MEAN, :], x0[:, bass.ds(n * CH, CH)]).then_inc(mu_ready, 1)
                for u in range(2):
                    n = i + u
                    pe.wait_ge(sq_ready, done(n))
                    pe.wait_ge(std_ready, free(n))
                    mm(PS[:, 2 + u, :], bd[:, MEAN, :], two[:, u, 0:CH]).then_inc(var_ready, 1)
            pe.wait_ge(ext_ready, 2)
            with pe.Fori(0, NCH // 2) as step:
                i = step * 2
                for u in range(2):
                    n = i + u
                    pe.wait_ge(q_out, free(n))
                    pe.wait_ge(k_out, free(n))
                    pe.wait_ge(v_out, free(n))
                    src = xe3[:, bass.ds(n * WS + SHIFT, WS), SHIFT:SHIFT + W]
                    mm(PS[:, u, :], bd[:, WQ, :], src)
                    mm(PS[:, 2 + u, :], bd[:, WK, :], src)
                    mm(PS[:, 4 + u, :], bd[:, WV, :], src).then_inc(qkv_ready, 1)
            pe.wait_ge(eca_step, 2)
            mm(PS[0:B, 6, 0:C], c_("bmask"), small[:, 16:32]).then_inc(eca_sum, 1)

            def scores(n, u):
                pe.wait_ge(staged, done(n, 4))
                pe.wait_ge(sub_ready, 2 * n + 4)
                for w in range(2):
                    mm(PS[64 * w:64 * (w + 1), u, :], qs[:, u, w, :], kb[:, u, w, :])
                    ins = mm(PS[64 * w:64 * (w + 1), 2, 0:P], qs[:, u, w, :], kvb[:, u, w, 0, :])
                ins.then_inc(s_ready, 1)
                pe.wait_ge(vt_out, 3 * n + 6)
                for w in range(2):
                    nc.tensor.transpose(PS[:, 4, w * P:(w + 1) * P], vs[:, u, w].rearrange("p d k -> p (d k)"), ident)
                    ins = nc.tensor.transpose(PS[:, 4, 256 + w * P:256 + (w + 1) * P], kvb[:, u, w, 1, :], ident)
                ins.then_inc(vt_ready, 1)

            def attend(n, u):
                pe.wait_ge(exp_ready, done(n))
                pe.wait_ge(pt_out, 2 * n + 4)
                for t in range(5):
                    ins = nc.tensor.transpose(PS[:, 6, P * t:P * (t + 1)] if t < 4 else PS[:, 7, 0:P], ee[:, u, P * t:P * (t + 1)], ident)
                ins.then_inc(pt_ready, 1)
                pe.wait_ge(pt_out, done(n, 2))
                pe.wait_ge(vt_out, done(n, 3))
                pe.wait_ge(on_ready, 2 * n + 4)
                for w in range(2):
                    part = slice(64 * w, 64 * (w + 1))
                    for t in range(4):
                        mm(PS[part, 3, 32 * t:32 * (t + 1)], pts[:, u, t, part],
                           v0[:, u, w, t].rearrange("p b c -> p (b c)"))
                    ins = mm(PS[part, 3, P:2 * P], pts[:, u, 4, part], v1[:, u, w, :])
                ins.then_inc(o_ready, 1)

            def back(n, u):
                pe.wait_ge(on_ready, done(n, 2))
                pe.wait_ge(ye_out, n + 2)
                nc.tensor.transpose(PS[:, 5, 0:P], on[:, u, :], ident).then_inc(ot_ready, 1)

            pe.wait_ge(eca_step, 3)
            for n in range(4):
                scores(n, n % 2)
                if n >= 2:
                    back(n - 2, n % 2)
                if n >= 1:
                    attend(n - 1, (n - 1) % 2)
            with pe.Fori(4 // 4, 32 // 4) as step:
                i = step * 4
                for jj in range(4):
                    n = i + jj
                    scores(n, jj % 2)
                    back(n - 2, jj % 2)
                    attend(n - 1, (jj - 1) % 2)
            back(30, 0)
            attend(31, 1)
            back(31, 1)
            pe.wait_ge(eca_gate, 1)
            pe.wait_ge(eca_step, 3)
            pe.wait_ge(pt_out, done(31, 2))
            mm(PS[:, 6, 32:48], cst[0:B, CCOL["bmt"][0]:CCOL["bmt"][1]], ecab[:, 108:108 + C]).then_inc(eca_back, 1)
            with pe.Fori(0, NCH // 2) as step:
                i = step * 2
                for u in range(2):
                    n = i + u
                    pe.wait_ge(yc_ready, done(n))
                    pe.wait_ge(sg_ready, free(n))
                    mm(PS[:, u, :], bd[:, SA, :], two[:, u, 0:CH]).then_inc(gate_ready, 1)
                for u in range(2):
                    n = i + u
                    pe.wait_ge(tt_ready, done(n))
                    pe.wait_ge(xl_ready, free(n))
                    mm(PS[:, 2 + u, :], bd[:, PO, :], two[:, u, 0:CH]).then_inc(po_ready, 1)
            pe.wait_ge(xl_ready, done(NCH - 1))
            pe.wait_ge(pads_ready, 2)
            with pe.Fori(0, NCH // 2) as step:
                i = step * 2
                for u in range(2):
                    n = i + u
                    pe.wait_ge(om_out, free(n, 2))
                    for h in range(2):
                        for t in range(KK):
                            ins = mm(PS[0:PAIRS * OC, 2 * h + u, :], woff[:, h, t, :],
                                     xp3[:, bass.ds(n * RPC + t // 3, RPC), t % 3:t % 3 + W], start=t == 0, stop=t == KK - 1)
                        ins.then_inc(om_ready, 1)
                    pe.wait_ge(om_out, done(n, 2))
                    pe.wait_ge(py_out, free(n, 2))
                    pe.wait_ge(mk_out, free(n, 2))
                    for r in range(RPC):
                        for h in range(2):
                            ins = mm(PS[64 * h:64 * (h + 1), 4 + 2 * u + r // 4, (r % 4) * PAIRS * OC:(r % 4 + 1) * PAIRS * OC],
                                     two[0:PAIRS * OC, u, h * CH + r * W:h * CH + (r + 1) * W], ident[0:PAIRS * OC, 0:PAIRS * OC])
                    ins.then_inc(tr_ready, 1)

            def px(n, y):
                pe.wait_ge(ab_ready, 2 * n + 4)
                for k in range(KK):
                    o = PS[:, 6, W * k:W * (k + 1)] if k < 5 else PS[:, 7, W * (k - 5):W * (k - 4)]
                    ins = mm(o, selb[:, k, :], sx[0:96, bass.ds(y * W, W)])
                ins.then_inc(bc_ready, 1)

            def taps(n, y, u, band):
                pe.wait_ge(wt_ready, done(n, 2))
                pe.wait_ge(u_ready, free(n))
                for k in range(KK):
                    ins = mm(PS[:, 3 * u + k // 3, 144 * (k % 3):144 * (k % 3 + 1)], wt[:, u, k, :],
                             img4[:, bass.ds(y + k // 3 if band is None else band * NR + TOP, NR), k, :])
                ins.then_inc(t_ready, 1)

            pe.wait_ge(py_out, done(NCH - 1, 2))
            pe.wait_ge(mk_out, done(NCH - 1, 2))
            pe.wait_ge(off_max, 1)
            mm(PS[0:1, 3, 0:P], small[:, 10:11], ident).then_inc(off_row, 1)

            def sample(p, g, band):
                pe.wait_ge(u_ready, p * H + LAST)
                pe.wait_ge(ab_ready, 2 * (p * H + LAST))
                for yc in range(NCH):
                    n, u = p * NCH + yc, yc % 2
                    pe.wait_ge(is_ready, done(n, 2))
                    pe.wait_ge(im_out, free(n, 3))
                    for r in range(RPC):
                        ins = mm(PS[:, 4 * u + r // 3, 144 * (r % 3):144 * (r % 3 + 1)],
                                 two[:, u, P * r:P * (r + 1)], w_("w"))
                    ins.then_inc(im_ready, 1)
                pe.wait_ge(im_out, (p * NCH + NCH + LAST) * 3)
                pe.wait_ge(ox_step, 20 * p + 40)
                px(p * H, 0)
                with pe.Fori(0, (H - RPC) // RPC) as step:
                    y0 = step * RPC
                    for r in range(RPC):
                        px(p * H + y0 + r + 1, y0 + r + 1)
                        taps(p * H + y0 + r, y0 + r, r % 2, band)
                for r in range(RPC):
                    y = H - RPC + r
                    if r < RPC - 1:
                        px(p * H + y + 1, y + 1)
                    taps(p * H + y, y, r % 2, band)

            branches(pe, sample)
            with pe.Fori(0, NCH // 2) as step:
                i = step * 2
                for u in range(2):
                    n = i + u
                    pe.wait_ge(ob_ready, done(n))
                    pe.wait_ge(z_ready, free(n))
                    for r in range(RPC):
                        for h in range(2):
                            ins = mm(PS[64 * h:64 * (h + 1), u, W * r:W * (r + 1)], two[:, u, 64 * r:64 * (r + 1)], ident[:, 64 * h:64 * (h + 1)])
                    ins.then_inc(ot2_ready, 1)
            pe.wait_ge(bn_sum, 1)
            mm(PS[:, 2, 0:1], c_("osum"), small[:, 2:3]).then_inc(bn_mean, 1)
            pe.wait_ge(bn_sq, 1)
            mm(PS[:, 2, 1:2], c_("osum"), small[:, 5:6]).then_inc(bn_var, 1)


def kernel(**inputs):
    import concourse.bacc as bacc
    from concourse.bass_utils import run_bass_kernel_spmd as run

    a = {k: np.ascontiguousarray(np.asarray(v)) for k, v in inputs.items()}
    L0, L1 = "L0_conv_", "L1_conv_"

    def head1(m):
        return np.concatenate([np.zeros((CS, m.shape[1]), np.float32), m])

    parts = {
        "wq": a[L0 + "wq"].T, "wk": a[L0 + "wk"].T, "wv": a[L0 + "wv"].T, "po": a[L0 + "po_w"].T, "sa": a[L0 + "sa_w"].T,
        "woff": a[L1 + "w_off"].transpose(1, 2, 3, 0).reshape(C, -1), "w": a[L1 + "w"].transpose(1, 2, 3, 0).reshape(C, -1),
        "ln_w": a[L0 + "ln_w"][:, None], "ln_b": a[L0 + "ln_b"][:, None], "dw_b": a[L0 + "dw_b"][:, None],
        "po_b": a[L0 + "po_b"][:, None], "dw": a[L0 + "dw_w"].reshape(C, KK),
        "down": head1(a[L0 + "down_w"].reshape(CS, 4)), "down_b": head1(a[L0 + "down_b"][:, None]),
        "b": a[L1 + "b"][:, None], "gamma": a[L1 + "gamma"][:, None], "beta": a[L1 + "beta"][:, None],
    }
    rows = {"w1": a[L0 + "eca_w1"], "w2": a[L0 + "eca_w2"], "w3": a[L0 + "eca_w3"], "wc": a[L0 + "eca_wc"], "sa_b": a[L0 + "sa_b"]}
    consts, sel = constants()
    arrays = {
        "x": a["x"],
        "wpack": np.ascontiguousarray(np.concatenate([parts[n] for n, _ in _WCOLS], axis=1)),
        "rpack": np.concatenate([rows[n].reshape(1, -1) for n, _ in _RCOLS], axis=1),
        "boff": a[L1 + "b_off"][:, None],
        "consts": consts, "sel": sel,
    }
    nc = bacc.Bacc("TRN2", target_bir_lowering=False, num_devices=1)
    aps = [nc.dram_tensor("in_" + n, v.shape, F32, kind="ExternalInput").ap() for n, v in arrays.items()]
    o = nc.dram_tensor("out_0", (B, C, H, W), F32, kind="ExternalOutput").ap()
    build(nc, *aps, o)
    r = run(nc, [{"in_" + n: v for n, v in arrays.items()}], core_ids=[0])
    return r.results[0]["out_0"]
```

```python
from contextlib import ExitStack

import numpy as np

import concourse.bass as bass
from concourse import mybir

F32 = mybir.dt.float32
BF16 = mybir.dt.bfloat16
ALU = mybir.AluOpType
ACT = mybir.ActivationFunctionType
AX = mybir.AxisListType

B, C, H, W = 8, 16, 64, 64
HW = H * W
P = B * C
WS = 8
NWR = H // WS
CS = C // 2
SCALE = CS ** -0.5
SHIFT = WS // 2
HE = H + SHIFT
K1 = WS * WS
K2 = (WS // 2) ** 2
CH = 512
NCH = HW // CH
RPC = CH // W
KK = 9
OC = 3 * KK
PAIRS = B // 2
BR = 4
NR = 2 * BR + 1
TOP = BR + 1
NBLK = -(-H // NR)
IR = TOP + NBLK * NR
LN_EPS, BN_EPS = 1e-6, 1e-5
FOLD = 27
AHEAD = NCH

_WCOLS = [("wq", C), ("wk", C), ("wv", C), ("po", C), ("sa", 1), ("woff", KK * OC), ("w", KK * C),
          ("ln_w", 1), ("ln_b", 1), ("dw_b", 1), ("po_b", 1), ("dw", KK), ("down", 4), ("down_b", 1),
          ("b", 1), ("gamma", 1), ("beta", 1)]
_RCOLS = [("w1", 3), ("w2", 3), ("w3", 3), ("wc", 9), ("sa_b", 1)]
_CCOLS = [("ident", P), ("eps_ln", 1), ("eps_bn", 1), ("bmask", B), ("h0", B), ("h1", B), ("ec", C), ("bmt", P), ("osum", P),
          ("negx", 1), ("kxadd", 1), ("xg", CH), ("jrel", NR),
          ("jabs", NBLK * NR), ("yabs", H * KK)]


def _columns(spec):
    at, out = 0, {}
    for name, n in spec:
        out[name] = (at, at + n)
        at += n
    return out, at


WCOL, NWC = _columns(_WCOLS)
RCOL, NRC = _columns(_RCOLS)
CCOL, NCC = _columns(_CCOLS)


def constants():
    c = np.zeros((P, NCC), np.float32)

    def put(name, a):
        c[:a.shape[0], CCOL[name][0]:CCOL[name][1]] = a.reshape(a.shape[0], -1)

    p = np.arange(P)
    bm = (p[:, None] // C == np.arange(B)).astype(np.float32)
    put("ident", np.eye(P, dtype=np.float32))
    put("bmask", bm)
    put("h0", bm * (p[:, None] % C < CS))
    put("h1", bm * (p[:, None] % C >= CS))
    put("ec", (p[:, None] % C == np.arange(C)).astype(np.float32))
    put("bmt", bm.T)
    put("osum", (p[:, None] % C == p[None] % C).astype(np.float32))
    put("negx", -(p[:, None] % W).astype(np.float32))
    ch = np.arange(PAIRS * OC) % OC
    isx = (ch >= KK) & (ch < 2 * KK)
    put("kxadd", (isx * (ch % 3 - 1.0))[:, None].astype(np.float32))
    put("xg", isx[:, None] * (np.arange(CH) % W)[None].astype(np.float32))
    put("jrel", np.tile(np.arange(NR) - float(BR), (P, 1)))
    put("jabs", np.tile(np.arange(NBLK * NR) * 1.0, (P, 1)))
    y, k = np.meshgrid(np.arange(H), np.arange(KK), indexing="ij")
    put("yabs", np.tile((y + k // 3 - 1.0).reshape(1, -1), (P, 1)))
    sel = np.zeros((2, 3, KK, KK, 2, W), np.float32)
    for s in range(3):
        for h in range(2):
            for k in range(KK):
                sel[h, s, k, k, h] = 1.0
    put("eps_ln", np.full((P, 1), LN_EPS))
    put("eps_bn", np.full((P, 1), BN_EPS))
    return c, sel.reshape(2 * 3 * KK, -1)


def build(nc, x, wpack, rpack, boff, consts, selc, out):
    ctx = ExitStack()
    with ctx:
        def sb(name, shape, dt=F32):
            return ctx.enter_context(nc.sbuf_tensor(name, shape, dt))

        def sem(name):
            return ctx.enter_context(nc.semaphore(name))

        px_dram = nc.dram_tensor("px_scratch", (B, 3, KK, HW), BF16, kind="Internal").ap()

        x0t = sb("x0", [P, HW])
        wr = sb("wr", [P, NWC])
        rp = sb("rp", [P, NRC])
        cst = sb("cst", [P, NCC])
        bcol = sb("bcol", [PAIRS * OC, 1])
        xp = sb("xp", [P, (H + 2) * (W + 2)])
        bd = sb("bd", [P, 6, P])
        MEAN, WQ, WK, WV, PO, SA = range(6)
        woff = sb("woff", [P, 2, KK, PAIRS * OC])
        selb = sb("selb", [2 * 3 * KK, KK, P], BF16)
        two = sb("two", [P, 2, 2 * CH])
        small = sb("small", [P, 64])
        ecab = sb("ecab", [B, 128])
        flag = sb("flag", [1, 1], mybir.dt.int32)

        def cutter(name, n):
            region, at = sb(name, [P, n]), [0]

            def cut(k):
                if k is None:
                    at[0] = 0
                    return None
                at[0] += k
                assert at[0] <= n, (name, at[0], n)
                return region[:, at[0] - k:at[0]]
            return cut

        cut = cutter("region", 27680)
        xe = cut(HE * HE)
        qw = cut(HW)
        kw = cut(HW)
        vw = cut(HW)
        kv = cut(NWR * NWR * 2 * K2)
        x1 = cut(HW)
        ye = cut(HE * HE)
        cut(None)
        img = cut(IR * KK * C)
        osam = cut(H * PAIRS * C)
        z = cut(HW)
        sx = z[:, 0:HW // 2].bitcast(BF16)[0:2 * 3 * KK, :]
        aw = cut(H * KK * NR)
        mk = cut(H * PAIRS * KK)
        cut2 = cutter("region2", 7776)
        kb = cut2(2 * 2 * B * K1).rearrange("p (u w k) -> p u w k", u=2, w=2)
        kvb = cut2(2 * 2 * 2 * B * K2).rearrange("p (u w t k) -> p u w t k", u=2, w=2, t=2)
        ee = cut2(2 * B * (K1 + K2)).rearrange("p (u k) -> p u k", u=2)
        pts = cut2(2 * 5 * P).rearrange("p (u t k) -> p u t k", u=2, t=5)
        v0 = cut2(2 * 2 * P).rearrange("p (u w a b c) -> p u w a b c", u=2, w=2, a=4, b=2)
        v1 = cut2(2 * 2 * P).rearrange("p (u w k) -> p u w k", u=2, w=2)
        qs = cut2(2 * 2 * K1).rearrange("p (u w k) -> p u w k", u=2, w=2)
        vs = cut2(2 * 2 * 2 * K1).rearrange("p (u w d k) -> p u w d k", u=2, w=2, d=2)
        on = cut2(2 * P).rearrange("p (u k) -> p u k", u=2)
        sm = cut2(2 * 3 * 2 * B).rearrange("p (u t k) -> p u t k", u=2, t=3)
        cut2(None)
        wt = cut2(2 * KK * P).rearrange("p (u k s) -> p u k s", u=2, k=KK)
        uu = cut2(4 * KK * NR * C).rearrange("p (u a o) -> p u a o", u=4, o=C)
        spl = osam[:, 0:3 * 2 * CH].bitcast(BF16).rearrange("p (u s k) -> p u s k", u=2, s=3)
        rest = osam[0:PAIRS * OC, 3 * 2 * CH:4 * 2 * CH]
        py = x0t[:, 0:H * PAIRS * KK]
        ab = x0t[:, H * PAIRS * KK:H * PAIRS * KK + 2 * KK * W].rearrange("p (u k) -> p u k", u=2)
        x0 = x0t[:, :]

        PS = ctx.enter_context(nc.psum_tensor("PS", [P, 8, 512], F32))

        def w_(name):
            return wr[:, WCOL[name][0]:WCOL[name][1]]

        def r_(name):
            return rp[:, RCOL[name][0]:RCOL[name][1]]

        def c_(name, parts=P):
            return cst[0:parts, CCOL[name][0]:CCOL[name][1]]

        def grid(flat, c):
            return flat.rearrange("p (r c) -> p r c", c=c)

        ident = c_("ident")
        xe3, ye3, x13, xp3 = grid(xe, HE), grid(ye, HE), grid(x1, W), grid(xp[:, :], W + 2)
        x03 = grid(x0, W)
        img4 = img.rearrange("p (r k o) -> p r k o", k=KK, o=C)
        os4 = osam.rearrange("p (r g o) -> p r g o", g=PAIRS, o=C)
        aw4 = aw.rearrange("p (r k j) -> p r k j", k=KK, j=NR)
        mk4 = mk.rearrange("p (r g k) -> p r g k", g=PAIRS, k=KK)
        py4 = py.rearrange("p (r g k) -> p r g k", g=PAIRS, k=KK)
        kv4 = kv.rearrange("p (w t k) -> p w t k", t=2, k=K2)

        def mid(ap, n):
            return ap.unsqueeze(1).to_broadcast([ap.shape[0], n, ap.shape[1]])

        def end(ap, n):
            return ap.unsqueeze(len(ap.shape)).to_broadcast(list(ap.shape) + [n])

        def done(n, per=1):
            return (n + 3) * per

        def free(n, per=1):
            return (n + 1) * per

        x_in, w_in = sem("x_in"), sem("w_in")
        bd_ready, pads_ready = sem("bd_ready"), sem("pads_ready")
        mu_ready, xc_ready, sq_ready, var_ready = sem("mu_ready"), sem("xc_ready"), sem("sq_ready"), sem("var_ready")
        std_ready, rstd_ready, xn_ready, ln_ready = sem("std_ready"), sem("rstd_ready"), sem("xn_ready"), sem("ln_ready")
        ext_ready = sem("ext_ready")
        qkv_ready, q_out, k_out, v_out = sem("qkv_ready"), sem("q_out"), sem("k_out"), sem("v_out")
        down_step, conv_step, eca_step = sem("down_step"), sem("conv_step"), sem("eca_step")
        eca_sum, eca_pre, eca_gate, eca_back = sem("eca_sum"), sem("eca_pre"), sem("eca_gate"), sem("eca_back")
        staged, s_ready, vt_ready, max_ready = sem("staged"), sem("s_ready"), sem("vt_ready"), sem("max_ready")
        sub_ready, exp_ready, sum_ready, rcp_ready = sem("sub_ready"), sem("exp_ready"), sem("sum_ready"), sem("rcp_ready")
        vt_out, pt_ready, pt_out, o_ready = sem("vt_out"), sem("pt_ready"), sem("pt_out"), sem("o_ready")
        on_ready, ot_ready, ye_out, yext_ready = sem("on_ready"), sem("ot_ready"), sem("ye_out"), sem("yext_ready")
        yc_ready, gate_ready, sg_ready, gx_ready = sem("yc_ready"), sem("gate_ready"), sem("sg_ready"), sem("gx_ready")
        tt_ready, po_ready, xl_ready = sem("tt_ready"), sem("po_ready"), sem("xl_ready")
        om_ready, om_out, tr_ready, py_out, mk_out = sem("om_ready"), sem("om_out"), sem("tr_ready"), sem("py_out"), sem("mk_out")
        hi_ready, rest_ready, mid_ready, lo_ready = sem("hi_ready"), sem("rest_ready"), sem("mid_ready"), sem("lo_ready")
        px_done = sem("px_done")
        px_stored = [sem("px_stored0"), sem("px_stored1")]
        zeros_ready = sem("zeros_ready")
        pool_turn = sem("pool_turn")
        act_turn = sem("act_turn")
        px_in, px_ready, row_out, fold_ready = sem("px_in"), sem("px_ready"), sem("row_out"), sem("fold_ready")
        is_ready, im_ready, im_out = sem("is_ready"), sem("im_ready"), sem("im_out")
        ad_ready, aa_ready, ar_ready, aw_ready = sem("ad_ready"), sem("aa_ready"), sem("ar_ready"), sem("aw_ready")
        bc_ready, ab_ready, wt_ready, t_ready = sem("bc_ready"), sem("ab_ready"), sem("wt_ready"), sem("t_ready")
        u_ready, os_ready = sem("u_ready"), sem("os_ready")
        off_max, off_row, off_step, flag_ready = sem("off_max"), sem("off_row"), sem("off_step"), sem("flag_ready")
        abs_ready, part_ready = sem("abs_ready"), sem("part_ready")
        ob_ready, ot2_ready, z_ready, bn_step = sem("ob_ready"), sem("ot2_ready"), sem("z_ready"), sem("bn_step")
        bn_sum, bn_mean, bn_sq, bn_var, bn_std, bn_aff = [sem("bn_" + n) for n in "sum mean sq var std aff".split()]
        f_ready, r_ready, stored = sem("f_ready"), sem("r_ready"), sem("stored")

        def branches(eng, streams, passes):
            eng.wait_ge(flag_ready, 1)
            large = eng.value_load(flag[0:1, 0:1], min_val=0, max_val=1)
            with eng.If(large == 0):
                streams()
                eng.nop()
            with eng.Else():
                with eng.Fori(0, PAIRS) as g:
                    with eng.Fori(0, NBLK) as band:
                        passes(g * NBLK + band, g, band)
                eng.nop()

        def stream(eng, pair):
            def chunks(f):
                f(0, 0)
                with eng.Fori(0, (NCH - 2) // 2) as i:
                    f(2 * i + 1, 1)
                    f(2 * i + 2, 0)
                f(NCH - 1, 1)
            with eng.Fori(0, PAIRS - 1) as g:
                pair(g, False, chunks)
            pair(PAIRS - 1, True, chunks)

        block = ctx.enter_context(nc.Block())
        LAST = 2

        @block.sync
        def _(sp):
            sp.dma_start(x0, x.rearrange("b c h w -> (b c) (h w)")).then_inc(x_in, 16)
            for b in range(B):
                sp.dma_start(wr[C * b:C * (b + 1), :], wpack).then_inc(w_in, 16)
            sp.dma_start(rp[:, :], rpack.to_broadcast([P, NRC])).then_inc(w_in, 16)
            sp.dma_start(cst[:, :], consts).then_inc(w_in, 16)
            for b in range(PAIRS):
                sp.dma_start(bcol[OC * b:OC * (b + 1), :], boff).then_inc(w_in, 16)
            sp.dma_start(two[0:2 * 3 * KK, :, :].rearrange("p a b -> p (a b)")[:, 0:KK * P], selc).then_inc(w_in, 16)

            sp.sem_inc(px_done, 2)
            with sp.Fori(0, NCH // 2) as step:
                i = step * 2
                for u in range(2):
                    n = i + u
                    sp.wait_ge(lo_ready, done(n))
                    for b in range(B):
                        row, h = OC * (b % PAIRS) + KK, b // PAIRS
                        sp.dma_start(px_dram[b, :, :, bass.ds(n * CH, CH)].rearrange("s k c -> k s c"),
                                     spl[row:row + KK, u, :, h * CH:(h + 1) * CH]).then_inc(px_stored[u], 16)
                    sp.wait_ge(px_stored[u], 16 * B * (step + 1))
                    sp.sem_inc(px_done, 1)

            def load_px(count, g, first, n):
                for h in range(2):
                    sp.dma_start(sx[3 * KK * h:3 * KK * (h + 1), bass.ds(first, n)],
                                 px_dram[bass.ds(g + h * PAIRS, 1), :, :, bass.ds(first, n)].rearrange("b s k c -> (b s k) c")).then_inc(px_in, 16)
                sp.wait_ge(px_in, 32 * count + 32)
                sp.sem_inc(px_ready, 1)

            def all_px():
                with sp.Fori(0, NCH) as c:
                    load_px(c, 0, c * CH, CH)

                def next_px(g):
                    with sp.Fori(0, NCH) as c:
                        sp.wait_ge(bc_ready, done(g * H + c * RPC + RPC - 1))
                        load_px((g + 1) * NCH + c, g + 1, c * CH, CH)
                with sp.Fori(0, PAIRS - 1) as g:
                    next_px(g)

            def pass_px(p, g, band):
                sp.wait_ge(bc_ready, p * H + LAST)
                load_px(p, g, 0, HW)

            branches(sp, all_px, pass_px)
            with sp.Fori(0, 4) as n:
                sp.wait_ge(r_ready, n + 1)
                sp.dma_start(out.rearrange("b c h w -> (b c) (h w)")[:, bass.ds(n * 1024, 1024)],
                             z[:, bass.ds(n * 1024, 1024)]).then_inc(stored, 16)
            sp.wait_ge(stored, 64)

        @block.gpsimd
        def _(pool):
            pool.memset(v0, 0.0).then_inc(pads_ready, 1)
            pool.memset(xp[:, :], 0.0).then_inc(pads_ready, 1)
            pool.wait_ge(ln_ready, done(NCH - 1))
            pool.tensor_copy(xe3[:, H:HE, 0:W], xe3[:, 0:SHIFT, 0:W]).then_inc(ext_ready, 1)
            pool.wait_ge(ext_ready, 1)
            pool.tensor_copy(xe3[:, :, W:HE], xe3[:, :, 0:SHIFT]).then_inc(ext_ready, 1)
            pool.sem_inc(staged, 8)
            pool.wait_ge(k_out, done(NCH - 1))
            pool.wait_ge(q_out, done(NCH - 1))
            pool.wait_ge(v_out, done(NCH - 1))
            pool.wait_ge(down_step, 8)
            with pool.Fori(0, 32 // 2) as step:
                i = step * 2
                for u in range(2):
                    n = i + u
                    pool.wait_ge(vt_ready, free(n))
                    pool.sem_inc(pool_turn, 1)
                    pool.tensor_copy(qs[:, u], qw[:, bass.ds(n * 2 * K1, 2 * K1)].rearrange("p (w k) -> p w k", w=2)).then_inc(staged, 1)
                    pool.tensor_copy(vs[:, u], vw[:, bass.ds(n * 2 * K1, 2 * K1)].rearrange("p (w k) -> p w k", w=2).unsqueeze(2).to_broadcast([P, 2, 2, K1])).then_inc(staged, 1)
                    pool.tensor_tensor(
                        kb[:, u].rearrange("p w (b k) -> p w b k", b=B),
                        kw[:, bass.ds(n * 2 * K1, 2 * K1)].rearrange("p (w k) -> p w k", w=2).unsqueeze(2).to_broadcast([P, 2, B, K1]),
                        mid(c_("h0"), 2).unsqueeze(3).to_broadcast([P, 2, B, K1]), ALU.mult).then_inc(staged, 1)
                    pool.tensor_tensor(
                        kvb[:, u].rearrange("p w t (b k) -> p (w t) b k", b=B),
                        kv[:, bass.ds(n * 4 * K2, 4 * K2)].rearrange("p (w k) -> p w k", w=4).unsqueeze(2).to_broadcast([P, 4, B, K2]),
                        mid(c_("h1"), 4).unsqueeze(3).to_broadcast([P, 4, B, K2]), ALU.mult).then_inc(staged, 1)
            pool.wait_ge(ye_out, done(31))
            pool.tensor_copy(ye3[:, 0:SHIFT, SHIFT:HE], ye3[:, H:HE, SHIFT:HE]).then_inc(yext_ready, 1)
            pool.wait_ge(yext_ready, 1)
            pool.tensor_copy(ye3[:, 0:H, 0:SHIFT], ye3[:, 0:H, W:HE]).then_inc(yext_ready, 1)
            pool.sem_inc(rest_ready, 2)
            with pool.Fori(0, NCH // 2) as step:
                i = step * 2
                for u in range(2):
                    n = i + u
                    pool.wait_ge(hi_ready, done(n))
                    pool.wait_ge(lo_ready, n + 2)
                    pool.sem_inc(pool_turn, 1)
                    pool.tensor_tensor(rest, two[0:PAIRS * OC, u, :], spl[0:PAIRS * OC, u, 0, :], ALU.subtract).then_inc(rest_ready, 1)
            pool.memset(img, 0.0).then_inc(zeros_ready, 1)
            pool.memset(wt, 0.0).then_inc(zeros_ready, 1)
            pool.sem_inc(is_ready, 4)
            pool.sem_inc(ad_ready, 2)
            pool.sem_inc(aw_ready, 2)
            pool.sem_inc(fold_ready, 2)
            pool.wait_ge(tr_ready, done(NCH - 1))
            pool.wait_ge(py_out, done(NCH - 1, 2))
            pool.wait_ge(mk_out, done(NCH - 1, 2))

            def stage(g, yc, u, h):
                pool.tensor_tensor(
                    two[:, u, :].rearrange("p (r h c) -> p r h c", h=2, c=W)[:, :, h, :],
                    xp3[:, bass.ds(RPC * yc + 1, RPC), 1:1 + W],
                    c_("bmask")[:, bass.ds(g + h * PAIRS, 1)].unsqueeze(2).to_broadcast([P, RPC, W]),
                    ALU.mult).then_inc(is_ready, 1)

            def difference(g, yc, rows_of_band):
                rows = bass.ds(RPC * yc, RPC)
                pool.tensor_tensor(
                    aw4[:, rows],
                    py4[:, rows, bass.ds(g, 1), :].rearrange("p r g k -> p (r g) k").unsqueeze(3).to_broadcast([P, RPC, KK, NR]),
                    mid(rows_of_band, RPC).unsqueeze(2).to_broadcast([P, RPC, KK, NR]), ALU.subtract).then_inc(ad_ready, 1)

            def modulate(n, g, yc):
                rows = bass.ds(RPC * yc, RPC)
                pool.wait_ge(ar_ready, done(n))
                pool.sem_inc(pool_turn, 1)
                pool.tensor_tensor(
                    aw4[:, rows], aw4[:, rows],
                    mk4[:, rows, bass.ds(g, 1), :].rearrange("p r g k -> p (r g) k").unsqueeze(3).to_broadcast([P, RPC, KK, NR]),
                    ALU.mult).then_inc(aw_ready, 1)

            def tables_ahead():
                pool.wait_ge(zeros_ready, 2)
                with pool.Fori(0, NCH // 2) as step:
                    for u in range(2):
                        yc = step * 2 + u
                        pool.wait_ge(im_ready, free(yc))
                        pool.sem_inc(pool_turn, 1)
                        for h in range(2):
                            stage(0, yc, u, h)
                difference(0, 0, c_("jrel"))
                modulate(0, 0, 0)

                def pair(g, last, chunks):
                    def chunk(c, u, end=False):
                        s = g * NCH + c
                        for r in range(RPC):
                            pool.wait_ge(u_ready, done(s * RPC + r))
                            pool.sem_inc(pool_turn, 1)
                            pool.tensor_tensor(uu[:, r % 4, FOLD:2 * FOLD, :], uu[:, r % 4, FOLD:2 * FOLD, :],
                                               uu[:, r % 4, 0:FOLD, :], ALU.add).then_inc(fold_ready, 1)
                            if r == 0 and not last:
                                pool.wait_ge(bc_ready, done(s * RPC))
                                pool.sem_inc(pool_turn, 1)
                            if r in (1, 2) and not last:
                                stage(g + 1, c, u, r - 1)
                            nxt = (g + 1, 0) if end else (g, c + 1)
                            if r == 0 and not (last and end):
                                difference(*nxt, c_("jrel"))
                            if r == 6 and not (last and end):
                                modulate(s + 1, *nxt)
                    chunks(lambda c, u: chunk(c, u, isinstance(c, int) and c == NCH - 1))
                stream(pool, pair)

            def tables(p, g, band):
                pool.wait_ge(zeros_ready, 2)
                for yc in range(NCH):
                    pool.wait_ge(im_ready, free(p * NCH + yc))
                    pool.sem_inc(pool_turn, 1)
                    for h in range(2):
                        stage(g, yc, yc % 2, h)
                pool.wait_ge(abs_ready, 1)
                pool.wait_ge(u_ready, p * H + LAST)
                pool.sem_inc(pool_turn, 1)
                for yc in range(NCH):
                    difference(g, yc, c_("jabs")[:, bass.ds(band * NR, NR)])
                for yc in range(NCH):
                    modulate(p * NCH + yc, g, yc)

            branches(pool, tables_ahead, tables)

        @block.vector
        def _(dve):
            v = nc.vector
            for s, n in ((xc_ready, 2), (rstd_ready, 2), (xn_ready, 2), (ln_ready, 2), (k_out, 2),
                         (max_ready, 4), (sub_ready, 4), (sum_ready, 4), (rcp_ready, 2), (on_ready, 4),
                         (yc_ready, 2), (gx_ready, 2), (tt_ready, 2), (xl_ready, 2), (om_out, 4),
                         (mid_ready, 2), (lo_ready, 2), (u_ready, 2), (os_ready, 2), (ob_ready, 2)):
                dve.sem_inc(s, n)
            dve.wait_ge(w_in, 240)
            bm = c_("bmask")
            v.tensor_scalar(bd[:, MEAN, :].rearrange("p (b c) -> p b c", b=B), end(bm, C), 1.0 / C, None, ALU.mult).then_inc(bd_ready, 1)
            for slot, name in ((WQ, "wq"), (WK, "wk"), (WV, "wv"), (PO, "po")):
                v.tensor_tensor(bd[:, slot, :].rearrange("p (b c) -> p b c", b=B), mid(w_(name), B), end(bm, C), ALU.mult).then_inc(bd_ready, 1)
            v.tensor_scalar(bd[:, SA, :].rearrange("p (b c) -> p b c", b=B), end(bm, C), w_("sa"), None, ALU.mult).then_inc(bd_ready, 1)
            for h in range(2):
                v.tensor_tensor(
                    woff[:, h].rearrange("p t (b k) -> p t b k", b=PAIRS),
                    w_("woff").rearrange("p (t k) -> p t k", k=OC).unsqueeze(2).to_broadcast([P, KK, PAIRS, OC]),
                    mid(bm[:, PAIRS * h:PAIRS * (h + 1)], KK).unsqueeze(3).to_broadcast([P, KK, PAIRS, OC]),
                    ALU.mult).then_inc(bd_ready, 1)
            v.tensor_copy(selb[:, :, :].rearrange("p k m -> p (k m)"), two[0:2 * 3 * KK, :, :].rearrange("p a b -> p (a b)")[:, 0:KK * P]).then_inc(bd_ready, 1)
            v.tensor_scalar(bcol[:, :], bcol[:, :], c_("kxadd", PAIRS * OC), None, ALU.add).then_inc(bd_ready, 1)
            v.memset(ecab[:, :], 0.0).then_inc(bd_ready, 1)
            dve.wait_ge(bd_ready, 11)
            with dve.Fori(0, NCH // 2) as step:
                i = step * 2
                for u in range(2):
                    n = i + u
                    rows = xe3[:, bass.ds(n * RPC, RPC), 0:W]
                    dve.wait_ge(mu_ready, done(n))
                    v.tensor_tensor(rows, x03[:, bass.ds(n * RPC, RPC), :], grid(PS[:, u, :], W), ALU.subtract).then_inc(xc_ready, 1)
                    dve.wait_ge(std_ready, done(n))
                    v.reciprocal(two[:, u, CH:2 * CH], two[:, u, CH:2 * CH]).then_inc(rstd_ready, 1)
                    dve.wait_ge(rstd_ready, done(n))
                    dve.wait_ge(xc_ready, done(n))
                    v.tensor_tensor(rows, rows, grid(two[:, u, CH:2 * CH], W), ALU.mult).then_inc(xn_ready, 1)
                    dve.wait_ge(xn_ready, done(n))
                    v.tensor_scalar(rows, rows, w_("ln_w"), w_("ln_b"), ALU.mult, ALU.add).then_inc(ln_ready, 1)
            with dve.Fori(0, NCH // 2) as step:
                i = step * 2
                for u in range(2):
                    n = i + u
                    dve.wait_ge(qkv_ready, done(n))
                    v.tensor_copy(kw[:, bass.ds(n * CH, CH)].rearrange("p (j r c) -> p r j c", j=NWR, r=WS),
                                  PS[:, 2 + u, :].rearrange("p (r j c) -> p r j c", j=NWR, r=WS)).then_inc(k_out, 1)
            dve.wait_ge(k_out, done(NCH - 1))
            dve.wait_ge(v_out, done(NCH - 1))
            for tap in range(4):
                for t, src in enumerate((kw, vw)):
                    o = kv4[:, :, t, :].rearrange("p w (r s) -> p w r s", r=4)
                    s4 = src.rearrange("p (w r a s b) -> p a b w r s", r=4, a=2, s=4, b=2)[:, tap // 2, tap % 2]
                    if tap == 0:
                        ins = v.tensor_scalar(o, s4, w_("down")[:, 0:1], w_("down_b") if t == 0 else 0.0, ALU.mult, ALU.add)
                    else:
                        dve.wait_ge(down_step, 2 * tap - 1 + t)
                        ins = v.scalar_tensor_tensor(o, s4, w_("down")[:, tap:tap + 1], o, ALU.mult, ALU.add)
                    ins.then_inc(down_step, 1)
            taps = [(0, 0)] + [(dy, dx) for dy in (-1, 0, 1) for dx in (-1, 0, 1) if (dy, dx) != (0, 0)]
            for n, (dy, dx) in enumerate(taps):
                wcol = w_("dw")[:, 3 * (dy + 1) + dx + 1:3 * (dy + 1) + dx + 2]
                if n == 0:
                    ins = v.tensor_scalar(x13, xe3[:, 0:H, 0:W], wcol, w_("dw_b"), ALU.mult, ALU.add)
                else:
                    ra, rb, ca, cb = max(0, -dy), H - max(0, dy), max(0, -dx), W - max(0, dx)
                    dve.wait_ge(conv_step, n)
                    ins = v.scalar_tensor_tensor(x13[:, ra:rb, ca:cb], xe3[:, ra + dy:rb + dy, ca + dx:cb + dx], wcol,
                                                 x13[:, ra:rb, ca:cb], ALU.mult, ALU.add)
                ins.then_inc(conv_step, 1)
            dve.wait_ge(conv_step, 9)
            v.reduce_sum(small[:, 0:1], x1, axis=AX.X).then_inc(eca_step, 1)
            dve.wait_ge(eca_step, 1)
            v.tensor_scalar(small[:, 16:32], c_("ec"), small[:, 0:1], None, ALU.mult).then_inc(eca_step, 1)
            dve.wait_ge(eca_sum, 1)
            v.tensor_scalar(ecab[:, 4:20], PS[0:B, 6, 0:C], 1.0 / HW, None, ALU.mult).then_inc(eca_step, 1)
            dve.wait_ge(eca_step, 3)
            steps = 3
            for t in range(3):
                for j, d in enumerate((1, 2, 4)):
                    zz = ecab[:, 33 + 20 * j:33 + 20 * j + C]
                    src = ecab[:, 4 + (t - 1) * d:4 + (t - 1) * d + C]
                    wc = r_("w%d" % (j + 1))[0:B, t:t + 1]
                    if t == 0:
                        ins = v.tensor_scalar(zz, src, wc, None, ALU.mult)
                    else:
                        dve.wait_ge(eca_step, steps - 2)
                        ins = v.scalar_tensor_tensor(zz, src, wc, zz, ALU.mult, ALU.add)
                    ins.then_inc(eca_step, 1)
                    steps += 1
            for j in range(3):
                for t in range(3):
                    src = ecab[:, 32 + 20 * j + t:32 + 20 * j + t + C]
                    wc = r_("wc")[0:B, 3 * j + t:3 * j + t + 1]
                    acc = ecab[:, 92:92 + C]
                    dve.wait_ge(eca_step, steps)
                    if j == t == 0:
                        ins = v.tensor_scalar(acc, src, wc, None, ALU.mult)
                    else:
                        ins = v.scalar_tensor_tensor(acc, src, wc, acc, ALU.mult, ALU.add)
                    ins.then_inc(eca_step, 1)
                    steps += 1
            dve.wait_ge(eca_step, steps)
            v.tensor_copy(ecab[:, 92:92 + C], ecab[:, 92:92 + C]).then_inc(eca_pre, 1)

            def scores(n, u):
                dve.wait_ge(s_ready, done(n))
                s0 = PS[:, u, :].rearrange("p (b k) -> p b k", b=B)
                s1 = PS[:, 2, 0:P].rearrange("p (b k) -> p b k", b=B)
                v.reduce_max(sm[:, u, 0, 0:B], s0, axis=AX.X).then_inc(max_ready, 1)
                v.reduce_max(sm[:, u, 0, B:2 * B], s1, axis=AX.X).then_inc(max_ready, 1)
                dve.wait_ge(pt_ready, free(n))
                dve.wait_ge(max_ready, done(n, 2))
                v.tensor_tensor(ee[:, u, 0:B * K1].rearrange("p (b k) -> p b k", b=B), s0,
                                end(sm[:, u, 0, 0:B], K1), ALU.subtract).then_inc(sub_ready, 1)
                v.tensor_tensor(ee[:, u, B * K1:].rearrange("p (b k) -> p b k", b=B), s1,
                                end(sm[:, u, 0, B:2 * B], K2), ALU.subtract).then_inc(sub_ready, 1)

            def sums(n, u):
                dve.wait_ge(exp_ready, done(n))
                v.reduce_sum(sm[:, u, 1, 0:B], ee[:, u, 0:B * K1].rearrange("p (b k) -> p b k", b=B), axis=AX.X).then_inc(sum_ready, 1)
                v.reduce_sum(sm[:, u, 1, B:2 * B], ee[:, u, B * K1:].rearrange("p (b k) -> p b k", b=B), axis=AX.X).then_inc(sum_ready, 1)
                dve.wait_ge(sum_ready, done(n, 2))
                v.reciprocal(sm[:, u, 2, :], sm[:, u, 1, :]).then_inc(rcp_ready, 1)
                dve.wait_ge(rcp_ready, done(n))
                dve.wait_ge(o_ready, done(n))
                dve.wait_ge(ot_ready, free(n))
                for hd in range(2):
                    v.tensor_tensor(on[:, u, :].rearrange("p (b c) -> p b c", b=B)[:, :, CS * hd:CS * (hd + 1)],
                                    PS[:, 3, hd * P:(hd + 1) * P].rearrange("p (b c) -> p b c", b=B)[:, :, CS * hd:CS * (hd + 1)],
                                    end(sm[:, u, 2, B * hd:B * (hd + 1)], CS), ALU.mult).then_inc(on_ready, 1)

            for n in range(4):
                scores(n, n % 2)
                if n >= 1:
                    sums(n - 1, (n - 1) % 2)
            with dve.Fori(4 // 4, 32 // 4) as step:
                i = step * 4
                for jj in range(4):
                    scores(i + jj, jj % 2)
                    sums(i + jj - 1, (jj - 1) % 2)
            sums(31, 1)
            dve.wait_ge(eca_back, 1)
            v.tensor_tensor(small[:, 32:48], PS[:, 6, 32:48], c_("ec"), ALU.mult).then_inc(eca_step, 1)
            dve.wait_ge(eca_step, steps + 1)
            v.reduce_sum(small[:, 1:2], small[:, 32:48], axis=AX.X).then_inc(eca_step, 1)
            dve.wait_ge(eca_step, steps + 2)
            dve.wait_ge(yext_ready, 2)

            def yc_(n, u):
                dve.wait_ge(po_ready, free(n))
                v.tensor_scalar(grid(two[:, u, 0:CH], W), ye3[:, bass.ds(n * RPC, RPC), 0:W],
                                small[:, 1:2], w_("down_b"), ALU.mult, ALU.add).then_inc(yc_ready, 1)

            def mix(n, u):
                dve.wait_ge(sg_ready, done(n))
                v.tensor_tensor(two[:, u, CH:], two[:, u, CH:], x1[:, bass.ds(n * CH, CH)], ALU.mult).then_inc(gx_ready, 1)
                dve.wait_ge(gx_ready, done(n))
                v.tensor_tensor(two[:, u, 0:CH], two[:, u, 0:CH], two[:, u, CH:], ALU.add).then_inc(tt_ready, 1)

            with dve.Fori(0, NCH // 2) as step:
                i = step * 2
                for u in range(2):
                    yc_(i + u, u)
                for u in range(2):
                    mix(i + u, u)
                for u in range(2):
                    n = i + u
                    dve.wait_ge(po_ready, done(n))
                    v.scalar_tensor_tensor(xp3[:, bass.ds(n * RPC + 1, RPC), 1:1 + W], grid(PS[:, 2 + u, :], W), w_("po_b"),
                                           x03[:, bass.ds(n * RPC, RPC), :], ALU.add, ALU.add).then_inc(xl_ready, 1)
            with dve.Fori(0, NCH // 2) as step:
                i = step * 2
                for u in range(2):
                    n = i + u
                    dve.wait_ge(om_ready, done(n, 2))
                    dve.wait_ge(tr_ready, free(n))
                    dve.wait_ge(rest_ready, free(n))
                    for h in range(2):
                        v.scalar_tensor_tensor(two[0:PAIRS * OC, u, h * CH:(h + 1) * CH], PS[0:PAIRS * OC, 2 * h + u, :],
                                               bcol[:, :], c_("xg", PAIRS * OC), ALU.add, ALU.add).then_inc(om_out, 1)
                    dve.wait_ge(rest_ready, done(n))
                    v.tensor_copy(spl[0:PAIRS * OC, u, 1, :], rest).then_inc(mid_ready, 1)
                    dve.wait_ge(mid_ready, done(n))
                    v.tensor_tensor(spl[0:PAIRS * OC, u, 2, :], rest, spl[0:PAIRS * OC, u, 1, :], ALU.subtract).then_inc(lo_ready, 1)
            dve.wait_ge(py_out, done(NCH - 1, 2))
            v.tensor_reduce(small[:, 10:11], py, AX.X, ALU.max, apply_absolute_value=True).then_inc(off_max, 1)
            dve.wait_ge(off_row, 1)
            v.reduce_max(small[0:1, 11:12], PS[0:1, 3, 0:P], axis=AX.X).then_inc(off_step, 1)
            dve.wait_ge(off_step, 1)
            v.tensor_scalar(flag[:, :], small[0:1, 11:12], float(BR), None, ALU.is_gt).then_inc(flag_ready, 1)

            def products(n, y, u, u4):
                dve.wait_ge(t_ready, done(n))
                v.tensor_tensor(
                    uu[:, u4].rearrange("p (b a) o -> p b a o", b=3), PS[:, 3 * u:3 * u + 3, 0:432].rearrange("p b (a o) -> p b a o", o=C),
                    aw4[:, bass.ds(y, 1), :, :].rearrange("p y (b k) j -> p (y b) (k j)", b=3).unsqueeze(3).to_broadcast([P, 3, 3 * NR, C]),
                    ALU.mult).then_inc(u_ready, 1)

            def total(y, g):
                return os4[:, bass.ds(y, 1), bass.ds(g, 1), :].rearrange("p y g o -> p (y g o)")

            def interpolate_all():
                def pair(g, last, chunks):
                    def add(n, y, u):
                        dve.wait_ge(fold_ready, done(n))
                        v.tensor_reduce(total(y, g), uu[:, u, FOLD:, :].rearrange("p a o -> p o a"), AX.X, ALU.add).then_inc(os_ready, 1)

                    def chunk(c, u):
                        s = g * NCH + c
                        dve.wait_ge(aw_ready, done(s))
                        for r in range(RPC):
                            products(s * RPC + r, c * RPC + r, r % 2, r % 4)
                            if r > 0 or not isinstance(c, int) or c > 0:
                                add(s * RPC + r - 1, c * RPC + r - 1, (r - 1) % 4)
                    chunks(chunk)
                    add(g * H + H - 1, H - 1, 3)
                stream(dve, pair)

            def interpolate(p, g, band):
                with dve.Fori(0, H // RPC) as step:
                    y0 = step * RPC
                    dve.wait_ge(aw_ready, p * NCH + NCH + LAST)
                    for r in range(RPC):
                        u = r % 2
                        y = y0 + r
                        n = p * H + y
                        products(n, y, u, u)
                        dve.wait_ge(u_ready, done(n))
                        dve.wait_ge(os_ready, n + LAST)
                        v.tensor_reduce(small[:, 16:32], uu[:, u].rearrange("p a o -> p o a"), AX.X, ALU.add).then_inc(part_ready, 1)
                        dve.wait_ge(part_ready, n + 1)
                        v.tensor_tensor(total(y, g), total(y, g), small[:, 16:32], ALU.add).then_inc(os_ready, 1)

            dve.wait_ge(flag_ready, 1)
            large = dve.value_load(flag[0:1, 0:1], min_val=0, max_val=1)
            with dve.If(large == 0):
                interpolate_all()
                dve.wait_ge(os_ready, done(PAIRS * H - 1))
            with dve.Else():
                dve.wait_ge(px_done, done(NCH - 1))
                v.memset(osam, 0.0).then_inc(off_step, 1)
                dve.wait_ge(off_step, 2)
                v.tensor_tensor(py4, py4, c_("yabs").rearrange("p (r k) -> p r k", k=KK).unsqueeze(2).to_broadcast([P, H, PAIRS, KK]),
                                ALU.add).then_inc(abs_ready, 1)
                with dve.Fori(0, PAIRS) as g:
                    with dve.Fori(0, NBLK) as band:
                        interpolate(g * NBLK + band, g, band)
                dve.wait_ge(os_ready, done(NBLK * PAIRS * H - 1))
            with dve.Fori(0, NCH // 2) as step:
                i = step * 2
                for u in range(2):
                    n = i + u
                    dve.wait_ge(ot2_ready, free(n))
                    v.tensor_copy(two[:, u, 0:CH], osam[:, bass.ds(n * CH, CH)]).then_inc(ob_ready, 1)
            dve.wait_ge(z_ready, done(NCH - 1))
            v.reduce_sum(small[:, 2:3], small[:, 8:16], axis=AX.X).then_inc(bn_sum, 1)
            dve.wait_ge(bn_mean, 1)
            v.tensor_scalar(small[:, 4:5], PS[:, 2, 0:1], -1.0 / (B * HW), None, ALU.mult).then_inc(bn_step, 1)
            dve.wait_ge(bn_std, 1)
            v.reciprocal(small[:, 6:7], small[:, 6:7]).then_inc(bn_step, 1)
            dve.wait_ge(bn_step, 2)
            v.tensor_tensor(small[:, 6:7], small[:, 6:7], w_("gamma"), ALU.mult).then_inc(bn_step, 1)
            dve.wait_ge(bn_step, 3)
            v.scalar_tensor_tensor(small[:, 7:8], small[:, 4:5], small[:, 6:7], w_("beta"), ALU.mult, ALU.add).then_inc(bn_aff, 1)
            with dve.Fori(0, 4) as n:
                dve.wait_ge(f_ready, n + 1)
                zc = z[:, bass.ds(n * 1024, 1024)]
                v.tensor_tensor(grid(zc, W), grid(zc, W), xp3[:, bass.ds(n * 16 + 1, 16), 1:1 + W], ALU.add).then_inc(r_ready, 1)

        @block.scalar
        def _(act):
            a = nc.scalar
            for s, n in ((sq_ready, 2), (std_ready, 2), (q_out, 2), (v_out, 2), (exp_ready, 2), (vt_out, 6), (pt_out, 4),
                         (ye_out, 2), (sg_ready, 2), (hi_ready, 2), (row_out, 2), (mk_out, 4), (py_out, 4), (im_out, 6), (ab_ready, 4), (wt_ready, 4), (aa_ready, 2), (ar_ready, 2), (z_ready, 2)):
                act.sem_inc(s, n)
            with act.Fori(0, NCH // 2) as step:
                i = step * 2
                for u in range(2):
                    n = i + u
                    act.wait_ge(bd_ready, 11)
                    act.wait_ge(xc_ready, done(n))
                    act.wait_ge(var_ready, free(n))
                    a.activation(grid(two[:, u, 0:CH], W), xe3[:, bass.ds(n * RPC, RPC), 0:W], ACT.Square).then_inc(sq_ready, 1)
                    act.wait_ge(var_ready, done(n))
                    act.wait_ge(xn_ready, free(n))
                    a.activation(two[:, u, CH:], PS[:, 2 + u, :], ACT.Sqrt, bias=c_("eps_ln")).then_inc(std_ready, 1)
            with act.Fori(0, NCH // 2) as step:
                i = step * 2
                for u in range(2):
                    n = i + u
                    act.wait_ge(qkv_ready, done(n))
                    for dst, bank, s in ((qw, u, q_out), (vw, 4 + u, v_out)):
                        a.activation(dst[:, bass.ds(n * CH, CH)].rearrange("p (j r c) -> p r j c", j=NWR, r=WS),
                                     PS[:, bank, :].rearrange("p (r j c) -> p r j c", j=NWR, r=WS), ACT.Copy).then_inc(s, 1)

            def values(n, u):
                act.wait_ge(vt_ready, done(n))
                act.wait_ge(o_ready, free(n))
                for h in range(2):
                    a.activation(v0[64 * h:64 * (h + 1), u, :, :, h, :],
                                 PS[64 * h:64 * (h + 1), 4, 0:256].rearrange("p (w a b c) -> p w a b c", w=2, a=4, b=2)[:, :, :, h, :],
                                 ACT.Copy).then_inc(vt_out, 1)
                a.activation(v1[:, u].rearrange("p w k -> p (w k)"), PS[:, 4, 256:512], ACT.Copy).then_inc(vt_out, 1)

            def exps(n, u):
                act.wait_ge(sub_ready, done(n, 2))
                a.activation(ee[:, u, :], ee[:, u, :], ACT.Exp, scale=SCALE).then_inc(exp_ready, 1)

            def probs(n, u):
                act.wait_ge(pt_ready, done(n))
                act.wait_ge(o_ready, free(n))
                a.activation(pts[:, u, 0:4, :].rearrange("p t k -> p (t k)"), PS[:, 6, :], ACT.Copy).then_inc(pt_out, 1)
                a.activation(pts[:, u, 4, :], PS[:, 7, 0:P], ACT.Copy).then_inc(pt_out, 1)

            def write(n, row, col):
                act.wait_ge(ot_ready, done(n))
                for_rows = ye3[:, bass.ds(row, WS), col:col + 2 * WS] if not isinstance(row, int) else ye3[:, row:row + WS, col:col + 2 * WS]
                a.activation(for_rows.rearrange("p r (w c) -> p w r c", w=2),
                             PS[:, 5, 0:P].rearrange("p (w r c) -> p w r c", w=2, r=WS), ACT.Copy).then_inc(ye_out, 1)

            act.wait_ge(pads_ready, 2)
            for n in range(4):
                values(n, n % 2)
                exps(n, n % 2)
                if n >= 1:
                    probs(n - 1, (n - 1) % 2)
                if n >= 2:
                    write(n - 2, SHIFT, 16 * (n - 2) + SHIFT)
            with act.Fori(1, NWR) as i:
                for jj in range(4):
                    n = 4 * i + jj
                    values(n, jj % 2)
                    exps(n, jj % 2)
                    probs(n - 1, (jj - 1) % 2)
                    write(n - 2, WS * i + SHIFT - (WS if jj < 2 else 0), 16 * ((jj - 2) % 4) + SHIFT)
            probs(31, 1)
            write(30, WS * (NWR - 1) + SHIFT, 32 + SHIFT)
            write(31, WS * (NWR - 1) + SHIFT, 48 + SHIFT)
            act.wait_ge(eca_pre, 1)
            a.activation(ecab[:, 108:108 + C], ecab[:, 92:92 + C], ACT.Sigmoid).then_inc(eca_gate, 1)
            with act.Fori(0, NCH // 2) as step:
                i = step * 2
                for u in range(2):
                    n = i + u
                    act.wait_ge(gate_ready, done(n))
                    act.wait_ge(tt_ready, free(n))
                    a.activation(two[:, u, CH:], PS[:, u, :], ACT.Sigmoid, bias=r_("sa_b")).then_inc(sg_ready, 1)
            with act.Fori(0, NCH // 2) as step:
                i = step * 2
                for u in range(2):
                    n = i + u
                    act.wait_ge(om_out, done(n, 2))
                    act.wait_ge(px_done, free(n))
                    a.activation(spl[0:PAIRS * OC, u, 0, :], two[0:PAIRS * OC, u, :], ACT.Copy).then_inc(hi_ready, 1)
                    act.wait_ge(tr_ready, done(n))
                    for q in range(2):
                        a.activation(py4[:, bass.ds(n * RPC + 4 * q, 4)],
                                     PS[:, 4 + 2 * u + q, 0:4 * PAIRS * OC].rearrange("p (r g k) -> p r g k", r=4, k=OC)[:, :, :, 0:KK],
                                     ACT.Copy).then_inc(py_out, 1)
                        a.activation(mk4[:, bass.ds(n * RPC + 4 * q, 4)],
                                     PS[:, 4 + 2 * u + q, 0:4 * PAIRS * OC].rearrange("p (r g k) -> p r g k", r=4, k=OC)[:, :, :, 2 * KK:3 * KK],
                                     ACT.Sigmoid).then_inc(mk_out, 1)

            def row(n, u, slot=None):
                act.wait_ge(bc_ready, done(n))
                a.activation(ab[:, u, 0:320], PS[:, 6, 0:320], ACT.Abs, bias=c_("negx")).then_inc(ab_ready, 1)
                a.activation(ab[:, u, 320:576], PS[:, 7, 0:256], ACT.Abs, bias=c_("negx")).then_inc(ab_ready, 1)
                act.wait_ge(t_ready, free(n))
                act.wait_ge(ab_ready, done(n, 2))
                for h in range(2):
                    a.activation(wt[W * h:W * (h + 1), u, :, W * h:W * (h + 1)],
                                 ab[W * h:W * (h + 1), u, :].rearrange("p (k c) -> p k c", k=KK), ACT.Relu, bias=1.0, scale=-1.0).then_inc(wt_ready, 1)
                    if slot is None or h == 1:
                        continue
                    a.activation(img4[:, bass.ds(slot, 1)].rearrange("p r k o -> p (r k o)"), PS[:, 7, 256:400], ACT.Copy).then_inc(row_out, 1)

            def image_chunk(n, yc, u):
                act.wait_ge(im_ready, done(n))
                act.sem_inc(act_turn, 1)
                for b, k in enumerate((3, 3, 2)):
                    a.activation(img4[:, bass.ds(RPC * yc + TOP + 3 * b, k)], PS[:, 4 * u + b, 0:144 * k].rearrange("p (r k o) -> p r k o", k=KK, o=C),
                                 ACT.Copy).then_inc(im_out, 1)

            def hat(n, yc, stage):
                rows = aw4[:, bass.ds(RPC * yc, RPC)].rearrange("p r k j -> p (r k j)")
                act.wait_ge((ad_ready, aa_ready)[stage], done(n))
                act.sem_inc(act_turn, 1)
                if stage == 0:
                    a.activation(rows, rows, ACT.Abs).then_inc(aa_ready, 1)
                else:
                    a.activation(rows, rows, ACT.Relu, bias=1.0, scale=-1.0).then_inc(ar_ready, 1)

            def weights_ahead():
                act.wait_ge(zeros_ready, 2)
                with act.Fori(0, (NCH - 2) // 2) as step:
                    for u in range(2):
                        image_chunk(step * 2 + u, step * 2 + u, u)
                image_chunk(NCH - 2, NCH - 2, 0)
                hat(0, 0, 0)
                hat(0, 0, 1)

                def pair(g, last, chunks):
                    def chunk(c, u):
                        s = g * NCH + c
                        first, end = (isinstance(c, int) and c == e for e in (0, NCH - 1))
                        for r in range(RPC):
                            slot = TOP + H - RPC + r if first else None if last else c * RPC + (TOP - RPC + r)
                            row(s * RPC + r, r % 2, slot)
                            if r in (4, 6) and not (last and end):
                                hat(s + 1, 0 if end else c + 1, (r - 4) // 2)
                    chunks(chunk)
                stream(act, pair)

            def weights(p, g, band):
                act.wait_ge(zeros_ready, 2)
                act.wait_ge(t_ready, p * H + LAST)
                for yc in range(NCH):
                    image_chunk(p * NCH + yc, yc, yc % 2)
                for stage in range(2):
                    for yc in range(NCH):
                        hat(p * NCH + yc, yc, stage)
                with act.Fori(0, H // RPC) as step:
                    for r in range(RPC):
                        row(p * H + step * RPC + r, r % 2)

            branches(act, weights_ahead, weights)
            with act.Fori(0, NCH // 2) as step:
                i = step * 2
                for u in range(2):
                    n = i + u
                    act.wait_ge(ot2_ready, done(n))
                    a.activation(z[:, bass.ds(n * CH, CH)], PS[:, u, :], ACT.Identity, bias=w_("b"),
                                 accum_out=small[:, bass.ds(n + 8, 1)]).then_inc(z_ready, 1)
            act.wait_ge(z_ready, done(NCH - 1))
            act.wait_ge(bn_step, 1)
            a.activation(aw[:, 0:HW], z, ACT.Square, bias=small[:, 4:5], accum_out=small[:, 5:6]).then_inc(bn_sq, 1)
            act.wait_ge(bn_var, 1)
            a.activation(small[:, 6:7], PS[:, 2, 1:2], ACT.Sqrt, bias=c_("eps_bn"), scale=1.0 / (B * HW)).then_inc(bn_std, 1)
            act.wait_ge(bn_aff, 1)
            with act.Fori(0, 4) as n:
                zc = z[:, bass.ds(n * 1024, 1024)]
                a.activation(zc, zc, ACT.Relu, bias=small[:, 7:8], scale=small[:, 6:7]).then_inc(f_ready, 1)

        @block.tensor
        def _(pe):
            def mm(o, l, r, start=True, stop=True):
                return nc.tensor.matmul(o, l, r, start=start, stop=stop)

            for s, n in ((mu_ready, 2), (var_ready, 2), (qkv_ready, 2), (s_ready, 2), (vt_ready, 2), (pt_ready, 2), (o_ready, 2),
                         (ot_ready, 2), (gate_ready, 2), (po_ready, 2), (om_ready, 4), (tr_ready, 2), (im_ready, 2), (bc_ready, 2),
                         (t_ready, 2), (ot2_ready, 2)):
                pe.sem_inc(s, n)
            pe.wait_ge(x_in, 16)
            pe.wait_ge(bd_ready, 11)
            with pe.Fori(0, NCH // 2) as step:
                i = step * 2
                for u in range(2):
                    n = i + u
                    pe.wait_ge(xc_ready, free(n))
                    mm(PS[:, u, :], bd[:, MEAN, :], x0[:, bass.ds(n * CH, CH)]).then_inc(mu_ready, 1)
                for u in range(2):
                    n = i + u
                    pe.wait_ge(sq_ready, done(n))
                    pe.wait_ge(std_ready, free(n))
                    mm(PS[:, 2 + u, :], bd[:, MEAN, :], two[:, u, 0:CH]).then_inc(var_ready, 1)
            pe.wait_ge(ext_ready, 2)
            with pe.Fori(0, NCH // 2) as step:
                i = step * 2
                for u in range(2):
                    n = i + u
                    pe.wait_ge(q_out, free(n))
                    pe.wait_ge(k_out, free(n))
                    pe.wait_ge(v_out, free(n))
                    src = xe3[:, bass.ds(n * WS + SHIFT, WS), SHIFT:SHIFT + W]
                    mm(PS[:, u, :], bd[:, WQ, :], src)
                    mm(PS[:, 2 + u, :], bd[:, WK, :], src)
                    mm(PS[:, 4 + u, :], bd[:, WV, :], src).then_inc(qkv_ready, 1)
            pe.wait_ge(eca_step, 2)
            mm(PS[0:B, 6, 0:C], c_("bmask"), small[:, 16:32]).then_inc(eca_sum, 1)

            def scores(n, u):
                pe.wait_ge(staged, done(n, 4))
                pe.wait_ge(sub_ready, 2 * n + 4)
                for w in range(2):
                    mm(PS[64 * w:64 * (w + 1), u, :], qs[:, u, w, :], kb[:, u, w, :])
                    ins = mm(PS[64 * w:64 * (w + 1), 2, 0:P], qs[:, u, w, :], kvb[:, u, w, 0, :])
                ins.then_inc(s_ready, 1)
                pe.wait_ge(vt_out, 3 * n + 6)
                for w in range(2):
                    nc.tensor.transpose(PS[:, 4, w * P:(w + 1) * P], vs[:, u, w].rearrange("p d k -> p (d k)"), ident)
                    ins = nc.tensor.transpose(PS[:, 4, 256 + w * P:256 + (w + 1) * P], kvb[:, u, w, 1, :], ident)
                ins.then_inc(vt_ready, 1)

            def attend(n, u):
                pe.wait_ge(exp_ready, done(n))
                pe.wait_ge(pt_out, 2 * n + 4)
                for t in range(5):
                    ins = nc.tensor.transpose(PS[:, 6, P * t:P * (t + 1)] if t < 4 else PS[:, 7, 0:P], ee[:, u, P * t:P * (t + 1)], ident)
                ins.then_inc(pt_ready, 1)
                pe.wait_ge(pt_out, done(n, 2))
                pe.wait_ge(vt_out, done(n, 3))
                pe.wait_ge(on_ready, 2 * n + 4)
                for w in range(2):
                    part = slice(64 * w, 64 * (w + 1))
                    for t in range(4):
                        mm(PS[part, 3, 32 * t:32 * (t + 1)], pts[:, u, t, part],
                           v0[:, u, w, t].rearrange("p b c -> p (b c)"))
                    ins = mm(PS[part, 3, P:2 * P], pts[:, u, 4, part], v1[:, u, w, :])
                ins.then_inc(o_ready, 1)

            def back(n, u):
                pe.wait_ge(on_ready, done(n, 2))
                pe.wait_ge(ye_out, n + 2)
                nc.tensor.transpose(PS[:, 5, 0:P], on[:, u, :], ident).then_inc(ot_ready, 1)

            pe.wait_ge(eca_step, 3)
            for n in range(4):
                scores(n, n % 2)
                if n >= 2:
                    back(n - 2, n % 2)
                if n >= 1:
                    attend(n - 1, (n - 1) % 2)
            with pe.Fori(4 // 4, 32 // 4) as step:
                i = step * 4
                for jj in range(4):
                    n = i + jj
                    scores(n, jj % 2)
                    back(n - 2, jj % 2)
                    attend(n - 1, (jj - 1) % 2)
            back(30, 0)
            attend(31, 1)
            back(31, 1)
            pe.wait_ge(eca_gate, 1)
            pe.wait_ge(eca_step, 3)
            pe.wait_ge(pt_out, done(31, 2))
            mm(PS[:, 6, 32:48], cst[0:B, CCOL["bmt"][0]:CCOL["bmt"][1]], ecab[:, 108:108 + C]).then_inc(eca_back, 1)
            with pe.Fori(0, NCH // 2) as step:
                i = step * 2
                for u in range(2):
                    n = i + u
                    pe.wait_ge(yc_ready, done(n))
                    pe.wait_ge(sg_ready, free(n))
                    mm(PS[:, u, :], bd[:, SA, :], two[:, u, 0:CH]).then_inc(gate_ready, 1)
                for u in range(2):
                    n = i + u
                    pe.wait_ge(tt_ready, done(n))
                    pe.wait_ge(xl_ready, free(n))
                    mm(PS[:, 2 + u, :], bd[:, PO, :], two[:, u, 0:CH]).then_inc(po_ready, 1)
            pe.wait_ge(xl_ready, done(NCH - 1))
            pe.wait_ge(pads_ready, 2)
            with pe.Fori(0, NCH // 2) as step:
                i = step * 2
                for u in range(2):
                    n = i + u
                    pe.wait_ge(om_out, free(n, 2))
                    for h in range(2):
                        for t in range(KK):
                            ins = mm(PS[0:PAIRS * OC, 2 * h + u, :], woff[:, h, t, :],
                                     xp3[:, bass.ds(n * RPC + t // 3, RPC), t % 3:t % 3 + W], start=t == 0, stop=t == KK - 1)
                        ins.then_inc(om_ready, 1)
                    pe.wait_ge(om_out, done(n, 2))
                    pe.wait_ge(py_out, free(n, 2))
                    pe.wait_ge(mk_out, free(n, 2))
                    for r in range(RPC):
                        for h in range(2):
                            ins = mm(PS[64 * h:64 * (h + 1), 4 + 2 * u + r // 4, (r % 4) * PAIRS * OC:(r % 4 + 1) * PAIRS * OC],
                                     two[0:PAIRS * OC, u, h * CH + r * W:h * CH + (r + 1) * W], ident[0:PAIRS * OC, 0:PAIRS * OC])
                    ins.then_inc(tr_ready, 1)

            def image_row(bank, at, u, r):
                return mm(PS[:, bank, at:at + KK * C], two[:, u, P * r:P * (r + 1)], w_("w"))

            def image_chunk(n, u):
                pe.wait_ge(is_ready, done(n, 2))
                pe.wait_ge(im_out, free(n, 3))
                for r in range(RPC):
                    ins = image_row(4 * u + r // 3, 144 * (r % 3), u, r)
                ins.then_inc(im_ready, 1)

            def px(n, y, image=None, before=False):
                pe.wait_ge(ab_ready, 2 * n + 4)
                if before:
                    pe.wait_ge(row_out, n + 2)
                if image is not None:
                    image_row(7, 256, *image)
                for k in range(KK):
                    o = PS[:, 6, W * k:W * (k + 1)] if k < 5 else PS[:, 7, W * (k - 5):W * (k - 4)]
                    ins = mm(o, selb[:, k, :], sx[:, bass.ds(y * W, W)])
                ins.then_inc(bc_ready, 1)

            def taps(n, y, u, band):
                pe.wait_ge(wt_ready, done(n, 2))
                pe.wait_ge(u_ready, free(n))
                for k in range(KK):
                    ins = mm(PS[:, 3 * u + k // 3, 144 * (k % 3):144 * (k % 3 + 1)], wt[:, u, k, :],
                             img4[:, bass.ds(y + k // 3 if band is None else band * NR + TOP, NR), k, :])
                ins.then_inc(t_ready, 1)

            pe.wait_ge(py_out, done(NCH - 1, 2))
            pe.wait_ge(mk_out, done(NCH - 1, 2))
            pe.wait_ge(off_max, 1)
            mm(PS[0:1, 3, 0:P], small[:, 10:11], ident).then_inc(off_row, 1)

            def sample_all():
                with pe.Fori(0, (NCH - 2) // 2) as step:
                    for u in range(2):
                        image_chunk(step * 2 + u, u)
                image_chunk(NCH - 2, 0)
                pe.wait_ge(im_out, done(NCH - 2, 3))
                pe.wait_ge(is_ready, done(NCH - 1, 2))
                pe.wait_ge(px_ready, 1)
                px(0, 0, image=(1, 0))

                def pair(g, last, chunks):
                    def chunk(c, u):
                        s = g * NCH + c
                        first, end = (isinstance(c, int) and c == e for e in (0, NCH - 1))
                        here = first or not last
                        for r in range(RPC):
                            n = s * RPC + r
                            if r < RPC - 1:
                                px(n + 1, c * RPC + r + 1, (1 - u, r + 1) if here else None, here)
                            elif not (last and end):
                                pe.wait_ge(px_ready, s + 2)
                                if not last:
                                    pe.wait_ge(is_ready, done(s + AHEAD, 2))
                                px(n + 1, 0 if end else (c + 1) * RPC, (u, 0) if not last else None, here)
                            taps(n, c * RPC + r, r % 2, None)
                    chunks(chunk)
                stream(pe, pair)

            def sample(p, g, band):
                pe.wait_ge(u_ready, p * H + LAST)
                pe.wait_ge(ab_ready, 2 * (p * H + LAST))
                for yc in range(NCH):
                    image_chunk(p * NCH + yc, yc % 2)
                pe.wait_ge(im_out, (p * NCH + NCH + LAST) * 3)
                pe.wait_ge(px_ready, p + 1)
                px(p * H, 0)
                with pe.Fori(0, (H - RPC) // RPC) as step:
                    y0 = step * RPC
                    for r in range(RPC):
                        px(p * H + y0 + r + 1, y0 + r + 1)
                        taps(p * H + y0 + r, y0 + r, r % 2, band)
                for r in range(RPC):
                    y = H - RPC + r
                    if r < RPC - 1:
                        px(p * H + y + 1, y + 1)
                    taps(p * H + y, y, r % 2, band)

            branches(pe, sample_all, sample)
            with pe.Fori(0, NCH // 2) as step:
                i = step * 2
                for u in range(2):
                    n = i + u
                    pe.wait_ge(ob_ready, done(n))
                    pe.wait_ge(z_ready, free(n))
                    for r in range(RPC):
                        for h in range(2):
                            ins = mm(PS[64 * h:64 * (h + 1), u, W * r:W * (r + 1)], two[:, u, 64 * r:64 * (r + 1)], ident[:, 64 * h:64 * (h + 1)])
                    ins.then_inc(ot2_ready, 1)
            pe.wait_ge(bn_sum, 1)
            mm(PS[:, 2, 0:1], c_("osum"), small[:, 2:3]).then_inc(bn_mean, 1)
            pe.wait_ge(bn_sq, 1)
            mm(PS[:, 2, 1:2], c_("osum"), small[:, 5:6]).then_inc(bn_var, 1)


def kernel(**inputs):
    import concourse.bacc as bacc
    from concourse.bass_utils import run_bass_kernel_spmd as run

    a = {k: np.ascontiguousarray(np.asarray(v)) for k, v in inputs.items()}
    L0, L1 = "L0_conv_", "L1_conv_"

    def head1(m):
        return np.concatenate([np.zeros((CS, m.shape[1]), np.float32), m])

    parts = {
        "wq": a[L0 + "wq"].T, "wk": a[L0 + "wk"].T, "wv": a[L0 + "wv"].T, "po": a[L0 + "po_w"].T, "sa": a[L0 + "sa_w"].T,
        "woff": a[L1 + "w_off"].transpose(1, 2, 3, 0).reshape(C, -1), "w": a[L1 + "w"].transpose(1, 2, 3, 0).reshape(C, -1),
        "ln_w": a[L0 + "ln_w"][:, None], "ln_b": a[L0 + "ln_b"][:, None], "dw_b": a[L0 + "dw_b"][:, None],
        "po_b": a[L0 + "po_b"][:, None], "dw": a[L0 + "dw_w"].reshape(C, KK),
        "down": head1(a[L0 + "down_w"].reshape(CS, 4)), "down_b": head1(a[L0 + "down_b"][:, None]),
        "b": a[L1 + "b"][:, None], "gamma": a[L1 + "gamma"][:, None], "beta": a[L1 + "beta"][:, None],
    }
    rows = {"w1": a[L0 + "eca_w1"], "w2": a[L0 + "eca_w2"], "w3": a[L0 + "eca_w3"], "wc": a[L0 + "eca_wc"], "sa_b": a[L0 + "sa_b"]}
    consts, sel = constants()
    arrays = {
        "x": a["x"],
        "wpack": np.ascontiguousarray(np.concatenate([parts[n] for n, _ in _WCOLS], axis=1)),
        "rpack": np.concatenate([rows[n].reshape(1, -1) for n, _ in _RCOLS], axis=1),
        "boff": a[L1 + "b_off"][:, None],
        "consts": consts, "sel": sel,
    }
    nc = bacc.Bacc("TRN2", target_bir_lowering=False, num_devices=1)
    aps = [nc.dram_tensor("in_" + n, v.shape, F32, kind="ExternalInput").ap() for n, v in arrays.items()]
    o = nc.dram_tensor("out_0", (B, C, H, W), F32, kind="ExternalOutput").ap()
    build(nc, *aps, o)
    r = run(nc, [{"in_" + n: v for n, v in arrays.items()}], core_ids=[0])
    return r.results[0]["out_0"]
```

```python
from contextlib import ExitStack

import numpy as np

import concourse.bass as bass
from concourse import mybir

F32 = mybir.dt.float32
BF16 = mybir.dt.bfloat16
ALU = mybir.AluOpType
ACT = mybir.ActivationFunctionType
AX = mybir.AxisListType

B, C, H, W = 8, 16, 64, 64
HW = H * W
P = B * C
WS = 8
NWR = H // WS
CS = C // 2
SCALE = CS ** -0.5
SHIFT = WS // 2
HE = H + SHIFT
K1 = WS * WS
K2 = (WS // 2) ** 2
CH = 512
NCH = HW // CH
RPC = CH // W
KK = 9
OC = 3 * KK
PAIRS = B // 2
BR = 4
NR = 2 * BR + 1
TOP = BR + 1
NBLK = -(-H // NR)
IR = TOP + NBLK * NR
LN_EPS, BN_EPS = 1e-6, 1e-5
FOLD = 27

_WCOLS = [("wq", C), ("wk", C), ("wv", C), ("po", C), ("sa", 1), ("woff", KK * OC), ("w", KK * C),
          ("ln_w", 1), ("ln_b", 1), ("dw_b", 1), ("po_b", 1), ("dw", KK), ("down", 4), ("down_b", 1),
          ("b", 1), ("gamma", 1), ("beta", 1)]
_RCOLS = [("w1", 3), ("w2", 3), ("w3", 3), ("wc", 9), ("sa_b", 1)]
_CCOLS = [("ident", P), ("eps_ln", 1), ("eps_bn", 1), ("bmask", B), ("bmod", PAIRS), ("h0", B), ("h1", B), ("ec", C), ("wide", 2 * P - B), ("spread", 4 * P), ("bmt", P), ("osum", P),
          ("negx", 1), ("kxadd", 1), ("xg", CH), ("jrel", NR),
          ("jabs", NBLK * NR), ("yabs", H * KK)]


def _columns(spec):
    at, out = 0, {}
    for name, n in spec:
        out[name] = (at, at + n)
        at += n
    return out, at


WCOL, NWC = _columns(_WCOLS)
RCOL, NRC = _columns(_RCOLS)
CCOL, NCC = _columns(_CCOLS)


def constants():
    c = np.zeros((P, NCC), np.float32)

    def put(name, a):
        c[:a.shape[0], CCOL[name][0]:CCOL[name][1]] = a.reshape(a.shape[0], -1)

    p = np.arange(P)
    bm = (p[:, None] // C == np.arange(B)).astype(np.float32)
    put("ident", np.eye(P, dtype=np.float32))
    put("bmask", bm)
    put("bmod", bm[:, :PAIRS] + bm[:, PAIRS:])
    put("h0", bm * (p[:, None] % C < CS))
    put("h1", bm * (p[:, None] % C >= CS))
    put("ec", (p[:, None] % C == np.arange(C)).astype(np.float32))
    put("bmt", bm.T)
    put("osum", (p[:, None] % C == p[None] % C).astype(np.float32))
    put("wide", np.concatenate([np.zeros((P, P - B)), bm / C, np.zeros((P, P - B))], axis=1))
    put("spread", (p[:, None, None] // B % 4 == np.arange(4)[None, :, None]) * (p[:, None, None] % B == p[None, None] // C))
    put("negx", -(p[:, None] % W).astype(np.float32))
    ch = np.arange(PAIRS * OC) % OC
    isx = (ch >= KK) & (ch < 2 * KK)
    put("kxadd", (isx * (ch % 3 - 1.0))[:, None].astype(np.float32))
    put("xg", isx[:, None] * (np.arange(CH) % W)[None].astype(np.float32))
    put("jrel", np.tile(np.arange(NR) - float(BR), (P, 1)))
    put("jabs", np.tile(np.arange(NBLK * NR) * 1.0, (P, 1)))
    y, k = np.meshgrid(np.arange(H), np.arange(KK), indexing="ij")
    put("yabs", np.tile((y + k // 3 - 1.0).reshape(1, -1), (P, 1)))
    sel = np.zeros((2, 3, KK, KK, 2, W), np.float32)
    for s in range(3):
        for h in range(2):
            for k in range(KK):
                sel[h, s, k, k, h] = 1.0
    put("eps_ln", np.full((P, 1), LN_EPS))
    put("eps_bn", np.full((P, 1), BN_EPS))
    return c, sel.reshape(2 * 3 * KK, -1)


def build(nc, x, wpack, rpack, boff, consts, selc, out):
    ctx = ExitStack()
    with ctx:
        def sb(name, shape, dt=F32):
            return ctx.enter_context(nc.sbuf_tensor(name, shape, dt))

        def sem(name):
            return ctx.enter_context(nc.semaphore(name))

        xr_dram = nc.dram_tensor("xr_scratch", (P, 3, HW), BF16, kind="Internal").ap()
        px_dram = nc.dram_tensor("px_scratch", (B, 3, KK, HW), BF16, kind="Internal").ap()

        x0t = sb("x0", [P, HW])
        wr = sb("wr", [P, NWC])
        rp = sb("rp", [P, NRC])
        cst = sb("cst", [P, NCC])
        bcol = sb("bcol", [PAIRS * OC, 1])
        xp = sb("xp", [P, (H + 2) * (W + 2)])
        bd = sb("bd", [P, 6, P])
        MEAN, WQ, WK, WV, PO, SA = range(6)
        woff = sb("woff", [P, 6, PAIRS * OC])
        selb = sb("selb", [2 * 3 * KK, KK, P], BF16)
        two = sb("two", [P, 2, 2 * CH])
        rs = two[:, 0, CH:CH + HW // C]
        small = sb("small", [P, 64])
        wsp = sb("wsp", [P, 2, KK * C], BF16)
        ecab = sb("ecab", [B, 128])
        flag = sb("flag", [1, 1], mybir.dt.int32)

        def cutter(name, n):
            region, at = sb(name, [P, n]), [0]

            def cut(k):
                if k is None:
                    at[0] = 0
                    return None
                at[0] += k
                assert at[0] <= n, (name, at[0], n)
                return region[:, at[0] - k:at[0]]
            return cut

        cut = cutter("region", 27680)
        xe = cut(HE * HE)
        qw = cut(HW)
        kw = cut(HW)
        vw = cut(HW)
        kv = cut(NWR * NWR * 2 * K2)
        x1 = cut(HW)
        ye = cut(HE * HE)
        cut(None)
        xs = cut(2 * (H + 2) * (W + 2)).rearrange("p (h r c) -> p h r c", h=2, c=W + 2)
        cut(None)
        img = cut(IR * KK * C)
        osam = cut(H * PAIRS * C)
        z = cut(HW)
        sx = z[:, 0:HW // 2].bitcast(BF16)[0:2 * 3 * KK, :]
        aw = cut(H * KK * NR)
        bns = aw[:, 0:6 * NCH]
        mk = cut(H * PAIRS * KK)
        cut2 = cutter("region2", 7776)
        kb = cut2(2 * 2 * B * K1).rearrange("p (u w k) -> p u w k", u=2, w=2)
        kvb = cut2(2 * 2 * 2 * B * K2).rearrange("p (u w t k) -> p u w t k", u=2, w=2, t=2)
        ee = cut2(2 * B * (K1 + K2)).rearrange("p (u k) -> p u k", u=2)
        pts = cut2(2 * 5 * P).rearrange("p (u t k) -> p u t k", u=2, t=5)
        v0 = cut2(2 * 2 * P).rearrange("p (u w a b c) -> p u w a b c", u=2, w=2, a=4, b=2)
        v1 = cut2(2 * 2 * P).rearrange("p (u w k) -> p u w k", u=2, w=2)
        qs = cut2(2 * 2 * K1).rearrange("p (u w k) -> p u w k", u=2, w=2)
        vs = cut2(2 * 2 * 2 * K1).rearrange("p (u w d k) -> p u w d k", u=2, w=2, d=2)
        on = cut2(2 * P).rearrange("p (u k) -> p u k", u=2)
        sm = cut2(2 * 3 * 2 * B).rearrange("p (u t k) -> p u t k", u=2, t=3)
        cut2(None)
        wt = cut2(2 * KK * P).rearrange("p (u k s) -> p u k s", u=2, k=KK)
        uu = cut2(4 * KK * NR * C).rearrange("p (u a o) -> p u a o", u=4, o=C)
        spl = osam[:, 0:3 * 2 * CH].bitcast(BF16).rearrange("p (u s k) -> p u s k", u=2, s=3)
        rest = osam[0:PAIRS * OC, 3 * 2 * CH:4 * 2 * CH]
        flat2 = uu.rearrange("p u a o -> p (u a o)")
        xsp = flat2[:, 0:3 * CH].bitcast(BF16).rearrange("p (u s k) -> p u s k", u=2, s=3)
        xrest = flat2[:, 3 * CH:4 * CH]
        wtmp = flat2[:, 4 * CH:4 * CH + KK * C]
        wparts = flat2[:, 5 * CH:5 * CH + 3 * KK * C // 2].bitcast(BF16).rearrange("p (s k) -> p s k", s=3)
        xrow = two[:, 0, :].bitcast(BF16).rearrange("p (u r h c) -> p u r h c", u=2, r=RPC, h=2)
        py = x0t[:, 0:H * PAIRS * KK]
        ab = x0t[:, H * PAIRS * KK:H * PAIRS * KK + 2 * KK * W].rearrange("p (u k) -> p u k", u=2)
        x0 = x0t[:, :]

        PS = ctx.enter_context(nc.psum_tensor("PS", [P, 8, 512], F32))

        def w_(name):
            return wr[:, WCOL[name][0]:WCOL[name][1]]

        def r_(name):
            return rp[:, RCOL[name][0]:RCOL[name][1]]

        def c_(name, parts=P):
            return cst[0:parts, CCOL[name][0]:CCOL[name][1]]

        def grid(flat, c):
            return flat.rearrange("p (r c) -> p r c", c=c)

        ident = c_("ident")
        xe3, ye3, x13, xp3 = grid(xe, HE), grid(ye, HE), grid(x1, W), grid(xp[:, :], W + 2)
        x03 = grid(x0, W)
        img4 = img.rearrange("p (r k o) -> p r k o", k=KK, o=C)
        os4 = osam.rearrange("p (r g o) -> p r g o", g=PAIRS, o=C)
        aw4 = aw.rearrange("p (r k j) -> p r k j", k=KK, j=NR)
        mk4 = mk.rearrange("p (r g k) -> p r g k", g=PAIRS, k=KK)
        py4 = py.rearrange("p (r g k) -> p r g k", g=PAIRS, k=KK)
        tap1 = two[:, 0, 0:WS * (W - 1)].rearrange("p (r c) -> p r c", c=W - 1)
        kv4 = kv.rearrange("p (w t k) -> p w t k", t=2, k=K2)

        def mid(ap, n):
            return ap.unsqueeze(1).to_broadcast([ap.shape[0], n, ap.shape[1]])

        def end(ap, n):
            return ap.unsqueeze(len(ap.shape)).to_broadcast(list(ap.shape) + [n])

        def done(n, per=1):
            return (n + 3) * per

        def free(n, per=1):
            return (n + 1) * per

        x_in, w_in = sem("x_in"), sem("w_in")
        bd_ready, pads_ready = sem("bd_ready"), sem("pads_ready")
        mu_ready, xc_ready, sq_ready, var_ready = sem("mu_ready"), sem("xc_ready"), sem("sq_ready"), sem("var_ready")
        std_ready, rstd_ready, xn_ready, ln_ready = sem("std_ready"), sem("rstd_ready"), sem("xn_ready"), sem("ln_ready")
        ext_ready = sem("ext_ready")
        rest_in, rb_ready = sem("rest_in"), sem("rb_ready")
        qkv_ready, q_out, k_out, v_out = sem("qkv_ready"), sem("q_out"), sem("k_out"), sem("v_out")
        lead_step, lead_ready = sem("lead_step"), sem("lead_ready")
        down_step, conv_step, eca_step = sem("down_step"), sem("conv_step"), sem("eca_step")
        x1_sum = sem("x1_sum")
        eca_sum, eca_pre, eca_gate, eca_back = sem("eca_sum"), sem("eca_pre"), sem("eca_gate"), sem("eca_back")
        staged, q_staged, s_ready, vt_ready, max_ready = sem("staged"), sem("q_staged"), sem("s_ready"), sem("vt_ready"), sem("max_ready")
        sub_ready, exp_ready, rcp_ready = sem("sub_ready"), sem("exp_ready"), sem("rcp_ready")
        vt_out, pt_ready, pt_out, o_ready = sem("vt_out"), sem("pt_ready"), sem("pt_out"), sem("o_ready")
        on_ready, ot_ready, ye_out, yext_ready = sem("on_ready"), sem("ot_ready"), sem("ye_out"), sem("yext_ready")
        yc_ready, gate_ready, sg_ready, gx_ready = sem("yc_ready"), sem("gate_ready"), sem("sg_ready"), sem("gx_ready")
        y_used, po_ready, xl_ready = sem("y_used"), sem("po_ready"), sem("xl_ready")
        om_ready, om_out, tr_ready, py_out, mk_out = sem("om_ready"), sem("om_out"), sem("tr_ready"), sem("py_out"), sem("mk_out")
        hi_ready, rest_ready, mid_ready, lo_ready = sem("hi_ready"), sem("rest_ready"), sem("mid_ready"), sem("lo_ready")
        px_done, xs_in, xs_ready = sem("px_done"), sem("xs_in"), sem("xs_ready")
        px_stored = [sem("px_stored0"), sem("px_stored1")]
        zeros_ready = sem("zeros_ready")
        pool_turn = sem("pool_turn")
        act_turn = sem("act_turn")
        px_in, px_ready, row_out, fold_ready = sem("px_in"), sem("px_ready"), sem("row_out"), sem("fold_ready")
        is_ready, im_ready, im_out = sem("is_ready"), sem("im_ready"), sem("im_out")
        ad_ready, aa_ready, ar_ready, aw_ready = sem("ad_ready"), sem("aa_ready"), sem("ar_ready"), sem("aw_ready")
        bc_ready, ab_ready, wt_ready, t_ready = sem("bc_ready"), sem("ab_ready"), sem("wt_ready"), sem("t_ready")
        u_ready, os_ready = sem("u_ready"), sem("os_ready")
        xhi_ready, xrest_ready, xmid_ready, xlo_ready = sem("xhi_ready"), sem("xrest_ready"), sem("xmid_ready"), sem("xlo_ready")
        wsp_step, clear_ready, xr_in, xr_ready = sem("wsp_step"), sem("clear_ready"), sem("xr_in"), sem("xr_ready")
        off_max, off_row, off_step, flag_ready = sem("off_max"), sem("off_row"), sem("off_step"), sem("flag_ready")
        abs_ready, part_ready = sem("abs_ready"), sem("part_ready")
        ob_ready, ot2_ready, z_ready, stats_ready, bn_step = sem("ob_ready"), sem("ot2_ready"), sem("z_ready"), sem("stats_ready"), sem("bn_step")
        bn_sum, bn_mean, bn_sq, bn_var, bn_std, bn_aff = [sem("bn_" + n) for n in "sum mean sq var std aff".split()]
        f_ready, r_ready, stored = sem("f_ready"), sem("r_ready"), sem("stored")

        def branches(eng, streams, passes):
            eng.wait_ge(flag_ready, 1)
            large = eng.value_load(flag[0:1, 0:1], min_val=0, max_val=1)
            with eng.If(large == 0):
                streams()
                eng.nop()
            with eng.Else():
                with eng.Fori(0, PAIRS) as g:
                    with eng.Fori(0, NBLK) as band:
                        passes(g * NBLK + band, g, band)
                eng.nop()

        def stream(eng, pair):
            def chunks(f):
                f(0, 0)
                with eng.Fori(0, (NCH - 2) // 2) as i:
                    f(2 * i + 1, 1)
                    f(2 * i + 2, 0)
                f(NCH - 1, 1)
            with eng.Fori(0, PAIRS - 1) as g:
                pair(g, False, chunks)
            pair(PAIRS - 1, True, chunks)

        block = ctx.enter_context(nc.Block())
        LAST = 2

        @block.sync
        def _(sp):
            flat_x = x.rearrange("b c h w -> (b c) (h w)")
            sp.dma_start(x0[:, 0:2 * CH], flat_x[:, 0:2 * CH]).then_inc(x_in, 16)
            sp.dma_start(cst[:, :], consts).then_inc(w_in, 16)
            sp.dma_start(two[0:2 * 3 * KK, :, :].rearrange("p a b -> p (a b)")[:, 0:KK * P], selc).then_inc(w_in, 16)
            sp.dma_start(x0[:, 2 * CH:], flat_x[:, 2 * CH:]).then_inc(rest_in, 16)

            edges = [0] + [16 * j + 1 for j in range(1, 4)] + [H + 2]
            for j in range(4):
                sp.wait_ge(xl_ready, done(2 * j + 1))
                for h in range(2):
                    for up in range(2):
                        a, b = max(edges[j], up), edges[j + 1]
                        sp.dma_start(xs[64 * up:64 * (up + 1), h, a - up:b - up, :],
                                     xp3[64 * h:64 * (h + 1), a:b, :]).then_inc(xs_in, 16)
                sp.wait_ge(xs_in, 64 * (j + 1))
                sp.sem_inc(xs_ready, 1)
            sp.sem_inc(px_done, 2)
            with sp.Fori(0, NCH // 2) as step:
                i = step * 2
                for u in range(2):
                    n = i + u
                    sp.wait_ge(lo_ready, done(n))
                    for b in range(B):
                        row, h = OC * (b % PAIRS) + KK, b // PAIRS
                        sp.dma_start(px_dram[b, :, :, bass.ds(n * CH, CH)].rearrange("s k c -> k s c"),
                                     spl[row:row + KK, u, :, h * CH:(h + 1) * CH]).then_inc(px_stored[u], 16)
                    sp.wait_ge(xlo_ready, done(n))
                    sp.dma_start(xr_dram[:, :, bass.ds(n * CH, CH)], xsp[:, u]).then_inc(px_stored[u], 16)
                    sp.wait_ge(px_stored[u], 16 * (B + 1) * (step + 1))
                    sp.sem_inc(px_done, 1)

            def load_px(count, g, first, n, chunks=1):
                for h in range(2):
                    sp.dma_start(sx[3 * KK * h:3 * KK * (h + 1), bass.ds(first, n)],
                                 px_dram[bass.ds(g + h * PAIRS, 1), :, :, bass.ds(first, n)].rearrange("b s k c -> (b s k) c")).then_inc(px_in, 16)
                sp.wait_ge(px_in, 32 * count + 32)
                sp.sem_inc(px_ready, chunks)

            def load_rows(count, g, c, u):
                for slot, part in enumerate((0, 1, 2, 0)):
                    for h in range(2):
                        at = 2 * C * slot + C * h
                        sp.dma_start(xrow[at:at + C, u, :, h, :],
                                     xr_dram[bass.ds(C * g + C * PAIRS * h, C), part, bass.ds(c * CH, CH)].rearrange("p (r c) -> p r c", c=W)).then_inc(xr_in, 16)
                sp.wait_ge(xr_in, 128 * count + 128)
                sp.sem_inc(xr_ready, 1)

            def load_ahead():
                load_px(0, 0, 0, CH)
                sp.wait_ge(clear_ready, 1)
                load_rows(0, 0, NCH - 1, 1)
                load_px(1, 0, CH, HW - CH, NCH - 1)
                with sp.Fori(0, PAIRS - 1) as g:
                    with sp.Fori(0, NCH // 2) as step:
                        for u in range(2):
                            c = 2 * step + u
                            s = g * NCH + c
                            sp.wait_ge(bc_ready, done(s * RPC))
                            load_rows(s + 1, g + 1, c, u)
                            sp.wait_ge(bc_ready, done(s * RPC + RPC - 1))
                            load_px(s + 2, g + 1, c * CH, CH)

            def pass_px(p, g, band):
                sp.wait_ge(bc_ready, p * H + LAST)
                load_px(p, g, 0, HW)

            branches(sp, load_ahead, pass_px)
            with sp.Fori(0, 4) as n:
                sp.wait_ge(r_ready, n + 1)
                sp.dma_start(out.rearrange("b c h w -> (b c) (h w)")[:, bass.ds(n * 1024, 1024)],
                             z[:, bass.ds(n * 1024, 1024)]).then_inc(stored, 16)
            sp.wait_ge(stored, 64)

        @block.gpsimd
        def _(pool):
            pool.memset(v0, 0.0).then_inc(pads_ready, 1)
            pool.memset(v1, 0.0).then_inc(pads_ready, 1)
            pool.wait_ge(pads_ready, 2)
            for h in range(2):
                pool.memset(v0[64 * h:64 * (h + 1), :, :, :, h, CS:CS + 1].rearrange("p u w a c -> p (u w a) c"), 1.0).then_inc(pads_ready, 1)
            pool.wait_ge(pads_ready, 4)
            pool.wait_ge(w_in, 80)
            pool.tensor_copy(v1.rearrange("p u w (b c) -> p (u w) b c", b=B)[:, :, :, 0:1],
                             c_("bmask").unsqueeze(1).unsqueeze(3).to_broadcast([P, 4, B, 1])).then_inc(pads_ready, 1)
            pool.memset(xp[:, :], 0.0).then_inc(pads_ready, 1)
            pool.wait_ge(ln_ready, done(NCH - 1))
            pool.tensor_copy(xe3[:, H:HE, 0:W], xe3[:, 0:SHIFT, 0:W]).then_inc(ext_ready, 1)
            pool.wait_ge(ext_ready, 1)
            pool.tensor_copy(xe3[:, :, W:HE], xe3[:, :, 0:SHIFT]).then_inc(ext_ready, 1)
            pool.sem_inc(staged, 4)
            pool.wait_ge(k_out, done(NCH - 1))
            pool.wait_ge(q_out, done(NCH - 1))
            pool.wait_ge(v_out, done(NCH - 1))
            def four(i):
                for jj in range(4):
                    n, u = 4 * i + jj, jj % 2
                    pool.wait_ge(vt_ready, free(n))
                    pool.sem_inc(pool_turn, 1)
                    pool.tensor_tensor(
                        kb[:, u].rearrange("p w (b k) -> p w b k", b=B),
                        kw[:, bass.ds(n * 2 * K1, 2 * K1)].rearrange("p (w k) -> p w k", w=2).unsqueeze(2).to_broadcast([P, 2, B, K1]),
                        mid(c_("h0"), 2).unsqueeze(3).to_broadcast([P, 2, B, K1]), ALU.mult).then_inc(staged, 1)
                    pool.wait_ge(down_step, 8 * NCH)
                    pool.tensor_tensor(
                        kvb[:, u].rearrange("p w t (b k) -> p (w t) b k", b=B),
                        kv[:, bass.ds(n * 4 * K2, 4 * K2)].rearrange("p (w k) -> p w k", w=4).unsqueeze(2).to_broadcast([P, 4, B, K2]),
                        mid(c_("h1"), 4).unsqueeze(3).to_broadcast([P, 4, B, K2]), ALU.mult).then_inc(staged, 1)
            with pool.Fori(0, NWR - 1) as i:
                four(i)
                pool.wait_ge(lead_step, 2 * i + 2)
                pool.sem_inc(pool_turn, 1)
                rows = x13[:, bass.ds(WS * i + WS, WS), 1:W]
                pool.tensor_tensor(rows, rows, tap1, ALU.add).then_inc(lead_ready, 1)
            four(NWR - 1)
            pool.wait_ge(ye_out, done(31))
            pool.tensor_copy(ye3[:, 0:SHIFT, SHIFT:HE], ye3[:, H:HE, SHIFT:HE]).then_inc(yext_ready, 1)
            pool.wait_ge(yext_ready, 1)
            pool.tensor_copy(ye3[:, 0:H, 0:SHIFT], ye3[:, 0:H, W:HE]).then_inc(yext_ready, 1)
            pool.sem_inc(gx_ready, 2)
            with pool.Fori(0, NCH // 2) as step:
                for u in range(2):
                    n = 2 * step + u
                    pool.wait_ge(sg_ready, done(n))
                    pool.sem_inc(pool_turn, 1)
                    pool.tensor_tensor(two[:, u, CH:], two[:, u, CH:], x1[:, bass.ds(n * CH, CH)], ALU.mult).then_inc(gx_ready, 1)
            pool.sem_inc(rest_ready, 2)
            pool.sem_inc(xrest_ready, 2)
            pool.memset(wt, 0.0).then_inc(zeros_ready, 1)
            with pool.Fori(0, NCH // 2) as step:
                i = step * 2
                for u in range(2):
                    n = i + u
                    pool.wait_ge(hi_ready, done(n))
                    pool.wait_ge(lo_ready, n + 2)
                    pool.sem_inc(pool_turn, 1)
                    pool.tensor_tensor(rest, two[0:PAIRS * OC, u, :], spl[0:PAIRS * OC, u, 0, :], ALU.subtract).then_inc(rest_ready, 1)
                    pool.wait_ge(xhi_ready, done(n))
                    pool.wait_ge(xlo_ready, n + 2)
                    pool.sem_inc(pool_turn, 1)
                    pool.tensor_tensor(grid(xrest, W), xp3[:, bass.ds(n * RPC + 1, RPC), 1:1 + W], grid(xsp[:, u, 0, :], W), ALU.subtract).then_inc(xrest_ready, 1)
            pool.wait_ge(om_ready, done(NCH - 1, 2))
            pool.memset(img4[:, 0:TOP], 0.0).then_inc(zeros_ready, 1)
            pool.memset(img4[:, TOP + H:IR], 0.0).then_inc(zeros_ready, 1)
            pool.sem_inc(ad_ready, 2)
            pool.sem_inc(aw_ready, 2)
            pool.sem_inc(fold_ready, 2)
            pool.wait_ge(tr_ready, done(NCH - 1))
            pool.wait_ge(py_out, done(NCH - 1, 2))
            pool.wait_ge(mk_out, done(NCH - 1, 2))

            def stage(g, yc, u, h):
                pool.tensor_tensor(
                    two[:, u, :].rearrange("p (r h c) -> p r h c", h=2, c=W)[:, :, h, :],
                    xp3[:, bass.ds(RPC * yc + 1, RPC), 1:1 + W],
                    c_("bmask")[:, bass.ds(g + h * PAIRS, 1)].unsqueeze(2).to_broadcast([P, RPC, W]),
                    ALU.mult).then_inc(is_ready, 1)

            def difference(g, yc, rows_of_band):
                rows = bass.ds(RPC * yc, RPC)
                pool.tensor_tensor(
                    aw4[:, rows],
                    py4[:, rows, bass.ds(g, 1), :].rearrange("p r g k -> p (r g) k").unsqueeze(3).to_broadcast([P, RPC, KK, NR]),
                    mid(rows_of_band, RPC).unsqueeze(2).to_broadcast([P, RPC, KK, NR]), ALU.subtract).then_inc(ad_ready, 1)

            def modulate(n, g, yc):
                rows = bass.ds(RPC * yc, RPC)
                pool.wait_ge(ar_ready, done(n))
                pool.sem_inc(pool_turn, 1)
                pool.tensor_tensor(
                    aw4[:, rows], aw4[:, rows],
                    mk4[:, rows, bass.ds(g, 1), :].rearrange("p r g k -> p (r g) k").unsqueeze(3).to_broadcast([P, RPC, KK, NR]),
                    ALU.mult).then_inc(aw_ready, 1)

            def tables_ahead():
                pool.wait_ge(zeros_ready, 3)
                difference(0, 0, c_("jrel"))
                pool.wait_ge(im_ready, done(NCH - 2))
                pool.memset(two[:, 0, :], 0.0).then_inc(clear_ready, 1)
                modulate(0, 0, 0)

                def pair(g, last, chunks):
                    def chunk(c, u, end=False):
                        s = g * NCH + c
                        for r in range(RPC):
                            pool.wait_ge(u_ready, done(s * RPC + r))
                            pool.sem_inc(pool_turn, 1)
                            pool.tensor_tensor(uu[:, r % 4, FOLD:2 * FOLD, :], uu[:, r % 4, FOLD:2 * FOLD, :],
                                               uu[:, r % 4, 0:FOLD, :], ALU.add).then_inc(fold_ready, 1)
                            nxt = (g + 1, 0) if end else (g, c + 1)
                            if r == 0 and not (last and end):
                                difference(*nxt, c_("jrel"))
                            if r == 6 and not (last and end):
                                modulate(s + 1, *nxt)
                    chunks(lambda c, u: chunk(c, u, isinstance(c, int) and c == NCH - 1))
                stream(pool, pair)

            def tables(p, g, band):
                pool.wait_ge(im_ready, done(NCH - 1))
                pool.wait_ge(zeros_ready, 3)
                for yc in range(NCH):
                    pool.wait_ge(im_ready, free(NCH + p * NCH + yc))
                    pool.sem_inc(pool_turn, 1)
                    for h in range(2):
                        stage(g, yc, yc % 2, h)
                pool.wait_ge(abs_ready, 1)
                pool.wait_ge(u_ready, p * H + LAST)
                pool.sem_inc(pool_turn, 1)
                for yc in range(NCH):
                    difference(g, yc, c_("jabs")[:, bass.ds(band * NR, NR)])
                for yc in range(NCH):
                    modulate(p * NCH + yc, g, yc)

            branches(pool, tables_ahead, tables)

        @block.vector
        def _(dve):
            v = nc.vector
            for s, n in ((xc_ready, 2), (xn_ready, 2), 
                         (max_ready, 4), (sub_ready, 4), (rcp_ready, 2), (on_ready, 4),
                         (yc_ready, 2), (xl_ready, 2), (om_out, 4),
                         (is_ready, 4), (mid_ready, 2), (lo_ready, 2), (xmid_ready, 2), (xlo_ready, 2), (u_ready, 2), (os_ready, 2), (ob_ready, 4)):
                dve.sem_inc(s, n)
            dve.wait_ge(w_in, 80)
            bm = c_("bmask")
            v.tensor_scalar(bd[:, MEAN, :].rearrange("p (b c) -> p b c", b=B), end(bm, C), 1.0 / C, None, ALU.mult).then_inc(bd_ready, 1)
            v.tensor_copy(selb[:, :, :].rearrange("p k m -> p (k m)"), two[0:2 * 3 * KK, :, :].rearrange("p a b -> p (a b)")[:, 0:KK * P]).then_inc(bd_ready, 1)
            def deviations(n, u):
                rows = bass.ds(n * RPC, RPC)
                dve.wait_ge(mu_ready, done(n))
                v.tensor_tensor(xe3[:, rows, 0:W], x03[:, rows, :], grid(PS[:, u, :], W), ALU.subtract).then_inc(xc_ready, 1)

            def normalise(n, u):
                rows = bass.ds(n * RPC, RPC)
                dve.wait_ge(rb_ready, done(n))
                v.tensor_tensor(xe3[:, rows, 0:W], xe3[:, rows, 0:W], grid(PS[:, u, :], W), ALU.mult).then_inc(xn_ready, 1)

            with dve.Fori(0, NCH // 2) as step:
                for u in range(2):
                    deviations(2 * step + u, u)
            for slot, name in ((WQ, "wq"), (WK, "wk"), (WV, "wv"), (PO, "po")):
                v.tensor_tensor(bd[:, slot, :].rearrange("p (b c) -> p b c", b=B), mid(w_(name), B), end(bm, C), ALU.mult).then_inc(bd_ready, 1)
            v.tensor_scalar(bd[:, SA, :].rearrange("p (b c) -> p b c", b=B), end(bm, C), w_("sa"), None, ALU.mult).then_inc(bd_ready, 1)
            for h in range(2):
                part = slice(64 * h, 64 * (h + 1))
                v.tensor_tensor(
                    woff[part, 0:3].rearrange("p t (b k) -> p t b k", b=PAIRS),
                    w_("woff")[part, 3 * h * OC:3 * (h + 1) * OC].rearrange("p (t k) -> p t k", k=OC).unsqueeze(2).to_broadcast([64, 3, PAIRS, OC]),
                    mid(c_("bmod")[part], 3).unsqueeze(3).to_broadcast([64, 3, PAIRS, OC]), ALU.mult).then_inc(bd_ready, 1)
            v.tensor_tensor(
                woff[:, 3:6].rearrange("p t (b k) -> p t b k", b=PAIRS),
                w_("woff")[:, 6 * OC:9 * OC].rearrange("p (t k) -> p t k", k=OC).unsqueeze(2).to_broadcast([P, 3, PAIRS, OC]),
                mid(c_("bmod"), 3).unsqueeze(3).to_broadcast([P, 3, PAIRS, OC]), ALU.mult).then_inc(bd_ready, 1)
            v.tensor_scalar(bcol[:, :], bcol[:, :], c_("kxadd", PAIRS * OC), None, ALU.add).then_inc(bd_ready, 1)
            v.memset(ecab[:, :], 0.0).then_inc(bd_ready, 1)
            dve.wait_ge(std_ready, 1)
            v.reciprocal(rs, rs).then_inc(rstd_ready, 1)
            dve.wait_ge(sq_ready, done(NCH - 1))
            with dve.Fori(0, NCH // 2) as step:
                for u in range(2):
                    normalise(2 * step + u, u)
            def halve(n):
                dve.wait_ge(v_out, done(n))
                dve.wait_ge(k_out, done(n))
                for tap in range(4):
                    for t, src in enumerate((kw, vw)):
                        o = kv4[:, bass.ds(NWR * n, NWR), t, :].rearrange("p w (r s) -> p w r s", r=4)
                        s4 = src[:, bass.ds(n * CH, CH)].rearrange("p (w r a s b) -> p a b w r s", r=4, a=2, s=4, b=2)[:, tap // 2, tap % 2]
                        if tap == 0:
                            ins = v.tensor_scalar(o, s4, w_("down")[:, 0:1], w_("down_b") if t == 0 else 0.0, ALU.mult, ALU.add)
                        else:
                            dve.wait_ge(down_step, 8 * n + 2 * tap - 1 + t)
                            ins = v.scalar_tensor_tensor(o, s4, w_("down")[:, tap:tap + 1], o, ALU.mult, ALU.add)
                        ins.then_inc(down_step, 1)

            with dve.Fori(0, NCH) as n:
                halve(n)

            def scores(n, u):
                dve.wait_ge(s_ready, done(n))
                s0 = PS[:, u, :].rearrange("p (b k) -> p b k", b=B)
                s1 = PS[:, 2, 0:P].rearrange("p (b k) -> p b k", b=B)
                v.reduce_max(sm[:, u, 0, 0:B], s0, axis=AX.X).then_inc(max_ready, 1)
                v.reduce_max(sm[:, u, 0, B:2 * B], s1, axis=AX.X).then_inc(max_ready, 1)
                dve.wait_ge(pt_ready, free(n))
                dve.wait_ge(max_ready, done(n, 2))
                v.tensor_tensor(ee[:, u, 0:B * K1].rearrange("p (b k) -> p b k", b=B), s0,
                                end(sm[:, u, 0, 0:B], K1), ALU.subtract).then_inc(sub_ready, 1)
                v.tensor_tensor(ee[:, u, B * K1:].rearrange("p (b k) -> p b k", b=B), s1,
                                end(sm[:, u, 0, B:2 * B], K2), ALU.subtract).then_inc(sub_ready, 1)

            def invert(n, u):
                dve.wait_ge(o_ready, done(n))
                v.reciprocal(sm[:, u, 2, :].rearrange("p (t b) -> p t b", t=2),
                             PS[:, 3, CS:CS + 2 * (P - CS)].rearrange("p (t k) -> p t k", t=2)[:, :, 0:P - CS:C]).then_inc(rcp_ready, 1)

            def normalise_heads(n, u):
                dve.wait_ge(rcp_ready, done(n))
                dve.wait_ge(ot_ready, free(n))
                for hd in range(2):
                    v.tensor_tensor(on[:, u, :].rearrange("p (b c) -> p b c", b=B)[:, :, CS * hd:CS * (hd + 1)],
                                    PS[:, 3, hd * P:(hd + 1) * P].rearrange("p (b c) -> p b c", b=B)[:, :, CS * hd:CS * (hd + 1)],
                                    end(sm[:, u, 2, B * hd:B * (hd + 1)], CS), ALU.mult).then_inc(on_ready, 1)

            taps = [(0, 0)] + [(dy, dx) for dy in (-1, 0, 1) for dx in (-1, 0, 1) if (dy, dx) != (0, 0)]

            def conv_taps(which, i):
                first, last = (isinstance(i, int) and i == e for e in (0, NWR - 1))
                before = 0 if first else (KK - 2) * i
                for t in which:
                    dy, dx = taps[t]
                    wcol = w_("dw")[:, 3 * (dy + 1) + dx + 1:3 * (dy + 1) + dx + 2]
                    above, below = int(first and dy < 0), int(last and dy > 0)
                    ca, cb = max(0, -dx), W - max(0, dx)
                    src = xe3[:, bass.ds(WS * i + above + dy, WS - above - below), ca + dx:cb + dx]
                    dst = x13[:, bass.ds(WS * i + above, WS - above - below), ca:cb]
                    if t == 0:
                        ins = v.tensor_scalar(dst, src, wcol, w_("dw_b"), ALU.mult, ALU.add)
                    else:
                        if t == 2 and not first:
                            dve.wait_ge(lead_ready, i)
                        else:
                            dve.wait_ge(conv_step, before + t)
                        ins = v.scalar_tensor_tensor(dst, src, wcol, dst, ALU.mult, ALU.add)
                    ins.then_inc(conv_step, 1)

            def four_steps(i, parts):
                for jj, which in enumerate(parts):
                    n = 4 * i + jj
                    started = not (isinstance(n, int) and n == 0)
                    scores(n, jj % 2)
                    conv_taps(which[:-1], i)
                    if started:
                        invert(n - 1, (jj - 1) % 2)
                    conv_taps(which[-1:], i)
                    if started:
                        normalise_heads(n - 1, (jj - 1) % 2)

            parts = (range(2, 4), range(4, 6), range(6, 8), range(8, 9))
            four_steps(0, (range(0, 3), range(3, 5), range(5, 7), range(7, 9)))
            with dve.Fori(1, NWR - 1) as i:
                four_steps(i, parts)
            four_steps(NWR - 1, parts)
            invert(31, 1)
            normalise_heads(31, 1)
            dve.wait_ge(conv_step, (KK - 2) * NWR + 2)
            v.reduce_sum(small[:, 48 + NWR:49 + NWR], x1[:, (H - WS) * W:], axis=AX.X).then_inc(eca_step, 1)
            dve.wait_ge(eca_step, 1)
            dve.wait_ge(x1_sum, NWR - 1)
            v.reduce_sum(small[:, 0:1], small[:, 49:49 + NWR], axis=AX.X).then_inc(eca_step, 1)
            dve.wait_ge(eca_step, 2)
            v.tensor_scalar(small[:, 16:32], c_("ec"), small[:, 0:1], None, ALU.mult).then_inc(eca_step, 1)
            dve.wait_ge(eca_sum, 1)
            v.tensor_scalar(ecab[:, 4:20], PS[0:B, 6, 0:C], 1.0 / HW, None, ALU.mult).then_inc(eca_step, 1)
            dve.wait_ge(eca_step, 4)
            steps = 4
            for t in range(3):
                for j, d in enumerate((1, 2, 4)):
                    zz = ecab[:, 33 + 20 * j:33 + 20 * j + C]
                    src = ecab[:, 4 + (t - 1) * d:4 + (t - 1) * d + C]
                    wc = r_("w%d" % (j + 1))[0:B, t:t + 1]
                    if t == 0:
                        ins = v.tensor_scalar(zz, src, wc, None, ALU.mult)
                    else:
                        dve.wait_ge(eca_step, steps - 2)
                        ins = v.scalar_tensor_tensor(zz, src, wc, zz, ALU.mult, ALU.add)
                    ins.then_inc(eca_step, 1)
                    steps += 1
            for j in range(3):
                for t in range(3):
                    src = ecab[:, 32 + 20 * j + t:32 + 20 * j + t + C]
                    wc = r_("wc")[0:B, 3 * j + t:3 * j + t + 1]
                    acc = ecab[:, 92:92 + C]
                    dve.wait_ge(eca_step, steps)
                    if j == t == 0:
                        ins = v.tensor_scalar(acc, src, wc, None, ALU.mult)
                    else:
                        ins = v.scalar_tensor_tensor(acc, src, wc, acc, ALU.mult, ALU.add)
                    ins.then_inc(eca_step, 1)
                    steps += 1
            dve.wait_ge(eca_step, steps)
            v.tensor_copy(ecab[:, 92:92 + C], ecab[:, 92:92 + C]).then_inc(eca_pre, 1)

            dve.wait_ge(eca_back, 1)
            v.tensor_tensor(small[:, 32:48], PS[:, 6, 32:48], c_("ec"), ALU.mult).then_inc(eca_step, 1)
            dve.wait_ge(eca_step, steps + 1)
            v.reduce_sum(small[:, 1:2], small[:, 32:48], axis=AX.X).then_inc(eca_step, 1)
            dve.wait_ge(eca_step, steps + 2)
            dve.wait_ge(yext_ready, 2)

            def attended(n, u):
                dve.wait_ge(y_used, free(n))
                v.tensor_scalar(grid(two[:, u, 0:CH], W), ye3[:, bass.ds(n * RPC, RPC), 0:W],
                                small[:, 1:2], w_("down_b"), ALU.mult, ALU.add).then_inc(yc_ready, 1)

            def residual(n):
                dve.wait_ge(po_ready, done(n))
                v.scalar_tensor_tensor(xp3[:, n * RPC + 1:(n + 1) * RPC + 1, 1:1 + W], grid(PS[:, 2 + n % 4, :], W), w_("po_b"),
                                       x03[:, n * RPC:(n + 1) * RPC, :], ALU.add, ALU.add).then_inc(xl_ready, 1)

            attended(0, 0)
            attended(1, 1)
            for n in range(NCH):
                if n + 2 < NCH:
                    attended(n + 2, n % 2)
                residual(n)
            w3, hi, md, lo = w_("w"), wparts[:, 0, :], wparts[:, 1, :], wparts[:, 2, :]
            v.tensor_copy(hi, w3).then_inc(wsp_step, 1)
            dve.wait_ge(wsp_step, 1)
            v.tensor_tensor(wtmp, w3, hi, ALU.subtract).then_inc(wsp_step, 1)
            dve.wait_ge(wsp_step, 2)
            v.tensor_copy(md, wtmp).then_inc(wsp_step, 1)
            dve.wait_ge(wsp_step, 3)
            v.tensor_tensor(lo, wtmp, md, ALU.subtract).then_inc(wsp_step, 1)
            dve.wait_ge(wsp_step, 4)
            v.memset(wsp[96:128, 1, :], 0.0).then_inc(wsp_step, 1)
            for slot, (one, other) in enumerate(((hi, lo), (hi, md), (hi, md), (md, None))):
                part = slice(32 * slot, 32 * (slot + 1))
                v.tensor_copy(wsp[part, 0, :], one[part, :]).then_inc(wsp_step, 1)
                if other is not None:
                    v.tensor_copy(wsp[part, 1, :], other[part, :]).then_inc(wsp_step, 1)
            with dve.Fori(0, NCH // 2) as step:
                i = step * 2
                for u in range(2):
                    n = i + u
                    dve.wait_ge(om_ready, done(n, 2))
                    dve.wait_ge(tr_ready, free(n))
                    dve.wait_ge(rest_ready, free(n))
                    for h in range(2):
                        v.scalar_tensor_tensor(two[0:PAIRS * OC, u, h * CH:(h + 1) * CH], PS[0:PAIRS * OC, 2 * h + u, :],
                                               bcol[:, :], c_("xg", PAIRS * OC), ALU.add, ALU.add).then_inc(om_out, 1)
                    dve.wait_ge(rest_ready, done(n))
                    v.tensor_copy(spl[0:PAIRS * OC, u, 1, :], rest).then_inc(mid_ready, 1)
                    dve.wait_ge(mid_ready, done(n))
                    v.tensor_tensor(spl[0:PAIRS * OC, u, 2, :], rest, spl[0:PAIRS * OC, u, 1, :], ALU.subtract).then_inc(lo_ready, 1)
                    dve.wait_ge(xrest_ready, done(n))
                    v.tensor_copy(xsp[:, u, 1, :], xrest).then_inc(xmid_ready, 1)
                    dve.wait_ge(xmid_ready, done(n))
                    v.tensor_tensor(xsp[:, u, 2, :], xrest, xsp[:, u, 1, :], ALU.subtract).then_inc(xlo_ready, 1)
            def stage(n, u):
                dve.wait_ge(im_ready, free(n))
                for h in range(2):
                    v.tensor_tensor(
                        two[:, u, :].rearrange("p (r h c) -> p r h c", h=2, c=W)[:, :, h, :],
                        xp3[:, bass.ds(RPC * n + 1, RPC), 1:1 + W],
                        c_("bmask")[:, h * PAIRS:h * PAIRS + 1].unsqueeze(2).to_broadcast([P, RPC, W]),
                        ALU.mult).then_inc(is_ready, 1)

            dve.wait_ge(tr_ready, done(NCH - 1))
            stage(0, 0)
            stage(1, 1)
            dve.wait_ge(py_out, done(NCH - 1, 2))
            v.tensor_reduce(small[:, 10:11], py, AX.X, ALU.max, apply_absolute_value=True).then_inc(off_max, 1)
            stage(2, 0)
            stage(3, 1)
            dve.wait_ge(off_row, 1)
            v.reduce_max(small[0:1, 11:12], PS[0:1, 3, 0:P], axis=AX.X).then_inc(off_step, 1)
            dve.wait_ge(off_step, 1)
            v.tensor_scalar(flag[:, :], small[0:1, 11:12], float(BR), None, ALU.is_gt).then_inc(flag_ready, 1)
            with dve.Fori(2, NCH // 2) as step:
                for u in range(2):
                    stage(2 * step + u, u)

            def products(n, y, u, u4):
                dve.wait_ge(t_ready, done(n))
                v.tensor_tensor(
                    uu[:, u4].rearrange("p (b a) o -> p b a o", b=3), PS[:, 3 * u:3 * u + 3, 0:432].rearrange("p b (a o) -> p b a o", o=C),
                    aw4[:, bass.ds(y, 1), :, :].rearrange("p y (b k) j -> p (y b) (k j)", b=3).unsqueeze(3).to_broadcast([P, 3, 3 * NR, C]),
                    ALU.mult).then_inc(u_ready, 1)

            def total(y, g):
                return os4[:, bass.ds(y, 1), bass.ds(g, 1), :].rearrange("p y g o -> p (y g o)")

            def interpolate_all():
                def pair(g, last, chunks):
                    def add(n, y, u):
                        dve.wait_ge(fold_ready, done(n))
                        v.tensor_reduce(total(y, g), uu[:, u, FOLD:, :].rearrange("p a o -> p o a"), AX.X, ALU.add).then_inc(os_ready, 1)

                    def chunk(c, u):
                        s = g * NCH + c
                        dve.wait_ge(aw_ready, done(s))
                        for r in range(RPC):
                            products(s * RPC + r, c * RPC + r, r % 2, r % 4)
                            if r > 0 or not isinstance(c, int) or c > 0:
                                add(s * RPC + r - 1, c * RPC + r - 1, (r - 1) % 4)
                    chunks(chunk)
                    add(g * H + H - 1, H - 1, 3)
                stream(dve, pair)

            def interpolate(p, g, band):
                with dve.Fori(0, H // RPC) as step:
                    y0 = step * RPC
                    dve.wait_ge(aw_ready, p * NCH + NCH + LAST)
                    for r in range(RPC):
                        u = r % 2
                        y = y0 + r
                        n = p * H + y
                        products(n, y, u, u)
                        dve.wait_ge(u_ready, done(n))
                        dve.wait_ge(os_ready, n + LAST)
                        v.tensor_reduce(small[:, 16:32], uu[:, u].rearrange("p a o -> p o a"), AX.X, ALU.add).then_inc(part_ready, 1)
                        dve.wait_ge(part_ready, n + 1)
                        v.tensor_tensor(total(y, g), total(y, g), small[:, 16:32], ALU.add).then_inc(os_ready, 1)

            dve.wait_ge(flag_ready, 1)
            large = dve.value_load(flag[0:1, 0:1], min_val=0, max_val=1)
            with dve.If(large == 0):
                interpolate_all()
                dve.wait_ge(os_ready, done(PAIRS * H - 1))
            with dve.Else():
                dve.wait_ge(px_done, done(NCH - 1))
                v.memset(osam, 0.0).then_inc(off_step, 1)
                dve.wait_ge(off_step, 2)
                v.tensor_tensor(py4, py4, c_("yabs").rearrange("p (r k) -> p r k", k=KK).unsqueeze(2).to_broadcast([P, H, PAIRS, KK]),
                                ALU.add).then_inc(abs_ready, 1)
                with dve.Fori(0, PAIRS) as g:
                    with dve.Fori(0, NBLK) as band:
                        interpolate(g * NBLK + band, g, band)
                dve.wait_ge(os_ready, done(NBLK * PAIRS * H - 1))
            def twice(n, u):
                dve.wait_ge(ot2_ready, free(n))
                for h in range(2):
                    v.tensor_copy(two[:, u, :].rearrange("p (r h c) -> p r h c", h=2, c=W)[:, :, h, :],
                                  osam[:, bass.ds(n * CH, CH)].rearrange("p (r c) -> p r c", c=W)).then_inc(ob_ready, 1)

            def stats(n):
                dve.wait_ge(z_ready, done(n, 2))
                v.bn_stats(bns[:, bass.ds(6 * n, 6)], z[:, bass.ds(n * CH, CH)]).then_inc(stats_ready, 1)

            twice(0, 0)
            twice(1, 1)
            with dve.Fori(0, (NCH - 2) // 2) as step:
                for u in range(2):
                    twice(2 * step + u + 2, u)
                    stats(2 * step + u)
            stats(NCH - 2)
            stats(NCH - 1)
            dve.wait_ge(stats_ready, NCH)
            v.bn_aggr(small[:, 2:4], bns).then_inc(bn_sum, 1)
            dve.wait_ge(bn_mean, 1)
            v.tensor_scalar(small[:, 4:5], PS[:, 6, 0:1], -1.0 / B, None, ALU.mult).then_inc(bn_step, 1)
            dve.wait_ge(bn_step, 1)
            v.tensor_tensor(small[:, 5:6], small[:, 2:3], small[:, 4:5], ALU.add).then_inc(bn_step, 1)
            dve.wait_ge(bn_step, 2)
            v.scalar_tensor_tensor(small[:, 9:10], small[:, 5:6], small[:, 5:6], small[:, 3:4], ALU.mult, ALU.add).then_inc(bn_sq, 1)
            dve.wait_ge(bn_std, 1)
            v.reciprocal(small[:, 6:7], small[:, 6:7]).then_inc(bn_step, 1)
            dve.wait_ge(bn_step, 3)
            v.tensor_tensor(small[:, 6:7], small[:, 6:7], w_("gamma"), ALU.mult).then_inc(bn_step, 1)
            dve.wait_ge(bn_step, 4)
            v.scalar_tensor_tensor(small[:, 7:8], small[:, 4:5], small[:, 6:7], w_("beta"), ALU.mult, ALU.add).then_inc(bn_aff, 1)
            with dve.Fori(0, 4) as n:
                dve.wait_ge(f_ready, n + 1)
                zc = z[:, bass.ds(n * 1024, 1024)]
                v.tensor_tensor(grid(zc, W), grid(zc, W), xp3[:, bass.ds(n * 16 + 1, 16), 1:1 + W], ALU.add).then_inc(r_ready, 1)

        @block.scalar
        def _(act):
            a = nc.scalar
            act.dma_start(wr[:, :], wpack).then_inc(w_in, 16)
            act.dma_start(rp[:, :], rpack.to_broadcast([P, NRC])).then_inc(w_in, 16)
            act.dma_start(bcol[:, :], boff).then_inc(w_in, 16)
            for s, n in ((k_out, 2), (q_staged, 4), (ln_ready, 2), (sq_ready, 2), (q_out, 2), (v_out, 2), (exp_ready, 2), (vt_out, 6), (pt_out, 4),
                         (ye_out, 2), (sg_ready, 2), (hi_ready, 2), (xhi_ready, 2), (row_out, 2), (mk_out, 4), (py_out, 4), (im_out, 6), (ab_ready, 4), (wt_ready, 4), (aa_ready, 2), (ar_ready, 2), (z_ready, 4)):
                act.sem_inc(s, n)
            def squares(n, u):
                act.wait_ge(xc_ready, done(n))
                act.wait_ge(var_ready, free(n))
                act.sem_inc(act_turn, 1)
                a.activation(grid(two[:, u, 0:CH], W), xe3[:, bass.ds(n * RPC, RPC), 0:W], ACT.Square).then_inc(sq_ready, 1)

            def affine(n):
                rows = xe3[:, bass.ds(n * RPC, RPC), 0:W]
                act.wait_ge(xn_ready, done(n))
                act.sem_inc(act_turn, 1)
                a.activation(rows, rows, ACT.Identity, bias=w_("ln_b"), scale=w_("ln_w")).then_inc(ln_ready, 1)

            act.wait_ge(bd_ready, 2)
            squares(0, 0)
            squares(1, 1)
            with act.Fori(1, NCH // 2) as step:
                for u in range(2):
                    squares(2 * step + u, u)
            act.wait_ge(var_ready, done(NCH - 1))
            a.activation(rs, PS[:, 2, 0:HW // C], ACT.Sqrt, bias=c_("eps_ln")).then_inc(std_ready, 1)
            with act.Fori(0, NCH) as n:
                affine(n)
            with act.Fori(0, NCH // 2) as step:
                i = step * 2
                for u in range(2):
                    n = i + u
                    act.wait_ge(qkv_ready, done(n))
                    for dst, bank, s in ((kw, 2 + u, k_out), (vw, 4 + u, v_out), (qw, u, q_out)):
                        a.activation(dst[:, bass.ds(n * CH, CH)].rearrange("p (j r c) -> p r j c", j=NWR, r=WS),
                                     PS[:, bank, :].rearrange("p (r j c) -> p r j c", j=NWR, r=WS), ACT.Copy).then_inc(s, 1)

            def values(n, u):
                act.wait_ge(vt_ready, done(n))
                act.wait_ge(o_ready, free(n))
                for h in range(2):
                    a.activation(v0[64 * h:64 * (h + 1), u, :, :, h, 0:CS],
                                 PS[64 * h:64 * (h + 1), 4, 0:256].rearrange("p (w a b c) -> p w a b c", w=2, a=4, b=2)[:, :, :, h, 0:CS],
                                 ACT.Copy).then_inc(vt_out, 1)
                a.activation(v1[:, u].rearrange("p w (b c) -> p (w b) c", b=B)[:, :, CS:], PS[:, 4, 256:512].rearrange("p (b c) -> p b c", c=C)[:, :, CS:],
                             ACT.Copy).then_inc(vt_out, 1)

            def exps(n, u):
                act.wait_ge(sub_ready, done(n, 2))
                a.activation(ee[:, u, :], ee[:, u, :], ACT.Exp, scale=SCALE).then_inc(exp_ready, 1)

            def probs(n, u):
                act.wait_ge(pt_ready, done(n))
                act.wait_ge(o_ready, free(n))
                a.activation(pts[:, u, 0:4, :].rearrange("p t k -> p (t k)"), PS[:, 6, :], ACT.Copy).then_inc(pt_out, 1)
                a.activation(pts[:, u, 4, :], PS[:, 7, 0:P], ACT.Copy).then_inc(pt_out, 1)

            def write(n, row, col):
                act.wait_ge(ot_ready, done(n))
                for_rows = ye3[:, bass.ds(row, WS), col:col + 2 * WS] if not isinstance(row, int) else ye3[:, row:row + WS, col:col + 2 * WS]
                a.activation(for_rows.rearrange("p r (w c) -> p w r c", w=2),
                             PS[:, 5, 0:P].rearrange("p (w r c) -> p w r c", w=2, r=WS), ACT.Copy).then_inc(ye_out, 1)

            act.wait_ge(pads_ready, 6)
            def stage(n, u):
                act.wait_ge(vt_ready, free(n))
                act.sem_inc(act_turn, 1)
                a.activation(qs[:, u], qw[:, bass.ds(n * 2 * K1, 2 * K1)].rearrange("p (w k) -> p w k", w=2), ACT.Copy).then_inc(q_staged, 1)
                a.activation(vs[:, u], vw[:, bass.ds(n * 2 * K1, 2 * K1)].rearrange("p (w k) -> p w k", w=2).unsqueeze(2).to_broadcast([P, 2, 2, K1]),
                             ACT.Copy).then_inc(q_staged, 1)

            act.wait_ge(v_out, done(NCH - 1))
            act.wait_ge(q_out, done(NCH - 1))
            for n in range(2):
                stage(n, n)
            def lead(i):
                if not isinstance(i, int):
                    act.wait_ge(lead_ready, i - 1)
                    act.sem_inc(act_turn, 1)
                a.activation(x13[:, bass.ds(WS * i, WS), :], xe3[:, bass.ds(WS * i, WS), 0:W], ACT.Identity,
                             bias=w_("dw_b"), scale=w_("dw")[:, 4:5]).then_inc(lead_step, 1)
                a.activation(tap1, xe3[:, bass.ds(WS * i - 1, WS), 0:W - 1], ACT.Copy, scale=w_("dw")[:, 0:1]).then_inc(lead_step, 1)

            def row_sum(i):
                act.wait_ge(conv_step, (KK - 2) * (i + 1) + 2)
                act.sem_inc(act_turn, 1)
                rows = x1[:, bass.ds(i * CH, CH)]
                a.activation(rows, rows, ACT.Copy, accum_out=small[:, bass.ds(i + 49, 1)]).then_inc(x1_sum, 1)

            for n in range(4):
                if n >= 1:
                    probs(n - 1, (n - 1) % 2)
                values(n, n % 2)
                if n >= 1:
                    stage(n + 1, (n + 1) % 2)
                exps(n, n % 2)
                if n == 0:
                    lead(1)
                if n >= 2:
                    write(n - 2, SHIFT, 16 * (n - 2) + SHIFT)

            def four(i, last):
                for jj in range(4):
                    n = 4 * i + jj
                    probs(n - 1, (jj - 1) % 2)
                    values(n, jj % 2)
                    if not last or jj < 3:
                        stage(n + 1, (jj + 1) % 2)
                    exps(n, jj % 2)
                    if jj == 1:
                        row_sum(i - 1)
                    if jj == 0 and not last:
                        lead(i + 1)
                    write(n - 2, WS * i + SHIFT - (WS if jj < 2 else 0), 16 * ((jj - 2) % 4) + SHIFT)

            with act.Fori(1, NWR - 1) as i:
                four(i, False)
            four(NWR - 1, True)
            probs(31, 1)
            write(30, WS * (NWR - 1) + SHIFT, 32 + SHIFT)
            write(31, WS * (NWR - 1) + SHIFT, 48 + SHIFT)
            act.wait_ge(eca_pre, 1)
            a.activation(ecab[:, 108:108 + C], ecab[:, 92:92 + C], ACT.Sigmoid).then_inc(eca_gate, 1)
            with act.Fori(0, NCH // 2) as step:
                i = step * 2
                for u in range(2):
                    n = i + u
                    act.wait_ge(gate_ready, done(n))
                    act.wait_ge(po_ready, free(n))
                    a.activation(two[:, u, CH:], PS[:, u, :], ACT.Sigmoid, bias=r_("sa_b")).then_inc(sg_ready, 1)
            with act.Fori(0, NCH // 2) as step:
                i = step * 2
                for u in range(2):
                    n = i + u
                    act.wait_ge(om_out, done(n, 2))
                    act.wait_ge(px_done, free(n))
                    a.activation(spl[0:PAIRS * OC, u, 0, :], two[0:PAIRS * OC, u, :], ACT.Copy).then_inc(hi_ready, 1)
                    a.activation(grid(xsp[:, u, 0, :], W), xp3[:, bass.ds(n * RPC + 1, RPC), 1:1 + W], ACT.Copy).then_inc(xhi_ready, 1)
                    act.wait_ge(tr_ready, done(n))
                    for q in range(2):
                        a.activation(py4[:, bass.ds(n * RPC + 4 * q, 4)],
                                     PS[:, 4 + 2 * u + q, 0:4 * PAIRS * OC].rearrange("p (r g k) -> p r g k", r=4, k=OC)[:, :, :, 0:KK],
                                     ACT.Copy).then_inc(py_out, 1)
                        a.activation(mk4[:, bass.ds(n * RPC + 4 * q, 4)],
                                     PS[:, 4 + 2 * u + q, 0:4 * PAIRS * OC].rearrange("p (r g k) -> p r g k", r=4, k=OC)[:, :, :, 2 * KK:3 * KK],
                                     ACT.Sigmoid).then_inc(mk_out, 1)

            def row(n, u, slot=None):
                act.wait_ge(bc_ready, done(n))
                a.activation(ab[:, u, 0:320], PS[:, 6, 0:320], ACT.Abs, bias=c_("negx")).then_inc(ab_ready, 1)
                a.activation(ab[:, u, 320:576], PS[:, 7, 0:256], ACT.Abs, bias=c_("negx")).then_inc(ab_ready, 1)
                act.wait_ge(t_ready, free(n))
                act.wait_ge(ab_ready, done(n, 2))
                for h in range(2):
                    a.activation(wt[W * h:W * (h + 1), u, :, W * h:W * (h + 1)],
                                 ab[W * h:W * (h + 1), u, :].rearrange("p (k c) -> p k c", k=KK), ACT.Relu, bias=1.0, scale=-1.0).then_inc(wt_ready, 1)
                    if slot is None or h == 1:
                        continue
                    a.activation(img4[:, bass.ds(slot, 1)].rearrange("p r k o -> p (r k o)"), PS[:, 7, 256:400], ACT.Copy).then_inc(row_out, 1)

            def image_chunk(n, yc, u):
                act.wait_ge(im_ready, done(n))
                act.sem_inc(act_turn, 1)
                for b, k in enumerate((3, 3, 2)):
                    a.activation(img4[:, bass.ds(RPC * yc + TOP + 3 * b, k)], PS[:, 4 * u + b, 0:144 * k].rearrange("p (r k o) -> p r k o", k=KK, o=C),
                                 ACT.Copy).then_inc(im_out, 1)

            def hat(n, yc, stage):
                rows = aw4[:, bass.ds(RPC * yc, RPC)].rearrange("p r k j -> p (r k j)")
                act.wait_ge((ad_ready, aa_ready)[stage], done(n))
                act.sem_inc(act_turn, 1)
                if stage == 0:
                    a.activation(rows, rows, ACT.Abs).then_inc(aa_ready, 1)
                else:
                    a.activation(rows, rows, ACT.Relu, bias=1.0, scale=-1.0).then_inc(ar_ready, 1)

            def weights_ahead():
                hat(0, 0, 0)
                hat(0, 0, 1)

                def pair(g, last, chunks):
                    def chunk(c, u):
                        s = g * NCH + c
                        first, end = (isinstance(c, int) and c == e for e in (0, NCH - 1))
                        for r in range(RPC):
                            slot = TOP + H - RPC + r if first else None if last else c * RPC + (TOP - RPC + r)
                            row(s * RPC + r, r % 2, slot)
                            if r in (4, 6) and not (last and end):
                                hat(s + 1, 0 if end else c + 1, (r - 4) // 2)
                    chunks(chunk)
                stream(act, pair)

            def weights(p, g, band):
                act.wait_ge(t_ready, p * H + LAST)
                for yc in range(NCH):
                    image_chunk(NCH + p * NCH + yc, yc, yc % 2)
                for stage in range(2):
                    for yc in range(NCH):
                        hat(p * NCH + yc, yc, stage)
                with act.Fori(0, H // RPC) as step:
                    for r in range(RPC):
                        row(p * H + step * RPC + r, r % 2)

            with act.Fori(0, NCH // 2) as step:
                for u in range(2):
                    image_chunk(step * 2 + u, step * 2 + u, u)
            act.wait_ge(zeros_ready, 3)
            branches(act, weights_ahead, weights)
            with act.Fori(0, NCH // 2) as step:
                i = step * 2
                for u in range(2):
                    n = i + u
                    act.wait_ge(ot2_ready, done(n))
                    for h in range(2):
                        part = slice(64 * h, 64 * (h + 1))
                        a.activation(z[part, bass.ds(n * CH, CH)].rearrange("p (b r c) -> p b r c", b=2, c=W),
                                     PS[part, 2 * u:2 * u + 2, :].rearrange("p b (r h c) -> p b r h c", h=2, c=W)[:, :, :, h, :],
                                     ACT.Identity, bias=w_("b")[part]).then_inc(z_ready, 1)
            act.wait_ge(bn_var, 1)
            a.activation(small[:, 6:7], PS[:, 6, 1:2], ACT.Sqrt, bias=c_("eps_bn"), scale=1.0 / B).then_inc(bn_std, 1)
            act.wait_ge(bn_aff, 1)
            with act.Fori(0, 4) as n:
                zc = z[:, bass.ds(n * 1024, 1024)]
                a.activation(zc, zc, ACT.Relu, bias=small[:, 7:8], scale=small[:, 6:7]).then_inc(f_ready, 1)

        @block.tensor
        def _(pe):
            def mm(o, l, r, start=True, stop=True):
                return nc.tensor.matmul(o, l, r, start=start, stop=stop)

            for s, n in ((rb_ready, 2), (mu_ready, 2), (var_ready, 2), (qkv_ready, 2), (s_ready, 2), (vt_ready, 2), (pt_ready, 2), (o_ready, 2),
                         (ot_ready, 2), (gate_ready, 2), (y_used, 2), (po_ready, 2), (om_ready, 4), (tr_ready, 2), (im_ready, 2), (bc_ready, 2),
                         (t_ready, 2), (ot2_ready, 2)):
                pe.sem_inc(s, n)
            pe.wait_ge(x_in, 16)
            pe.wait_ge(bd_ready, 1)
            def means(n, u):
                pe.wait_ge(xc_ready, free(n))
                mm(PS[:, u, :], bd[:, MEAN, :], x0[:, bass.ds(n * CH, CH)]).then_inc(mu_ready, 1)

            def variances(n, u):
                pe.wait_ge(sq_ready, done(n))
                for q in (2 * n, 2 * n + 1):
                    at = CCOL["wide"][0] + P - B - B * q
                    ins = mm(PS[:, 2, 0:HW // C], cst[:, at:at + P], two[:, u, HW // C * (q % 2):HW // C * (q % 2 + 1)],
                             start=q == 0, stop=q == C - 1)
                ins.then_inc(var_ready, 1)

            for n in range(NCH + 1):
                if n == 2:
                    pe.wait_ge(rest_in, 16)
                if n < NCH:
                    means(n, n % 2)
                if n >= 1:
                    variances(n - 1, (n - 1) % 2)
            pe.wait_ge(rstd_ready, 1)
            for n in range(NCH):
                pe.wait_ge(xc_ready, done(min(n, 1) + NCH - 2))
                pe.wait_ge(xn_ready, free(n))
                for q in (2 * n, 2 * n + 1):
                    part, at = slice(32 * (q // 4), 32 * (q // 4 + 1)), CCOL["spread"][0] + P * (q % 4)
                    ins = mm(PS[:, n % 2, HW // C * (q % 2):HW // C * (q % 2 + 1)], cst[part, at:at + P], rs[part, :])
                ins.then_inc(rb_ready, 1)
            pe.wait_ge(bd_ready, 12)
            pe.wait_ge(ext_ready, 2)
            with pe.Fori(0, NCH // 2) as step:
                i = step * 2
                for u in range(2):
                    n = i + u
                    pe.wait_ge(q_out, free(n))
                    pe.wait_ge(k_out, free(n))
                    pe.wait_ge(v_out, free(n))
                    src = xe3[:, bass.ds(n * WS + SHIFT, WS), SHIFT:SHIFT + W]
                    mm(PS[:, u, :], bd[:, WQ, :], src)
                    mm(PS[:, 2 + u, :], bd[:, WK, :], src)
                    mm(PS[:, 4 + u, :], bd[:, WV, :], src).then_inc(qkv_ready, 1)
            def scores(n, u):
                pe.wait_ge(staged, done(n, 2))
                pe.wait_ge(q_staged, done(n, 2))
                pe.wait_ge(sub_ready, 2 * n + 4)
                for w in range(2):
                    mm(PS[64 * w:64 * (w + 1), u, :], qs[:, u, w, :], kb[:, u, w, :])
                    ins = mm(PS[64 * w:64 * (w + 1), 2, 0:P], qs[:, u, w, :], kvb[:, u, w, 0, :])
                ins.then_inc(s_ready, 1)

            def values(n, u):
                pe.wait_ge(vt_out, 3 * n + 6)
                for w in range(2):
                    nc.tensor.transpose(PS[:, 4, w * P:(w + 1) * P], vs[:, u, w].rearrange("p d k -> p (d k)"), ident)
                    ins = nc.tensor.transpose(PS[:, 4, 256 + w * P:256 + (w + 1) * P], kvb[:, u, w, 1, :], ident)
                ins.then_inc(vt_ready, 1)

            def probs(n, u):
                pe.wait_ge(exp_ready, done(n))
                pe.wait_ge(pt_out, 2 * n + 4)
                for t in range(5):
                    ins = nc.tensor.transpose(PS[:, 6, P * t:P * (t + 1)] if t < 4 else PS[:, 7, 0:P], ee[:, u, P * t:P * (t + 1)], ident)
                ins.then_inc(pt_ready, 1)

            def attend(n, u):
                pe.wait_ge(pt_out, done(n, 2))
                pe.wait_ge(vt_out, done(n, 3))
                pe.wait_ge(on_ready, 2 * n + 4)
                for w in range(2):
                    part = slice(64 * w, 64 * (w + 1))
                    for t in range(4):
                        mm(PS[part, 3, 32 * t:32 * (t + 1)], pts[:, u, t, part],
                           v0[:, u, w, t].rearrange("p b c -> p (b c)"))
                    ins = mm(PS[part, 3, P:2 * P], pts[:, u, 4, part], v1[:, u, w, :])
                ins.then_inc(o_ready, 1)

            def back(n, u):
                pe.wait_ge(on_ready, done(n, 2))
                pe.wait_ge(ye_out, n + 2)
                nc.tensor.transpose(PS[:, 5, 0:P], on[:, u, :], ident).then_inc(ot_ready, 1)

            for n in range(4):
                scores(n, n % 2)
                if n >= 1:
                    probs(n - 1, (n - 1) % 2)
                values(n, n % 2)
                if n >= 2:
                    back(n - 2, n % 2)
                if n >= 1:
                    attend(n - 1, (n - 1) % 2)
            with pe.Fori(1, NWR) as i:
                for jj in range(4):
                    n = 4 * i + jj
                    scores(n, jj % 2)
                    probs(n - 1, (jj - 1) % 2)
                    values(n, jj % 2)
                    back(n - 2, jj % 2)
                    attend(n - 1, (jj - 1) % 2)
            probs(31, 1)
            back(30, 0)
            attend(31, 1)
            back(31, 1)
            pe.wait_ge(pt_out, done(31, 2))
            pe.wait_ge(eca_step, 3)
            mm(PS[0:B, 6, 0:C], c_("bmask"), small[:, 16:32]).then_inc(eca_sum, 1)
            pe.wait_ge(eca_gate, 1)
            pe.wait_ge(eca_step, 4)
            pe.wait_ge(pt_out, done(31, 2))
            mm(PS[:, 6, 32:48], cst[0:B, CCOL["bmt"][0]:CCOL["bmt"][1]], ecab[:, 108:108 + C]).then_inc(eca_back, 1)
            def gate(n):
                u = n % 2
                pe.wait_ge(yc_ready, done(n))
                pe.wait_ge(sg_ready, free(n))
                mm(PS[:, u, :], bd[:, SA, :], two[:, u, 0:CH]).then_inc(gate_ready, 1)
                if n >= 4:
                    pe.wait_ge(xl_ready, done(n - 4))
                mm(PS[:, 2 + n % 4, :], bd[:, PO, :], two[:, u, 0:CH], stop=False).then_inc(y_used, 1)

            gate(0)
            gate(1)
            for n in range(NCH):
                pe.wait_ge(gx_ready, done(n))
                mm(PS[:, 2 + n % 4, :], bd[:, PO, :], two[:, n % 2, CH:], start=False).then_inc(po_ready, 1)
                if n + 2 < NCH:
                    gate(n + 2)
            pe.wait_ge(xl_ready, done(NCH - 1))
            def offsets(n, u):
                pe.wait_ge(om_out, free(n, 2))
                for h in range(2):
                    for t in range(6):
                        rows = 128 if t < 3 else 64
                        ins = mm(PS[0:PAIRS * OC, 2 * h + u, :], woff[0:rows, t, :],
                                 xs[0:rows, h, bass.ds(n * RPC + 2 * (t // 3), RPC), t % 3:t % 3 + W], start=t == 0, stop=t == 5)
                    ins.then_inc(om_ready, 1)

            def to_samples(n, u):
                pe.wait_ge(om_out, done(n, 2))
                pe.wait_ge(py_out, free(n, 2))
                pe.wait_ge(mk_out, free(n, 2))
                for r in range(RPC):
                    for h in range(2):
                        ins = mm(PS[64 * h:64 * (h + 1), 4 + 2 * u + r // 4, (r % 4) * PAIRS * OC:(r % 4 + 1) * PAIRS * OC],
                                 two[0:PAIRS * OC, u, h * CH + r * W:h * CH + (r + 1) * W], ident[0:PAIRS * OC, 0:PAIRS * OC])
                ins.then_inc(tr_ready, 1)

            pe.wait_ge(xs_ready, 1)
            offsets(0, 0)
            with pe.Fori(0, (NCH - 2) // 2) as step:
                pe.wait_ge(xs_ready, step + 2)
                for u in range(2):
                    offsets(step * 2 + u + 1, 1 - u)
                    to_samples(step * 2 + u, u)
            pe.wait_ge(xs_ready, 4)
            offsets(NCH - 1, 1)
            to_samples(NCH - 2, 0)
            to_samples(NCH - 1, 1)

            def image_row(bank, at, u, r):
                return mm(PS[:, bank, at:at + KK * C], two[:, u, P * r:P * (r + 1)], w_("w"))

            def image_chunk(n, u):
                pe.wait_ge(is_ready, done(n, 2))
                pe.wait_ge(im_out, free(n, 3))
                for r in range(RPC):
                    ins = image_row(4 * u + r // 3, 144 * (r % 3), u, r)
                ins.then_inc(im_ready, 1)

            def px(n, y, image=None, before=False):
                pe.wait_ge(ab_ready, 2 * n + 4)
                if before:
                    pe.wait_ge(row_out, n + 2)
                if image is not None:
                    rows = xrow[:, image[0], image[1]].rearrange("p h c -> p (h c)")
                    mm(PS[:, 7, 256:256 + KK * C], rows, wsp[:, 0, :], stop=False)
                    mm(PS[:, 7, 256:256 + KK * C], rows, wsp[:, 1, :], start=False)
                for k in range(KK):
                    o = PS[:, 6, W * k:W * (k + 1)] if k < 5 else PS[:, 7, W * (k - 5):W * (k - 4)]
                    ins = mm(o, selb[:, k, :], sx[:, bass.ds(y * W, W)])
                ins.then_inc(bc_ready, 1)

            def taps(n, y, u, band):
                pe.wait_ge(wt_ready, done(n, 2))
                pe.wait_ge(u_ready, free(n))
                for k in range(KK):
                    ins = mm(PS[:, 3 * u + k // 3, 144 * (k % 3):144 * (k % 3 + 1)], wt[:, u, k, :],
                             img4[:, bass.ds(y + k // 3 if band is None else band * NR + TOP, NR), k, :])
                ins.then_inc(t_ready, 1)

            pe.wait_ge(py_out, done(NCH - 1, 2))
            pe.wait_ge(mk_out, done(NCH - 1, 2))
            pe.wait_ge(om_out, done(NCH - 1, 2))
            image_chunk(0, 0)
            image_chunk(1, 1)
            pe.wait_ge(off_max, 1)
            mm(PS[0:1, 3, 0:P], small[:, 10:11], ident).then_inc(off_row, 1)
            with pe.Fori(1, NCH // 2) as step:
                for u in range(2):
                    image_chunk(step * 2 + u, u)
            pe.wait_ge(zeros_ready, 3)

            def sample_all():
                pe.wait_ge(im_out, done(NCH - 1, 3))
                pe.wait_ge(xr_ready, 1)
                pe.wait_ge(px_ready, 1)
                px(0, 0, image=(1, 0))

                def pair(g, last, chunks):
                    def chunk(c, u):
                        s = g * NCH + c
                        first, end = (isinstance(c, int) and c == e for e in (0, NCH - 1))
                        here = first or not last
                        for r in range(RPC):
                            n = s * RPC + r
                            if r < RPC - 1:
                                px(n + 1, c * RPC + r + 1, (1 - u, r + 1) if here else None, here)
                            elif not (last and end):
                                pe.wait_ge(px_ready, s + 2)
                                if not last:
                                    pe.wait_ge(xr_ready, s + 2)
                                px(n + 1, 0 if end else (c + 1) * RPC, (u, 0) if not last else None, here)
                            taps(n, c * RPC + r, r % 2, None)
                    chunks(chunk)
                stream(pe, pair)

            def sample(p, g, band):
                pe.wait_ge(u_ready, p * H + LAST)
                pe.wait_ge(ab_ready, 2 * (p * H + LAST))
                for yc in range(NCH):
                    image_chunk(NCH + p * NCH + yc, yc % 2)
                pe.wait_ge(im_out, (p * NCH + 2 * NCH + LAST) * 3)
                pe.wait_ge(px_ready, p + 1)
                px(p * H, 0)
                with pe.Fori(0, (H - RPC) // RPC) as step:
                    y0 = step * RPC
                    for r in range(RPC):
                        px(p * H + y0 + r + 1, y0 + r + 1)
                        taps(p * H + y0 + r, y0 + r, r % 2, band)
                for r in range(RPC):
                    y = H - RPC + r
                    if r < RPC - 1:
                        px(p * H + y + 1, y + 1)
                    taps(p * H + y, y, r % 2, band)

            branches(pe, sample_all, sample)
            with pe.Fori(0, NCH // 2) as step:
                i = step * 2
                for u in range(2):
                    n = i + u
                    pe.wait_ge(ob_ready, done(n, 2))
                    pe.wait_ge(z_ready, free(n, 2))
                    for r in range(RPC):
                        ins = nc.tensor.transpose(PS[:, 2 * u + r // 4, P * (r % 4):P * (r % 4 + 1)], two[:, u, P * r:P * (r + 1)], ident)
                    ins.then_inc(ot2_ready, 1)
            pe.wait_ge(bn_sum, 1)
            mm(PS[:, 6, 0:1], c_("osum"), small[:, 2:3]).then_inc(bn_mean, 1)
            pe.wait_ge(bn_sq, 1)
            mm(PS[:, 6, 1:2], c_("osum"), small[:, 9:10]).then_inc(bn_var, 1)


def kernel(**inputs):
    import concourse.bacc as bacc
    from concourse.bass_utils import run_bass_kernel_spmd as run

    a = {k: np.ascontiguousarray(np.asarray(v)) for k, v in inputs.items()}
    L0, L1 = "L0_conv_", "L1_conv_"

    def head1(m):
        return np.concatenate([np.zeros((CS, m.shape[1]), np.float32), m])

    parts = {
        "wq": a[L0 + "wq"].T, "wk": a[L0 + "wk"].T, "wv": a[L0 + "wv"].T, "po": a[L0 + "po_w"].T, "sa": a[L0 + "sa_w"].T,
        "woff": a[L1 + "w_off"].transpose(1, 2, 3, 0).reshape(C, -1), "w": a[L1 + "w"].transpose(1, 2, 3, 0).reshape(C, -1),
        "ln_w": a[L0 + "ln_w"][:, None], "ln_b": a[L0 + "ln_b"][:, None], "dw_b": a[L0 + "dw_b"][:, None],
        "po_b": a[L0 + "po_b"][:, None], "dw": a[L0 + "dw_w"].reshape(C, KK),
        "down": head1(a[L0 + "down_w"].reshape(CS, 4)), "down_b": head1(a[L0 + "down_b"][:, None]),
        "b": a[L1 + "b"][:, None], "gamma": a[L1 + "gamma"][:, None], "beta": a[L1 + "beta"][:, None],
    }
    rows = {"w1": a[L0 + "eca_w1"], "w2": a[L0 + "eca_w2"], "w3": a[L0 + "eca_w3"], "wc": a[L0 + "eca_wc"], "sa_b": a[L0 + "sa_b"]}
    consts, sel = constants()
    arrays = {
        "x": a["x"],
        "wpack": np.tile(np.concatenate([parts[n] for n, _ in _WCOLS], axis=1), (B, 1)),
        "rpack": np.concatenate([rows[n].reshape(1, -1) for n, _ in _RCOLS], axis=1),
        "boff": np.tile(a[L1 + "b_off"][:, None], (PAIRS, 1)),
        "consts": consts, "sel": sel,
    }
    nc = bacc.Bacc("TRN2", target_bir_lowering=False, num_devices=1)
    aps = [nc.dram_tensor("in_" + n, v.shape, F32, kind="ExternalInput").ap() for n, v in arrays.items()]
    o = nc.dram_tensor("out_0", (B, C, H, W), F32, kind="ExternalOutput").ap()
    build(nc, *aps, o)
    r = run(nc, [{"in_" + n: v for n, v in arrays.items()}], core_ids=[0])
    return r.results[0]["out_0"]
```
